# Optimizing a Trainium2 kernel written in Bass

```python
import numpy as np
import jax
import jax.numpy as jnp

def _softmax(x, axis=-1):
    return jax.nn.softmax(x, axis=axis)

def _gelu(x):
    return jax.nn.gelu(x, approximate=True)

def _silu(x):
    return jax.nn.silu(x)

def _sigmoid(x):
    return jax.nn.sigmoid(x)

def _layernorm(x, axis=-1, eps=1e-05):
    m = jnp.mean(x, axis=axis, keepdims=True)
    v = jnp.var(x, axis=axis, keepdims=True)
    return (x - m) / jnp.sqrt(v + eps)

def _scatter_add(tgt, idx, src, axis=0):
    return tgt.at[idx].add(src)

def _segment_sum(src, seg, n):
    return jax.ops.segment_sum(src, seg, n)
kernel_name = 'mk_decoder_postln_d1_seqx_r8_4095b5'

def setup_inputs(seed: int=0):
    np.random.seed(seed)
    _w = jnp.asarray

    def _rec_inputs():
        import jax
        import jax.numpy as jnp
        _rk = jax.random.key(seed)
        x = 0.002226 + 0.9996 * jax.random.normal(jax.random.fold_in(_rk, 1), (64, 128, 128), jnp.float32)
        _lenS = 128 - jax.random.randint(jax.random.fold_in(_rk, 7), (64,), 0, max(1, 128 // 4) + 1, jnp.int32)
        _lenS2 = 120 - jax.random.randint(jax.random.fold_in(_rk, 8), (64,), 0, max(1, 120 // 4) + 1, jnp.int32)
        _ctx_1024P = jax.random.normal(jax.random.fold_in(_rk, 11), (64, 16, 128), jnp.float32)
        _ctx_1024c = jax.random.dirichlet(jax.random.fold_in(_rk, 511), 0.3 * jnp.ones((16,), jnp.float32), (64, 120))
        _ctx_1024t = jnp.einsum('bsk,bkd->bsd', _ctx_1024c, _ctx_1024P)
        _ctx_1024t = _ctx_1024t * jax.lax.rsqrt(jnp.mean(jnp.square(_ctx_1024t)) + 1e-12) * 0.953939
        ctx_1024 = -0.000125008 + 0.999885 * (_ctx_1024t + 0.3 * jax.random.normal(jax.random.fold_in(_rk, 611), (64, 120, 128), jnp.float32))
        return (x, ctx_1024)
    x, ctx_1024 = _rec_inputs()

    def _L0_attn_setup():
        import jax, jax.numpy as jnp
        import numpy as np
        D_MODEL = 128
        N_HEADS = 16
        D_HEAD = D_MODEL // N_HEADS
        key = jax.random.key(seed)
        ks = jax.random.split(key, 5)
        B, S = (1, 256)
        x = jax.random.normal(ks[0], (B, S, D_MODEL), dtype=jnp.float32)
        lim = float(np.sqrt(6.0 / (2 * D_MODEL)))

        def w(k):
            return jax.random.uniform(k, (D_MODEL, D_MODEL), jnp.float32, -lim, lim)
        return {'x': x, 'Wq': w(ks[1]), 'bq': jnp.zeros((D_MODEL,), jnp.float32), 'Wk': w(ks[2]), 'bk': jnp.zeros((D_MODEL,), jnp.float32), 'Wv': w(ks[3]), 'bv': jnp.zeros((D_MODEL,), jnp.float32), 'Wo': w(ks[4]), 'bo': jnp.zeros((D_MODEL,), jnp.float32)}
    _L0_attn_all = _L0_attn_setup()
    _L0_attn_in = {k: v for k, v in _L0_attn_all.items() if k in ('Wq', 'bq', 'Wk', 'bk', 'Wv', 'bv', 'Wo', 'bo')}
    del _L0_attn_all

    def _L0_xattn_setup():
        import jax, jax.numpy as jnp
        import numpy as np
        EPS = 1e-05

        def layer_norm(x, g, b):
            mu = jnp.mean(x, axis=-1, keepdims=True)
            var = jnp.var(x, axis=-1, keepdims=True)
            return (x - mu) * jax.lax.rsqrt(var + EPS) * g + b
        key = jax.random.key(seed)
        ks = jax.random.split(key, 8)
        dim, heads, dim_head = (128, 16, 64)
        inner = heads * dim_head
        b, n, m = (8, 512, 64)
        s = dim ** (-0.5)
        return {'x': jax.random.normal(ks[0], (b, n, dim), jnp.float32), 'latents': jax.random.normal(ks[1], (b, m, dim), jnp.float32), 'ln_m_g': jnp.ones((dim,), jnp.float32), 'ln_m_b': jnp.zeros((dim,), jnp.float32), 'ln_l_g': jnp.ones((dim,), jnp.float32), 'ln_l_b': jnp.zeros((dim,), jnp.float32), 'Wq': jax.random.normal(ks[2], (dim, inner), jnp.float32) * s, 'Wkv': jax.random.normal(ks[3], (dim, 2 * inner), jnp.float32) * s, 'Wout': jax.random.normal(ks[4], (inner, dim), jnp.float32) * s}
    _L0_xattn_all = _L0_xattn_setup()
    _L0_xattn_in = {k: v for k, v in _L0_xattn_all.items() if k in ('ln_m_g', 'ln_m_b', 'ln_l_g', 'ln_l_b', 'Wq', 'Wkv', 'Wout')}
    del _L0_xattn_all

    def _L0_ffn_setup():
        import jax, jax.numpy as jnp
        import numpy as np
        B, S, D = (1, 256, 128)
        E, K, F = (8, 2, 176)
        NS = 2
        SCALE = 2.5

        def _swiglu_mlp(x, wg, wu, wd):
            return jax.nn.silu(x @ wg) * (x @ wu) @ wd
        key = jax.random.key(seed)
        ks = jax.random.split(key, 8)
        s = 0.02
        return {'hidden_states': jax.random.normal(ks[0], (B, S, D), jnp.float32), 'gate_w': jax.random.normal(ks[1], (E, D), jnp.float32) * s, 'w_gate': jax.random.normal(ks[2], (E, D, F), jnp.float32) * s, 'w_up': jax.random.normal(ks[3], (E, D, F), jnp.float32) * s, 'w_down': jax.random.normal(ks[4], (E, F, D), jnp.float32) * s, 'sw_gate': jax.random.normal(ks[5], (D, F * NS), jnp.float32) * s, 'sw_up': jax.random.normal(ks[6], (D, F * NS), jnp.float32) * s, 'sw_down': jax.random.normal(ks[7], (F * NS, D), jnp.float32) * s}
    _L0_ffn_all = _L0_ffn_setup()
    _L0_ffn_in = {k: v for k, v in _L0_ffn_all.items() if k in ('gate_w', 'w_gate', 'w_up', 'w_down', 'sw_gate', 'sw_up', 'sw_down')}
    del _L0_ffn_all
    return {'x': x, 'ctx_1024': ctx_1024, 'L0_attn_Wq': _L0_attn_in['Wq'], 'L0_attn_bq': _L0_attn_in['bq'], 'L0_attn_Wk': _L0_attn_in['Wk'], 'L0_attn_bk': _L0_attn_in['bk'], 'L0_attn_Wv': _L0_attn_in['Wv'], 'L0_attn_bv': _L0_attn_in['bv'], 'L0_attn_Wo': _L0_attn_in['Wo'], 'L0_attn_bo': _L0_attn_in['bo'], 'L0_xattn_ln_m_g': _L0_xattn_in['ln_m_g'], 'L0_xattn_ln_m_b': _L0_xattn_in['ln_m_b'], 'L0_xattn_ln_l_g': _L0_xattn_in['ln_l_g'], 'L0_xattn_ln_l_b': _L0_xattn_in['ln_l_b'], 'L0_xattn_Wq': _L0_xattn_in['Wq'], 'L0_xattn_Wkv': _L0_xattn_in['Wkv'], 'L0_xattn_Wout': _L0_xattn_in['Wout'], 'L0_ffn_gate_w': _L0_ffn_in['gate_w'], 'L0_ffn_w_gate': _L0_ffn_in['w_gate'], 'L0_ffn_w_up': _L0_ffn_in['w_up'], 'L0_ffn_w_down': _L0_ffn_in['w_down'], 'L0_ffn_sw_gate': _L0_ffn_in['sw_gate'], 'L0_ffn_sw_up': _L0_ffn_in['sw_up'], 'L0_ffn_sw_down': _L0_ffn_in['sw_down']}

def reference(x, ctx_1024, L0_attn_Wq, L0_attn_bq, L0_attn_Wk, L0_attn_bk, L0_attn_Wv, L0_attn_bv, L0_attn_Wo, L0_attn_bo, L0_xattn_ln_m_g, L0_xattn_ln_m_b, L0_xattn_ln_l_g, L0_xattn_ln_l_b, L0_xattn_Wq, L0_xattn_Wkv, L0_xattn_Wout, L0_ffn_gate_w, L0_ffn_w_gate, L0_ffn_w_up, L0_ffn_w_down, L0_ffn_sw_gate, L0_ffn_sw_up, L0_ffn_sw_down):
    import jax
    import jax.numpy as jnp

    def _L0_attn_ref(x, Wq, bq, Wk, bk, Wv, bv, Wo, bo):
        import jax, jax.numpy as jnp
        import numpy as np
        D_MODEL = 128
        N_HEADS = 16
        D_HEAD = D_MODEL // N_HEADS
        B, S, _ = x.shape
        H, d = (N_HEADS, D_HEAD)
        q = x @ Wq.T + bq
        k = x @ Wk.T + bk
        v = x @ Wv.T + bv

        def to_z(t):
            return t.reshape(B, S, H, d).transpose(0, 2, 1, 3).reshape(B * H, S, d)
        q = jax.nn.softplus(to_z(q))
        k = jax.nn.softplus(to_z(k))
        v = to_z(v)
        kv = jnp.cumsum(k[:, :, :, None] * v[:, :, None, :], axis=1)
        k1 = jnp.cumsum(k, axis=1)
        num = jnp.einsum('zsD,zsDe->zse', q, kv)
        den = jnp.sum(q * k1, axis=-1, keepdims=True)
        out = num / den
        out = out.reshape(B, H, S, d).transpose(0, 2, 1, 3).reshape(B, S, H * d)
        return out @ Wo.T + bo

    def _L0_xattn_ref(x, latents, ln_m_g, ln_m_b, ln_l_g, ln_l_b, Wq, Wkv, Wout):
        import jax, jax.numpy as jnp
        import numpy as np
        EPS = 1e-05

        def layer_norm(x, g, b):
            mu = jnp.mean(x, axis=-1, keepdims=True)
            var = jnp.var(x, axis=-1, keepdims=True)
            return (x - mu) * jax.lax.rsqrt(var + EPS) * g + b
        heads, dim_head = (16, 64)
        scale = dim_head ** (-0.5)
        x = layer_norm(x, ln_m_g, ln_m_b)
        lat = layer_norm(latents, ln_l_g, ln_l_b)
        b, m, _ = lat.shape
        q = lat @ Wq
        kv_input = jnp.concatenate([x, lat], axis=1)
        kv = kv_input @ Wkv
        k, v = jnp.split(kv, 2, axis=-1)

        def split_heads(t):
            return t.reshape(t.shape[0], t.shape[1], heads, dim_head).transpose(0, 2, 1, 3)
        q, k, v = (split_heads(q), split_heads(k), split_heads(v))
        dots = jnp.einsum('bhid,bhjd->bhij', q, k) * scale
        attn = jax.nn.softmax(dots, axis=-1)
        out = jnp.einsum('bhij,bhjd->bhid', attn, v)
        out = out.transpose(0, 2, 1, 3).reshape(b, m, heads * dim_head)
        return out @ Wout

    def _L0_ffn_ref(hidden_states, gate_w, w_gate, w_up, w_down, sw_gate, sw_up, sw_down):
        import jax, jax.numpy as jnp
        import numpy as np
        B, S, D = (1, 256, 128)
        E, K, F = (8, 2, 176)
        NS = 2
        SCALE = 2.5

        def _swiglu_mlp(x, wg, wu, wd):
            return jax.nn.silu(x @ wg) * (x @ wu) @ wd
        identity = hidden_states
        x = hidden_states.reshape(-1, hidden_states.shape[-1])
        T = x.shape[0]
        logits = x.astype(jnp.float32) @ gate_w.astype(jnp.float32).T
        scores = jax.nn.softmax(logits, axis=-1)
        topk_w, topk_i = jax.lax.top_k(scores, K)
        topk_w = topk_w / (topk_w.sum(-1, keepdims=True) + 1e-20) * SCALE
        combine = jnp.zeros((T, E), jnp.float32).at[jnp.arange(T)[:, None], topk_i].set(topk_w)
        g = jax.nn.silu(jnp.einsum('td,edf->etf', x, w_gate)) * jnp.einsum('td,edf->etf', x, w_up)
        expert_out = jnp.einsum('etf,efd->etd', g, w_down)
        y = jnp.einsum('te,etd->td', combine, expert_out).astype(x.dtype)
        y = y.reshape(identity.shape)
        return y + _swiglu_mlp(identity, sw_gate, sw_up, sw_down)
    x = _layernorm(x + _L0_attn_ref(x, L0_attn_Wq, L0_attn_bq, L0_attn_Wk, L0_attn_bk, L0_attn_Wv, L0_attn_bv, L0_attn_Wo, L0_attn_bo), axis=-1)
    x = _layernorm(x + _L0_xattn_ref(ctx_1024, x, L0_xattn_ln_m_g, L0_xattn_ln_m_b, L0_xattn_ln_l_g, L0_xattn_ln_l_b, L0_xattn_Wq, L0_xattn_Wkv, L0_xattn_Wout), axis=-1)
    x = _layernorm(x + _L0_ffn_ref(x, L0_ffn_gate_w, L0_ffn_w_gate, L0_ffn_w_up, L0_ffn_w_down, L0_ffn_sw_gate, L0_ffn_sw_up, L0_ffn_sw_down), axis=-1)
    return x

_drawn_inputs = setup_inputs


def setup_inputs(seed=0):
    import zlib

    import numpy as np

    out = dict(_drawn_inputs(seed))
    spreads = {'L0_attn_bq': (0.0, 0.8),
     'L0_attn_bk': (0.0, 0.8),
     'L0_attn_bv': (0.0, 0.1),
     'L0_attn_bo': (0.0, 0.1),
     'L0_xattn_ln_m_g': (1.0, 0.2),
     'L0_xattn_ln_m_b': (0.0, 0.1),
     'L0_xattn_ln_l_g': (1.0, 0.2),
     'L0_xattn_ln_l_b': (0.0, 0.1)}
    factors = {'L0_ffn_gate_w': 5.396,
     'L0_ffn_w_gate': 4.684,
     'L0_ffn_w_up': 4.676,
     'L0_ffn_w_down': 4.66,
     'L0_ffn_sw_gate': 5.935,
     'L0_ffn_sw_up': 5.901,
     'L0_ffn_sw_down': 5.943}
    for name, (base, spread) in spreads.items():
        noise = np.random.default_rng([zlib.crc32(name.encode()), seed]).standard_normal(out[name].shape)
        drawn = base * np.exp(spread * noise) if base else spread * noise
        out[name] = jnp.asarray(drawn.astype(out[name].dtype))
    for name, factor in factors.items():
        out[name] = (out[name] * factor).astype(out[name].dtype)
    return out
```

```python
from contextlib import ExitStack

import concourse.bass as bass
from concourse import mybir

F32 = mybir.dt.float32
F32R = mybir.dt.float32r
ALU = mybir.AluOpType
ACT = mybir.ActivationFunctionType
AX = mybir.AxisListType.X

P = 128
B = 64
S = 128
D = 128
C = 120
H = 16
EPS = 1e-5


def wait(engine, semaphore, count):
    if not isinstance(count, int) or count > 0:
        engine.wait_ge(semaphore, count)


def wait_apart(engine, opened, *waits):
    waits = [(semaphore, count if isinstance(count, int) else engine.to_reg(count)) for semaphore, count in waits]
    engine.wait_ge(opened, 1)
    for semaphore, count in waits:
        wait(engine, semaphore, count)


def pipelined(engine, step, count=B, head=4, tail=4):
    for t in range(head):
        step(t, t % 2)
    with engine.Fori(head // 2, count // 2) as i:
        for parity in range(2):
            step(i * 2 + parity, parity)
    for t in range(count, count + tail):
        step(t, t % 2)


def there(s, count=B):
    return not isinstance(s, int) or 0 <= s < count


def landed(s, parity):
    return (s - parity) * 8 + 16


class Room:

    def __init__(self, nc, stack, tag):
        self.nc, self.stack, self.tag = nc, stack, tag

    def sbuf(self, name, shape, dtype=F32):
        return self.stack.enter_context(self.nc.sbuf_tensor(f"{self.tag}_{name}", shape, dtype))

    def psum(self, name, shape):
        return self.stack.enter_context(self.nc.psum_tensor(f"{self.tag}_{name}", shape, F32))

    def sem(self, name):
        return self.stack.enter_context(self.nc.semaphore(f"{self.tag}_{name}"))


def constants(nc, ident, tri):
    with ExitStack() as stack:
        room = Room(nc, stack, "const")
        filled = room.sem("filled")
        shaped = room.sem("shaped")
        block = stack.enter_context(nc.Block())

        @block.gpsimd
        def _(pool):
            nc.gpsimd.memset(ident[:], 0.0).then_inc(filled, 1)
            nc.gpsimd.memset(tri[:], 1.0).then_inc(filled, 1)
            pool.wait_ge(filled, 2)
            nc.gpsimd.affine_select(out=ident[:], in_=ident[:], compare_op=ALU.not_equal, fill=1.0, base=0,
                                    pattern=[[-1, P]], channel_multiplier=1).then_inc(shaped, 1)
            nc.gpsimd.affine_select(out=tri[:], in_=tri[:], compare_op=ALU.is_ge, fill=0.0, base=0,
                                    pattern=[[1, P]], channel_multiplier=-1).then_inc(shaped, 1)
            pool.wait_ge(shaped, 2)


def linear_attention(nc, X, nkv, ident, tri, x, ctx, weights, biases):
    E = D // H
    NE = E + 1
    QK = 2 * D
    with ExitStack() as stack:
        room = Room(nc, stack, "lin")
        w_rows = room.sbuf("w_rows", [P, 4, D])
        w_qkv = room.sbuf("w_qkv", [P, 3 * D])
        w_o = room.sbuf("w_o", [P, D])
        b_qkv = room.sbuf("b_qkv", [P, 3 * D])
        b_o = room.sbuf("b_o", [P, D])
        x_rows = room.sbuf("x_rows", [P, 2, D])
        c_rows = room.sbuf("c_rows", [C, 2, D])
        xT = room.sbuf("xT", [P, 2, S])
        z = room.sbuf("z", [P, 2, 3 * D])
        mag = room.sbuf("mag", [P, QK])
        dec = room.sbuf("dec", [P, QK])
        log = room.sbuf("log", [P, 2, QK])
        qk = room.sbuf("qk", [P, 2, QK])
        kv = room.sbuf("kv", [P, 2, E, H, E])
        prod = room.sbuf("prod", [P, NE, H, E])
        numden = room.sbuf("numden", [P, NE, H])
        inv = room.sbuf("inv", [P, H])
        att = room.sbuf("att", [P, 2, H, E])
        attT = room.sbuf("attT", [P, 2, S])
        stat = room.sbuf("stat", [P, 3, 6])
        mom = room.sbuf("mom", [P, 3, 2, 2])
        rstd = room.sbuf("rstd", [P, 3, 2])
        vare = room.sbuf("vare", [P, 3, 2])
        half = room.sbuf("half", [P, 1])
        nlat = room.sbuf("nlat", [P, 2, D])
        nctx = room.sbuf("nctx", [C, 2, D])
        ps_xT = room.psum("ps_xT", [P, 512])
        ps_qkv = room.psum("ps_qkv", [P, 512])
        ps_cum = room.psum("ps_cum", [P, 3 * 512])
        ps_aT = room.psum("ps_aT", [P, 512])
        ps_y = room.psum("ps_y", [P, 2, 512])

        w_loaded = room.sem("w_loaded")
        b_loaded = room.sem("b_loaded")
        res_loaded = [room.sem(f"res_loaded{n}") for n in range(4)]
        x_loaded = [room.sem(f"x_loaded{n}") for n in range(2)]
        c_loaded = [room.sem(f"c_loaded{n}") for n in range(2)]
        lat_stored = [room.sem(f"lat_stored{n}") for n in range(2)]
        ctx_stored = [room.sem(f"ctx_stored{n}") for n in range(2)]
        wT_psum, wT_ready = room.sem("wT_psum"), room.sem("wT_ready")
        half_ready = room.sem("half_ready")
        xT_psum, xT_ready = room.sem("xT_psum"), room.sem("xT_ready")
        qkv_psum, z_ready = room.sem("qkv_psum"), room.sem("z_ready")
        mag_ready, dec_ready, log_ready = room.sem("mag_ready"), room.sem("dec_ready"), room.sem("log_ready")
        qk_ready, kv_ready = room.sem("qk_ready"), room.sem("kv_ready")
        cum_psum, prod_ready = room.sem("cum_psum"), room.sem("prod_ready")
        numden_ready, inv_ready, att_ready = room.sem("numden_ready"), room.sem("inv_ready"), room.sem("att_ready")
        aT_psum, aT_ready, y_psum = room.sem("aT_psum"), room.sem("aT_ready"), room.sem("y_psum")
        res_ready, sum_ready = room.sem("res_ready"), room.sem("sum_ready")
        stat_ready = [room.sem(f"stat_ready{k}") for k in range(3)]
        mom_ready = [room.sem(f"mom_ready{k}") for k in range(3)]
        vare_ready = [room.sem(f"vare_ready{k}") for k in range(3)]
        rstd_ready = [room.sem(f"rstd_ready{k}") for k in range(3)]
        x1_ready, nlat_ready, nctx_ready = room.sem("x1_ready"), room.sem("nlat_ready"), room.sem("nctx_ready")
        block = stack.enter_context(nc.Block())
        QUART = B // 4

        @block.sync
        def _(sp):
            for n, w in enumerate(weights):
                sp.dma_start(w_rows[:, n, :], w).then_inc(w_loaded, 16)
            for n in range(3):
                sp.dma_start(b_qkv[:, n * D:(n + 1) * D],
                             biases[n].rearrange("(o d) -> o d", o=1).broadcast_to([P, D])).then_inc(b_loaded, 16)
            sp.dma_start(b_o[:], biases[3].rearrange("(o d) -> o d", o=1).broadcast_to([P, D])).then_inc(b_loaded, 16)

            for n in range(4):
                sp.dma_start(X[:, n * QUART * D:(n + 1) * QUART * D].rearrange("s (b d) -> s b d", d=D),
                             x[n * QUART:(n + 1) * QUART].rearrange("b s d -> s b d")).then_inc(res_loaded[n], 16)

            def step(t, par):
                if there(t):
                    wait(sp, xT_psum, t - 1)
                    sp.dma_start(x_rows[:, par, :], x[bass.ds(t, 1)].rearrange("o s d -> s (o d)")
                                 ).then_inc(x_loaded[par], 16)
                    wait(sp, nctx_ready, t - 1)
                    sp.dma_start(c_rows[:, par, :], ctx[bass.ds(t, 1)].rearrange("o s d -> s (o d)")
                                 ).then_inc(c_loaded[par], 16)

            pipelined(sp, step)

        @block.gpsimd
        def _(pool):
            nc.gpsimd.memset(half[:], -0.5).then_inc(half_ready, 1)
            pool.wait_ge(half_ready, 1)
            pool.wait_ge(b_loaded, 64)
            for n in range(4):
                pool.wait_ge(res_loaded[n], 16)

            def inverse_deviation(k, rows, s, par):
                wait_apart(pool, half_ready, (mom_ready[k], s + 1))
                nc.gpsimd.tensor_scalar(vare[0:rows, k, par:par + 1], mom[0:rows, k, par, 1:2], EPS, None,
                                        ALU.add).then_inc(vare_ready[k], 1)
                pool.wait_ge(vare_ready[k], s + 1)
                nc.gpsimd.tensor_tensor(rstd[0:rows, k, par:par + 1], vare[0:rows, k, par:par + 1],
                                        half[0:rows, :], ALU.pow).then_inc(rstd_ready[k], 1)

            def step(t, par):
                s2 = t - 2
                if there(t):
                    nc.gpsimd.tensor_tensor(X[:, bass.ds(t * D, D)], X[:, bass.ds(t * D, D)], b_o[:],
                                            ALU.add).then_inc(res_ready, 1)
                if there(s2):
                    inverse_deviation(0, P, s2, par)
                    inverse_deviation(1, P, s2, par)
                if there(t):
                    inverse_deviation(2, C, t, par)
                    pool.wait_ge(z_ready, t + 1)
                    pool.wait_ge(qk_ready, t + 1)
                    wait(pool, cum_psum, t - 1)
                    k = qk[:, par, D:QK].rearrange("p (h d) -> p h d", h=H)
                    v = z[:, par, QK:3 * D].rearrange("p (h e) -> p e h", h=H)
                    nc.gpsimd.tensor_tensor(kv[:, par], k.unsqueeze(1).broadcast_to([P, E, H, E]),
                                            v.unsqueeze(3).broadcast_to([P, E, H, E]), ALU.mult
                                            ).then_inc(kv_ready, 1)

            pipelined(pool, step)

        @block.scalar
        def _(act):
            for n in range(4):
                act.wait_ge(wT_psum, 4)
                dst = w_qkv[:, n * D:(n + 1) * D] if n < 3 else w_o[:]
                nc.scalar.copy(dst, ps_xT[:, n * D:(n + 1) * D]).then_inc(wT_ready, 1)

            def step(t, par):
                s2, s1, s3 = t - 2, t - 1, t - 3
                if there(t):
                    act.wait_ge(xT_psum, t + 1)
                    wait(act, qkv_psum, t - 1)
                    nc.scalar.copy(xT[:, par, :], ps_xT[:, 0:S]).then_inc(xT_ready, 1)
                if there(s2):
                    act.wait_ge(aT_psum, s2 + 1)
                    wait(act, y_psum, s2 - 1)
                    nc.scalar.copy(attT[:, par, :], ps_aT[:, 0:S]).then_inc(aT_ready, 1)
                if there(s1):
                    act.wait_ge(nctx_ready, s1 + 1)
                    act.dma_start(nkv[bass.ds(s1, 1), 0:C, :].rearrange("o s d -> s (o d)"),
                                  nctx[0:C, 1 - par, :]).then_inc(ctx_stored[1 - par], 16)
                if there(s3):
                    act.wait_ge(nlat_ready, s3 + 1)
                    act.dma_start(nkv[bass.ds(s3, 1), C:C + S, :].rearrange("o s d -> s (o d)"),
                                  nlat[:, 1 - par, :]).then_inc(lat_stored[1 - par], 16)
                if there(t):
                    act.wait_ge(z_ready, t + 1)
                    wait(act, dec_ready, t)
                    nc.scalar.activation(mag[:], z[:, par, 0:QK], ACT.Abs).then_inc(mag_ready, 1)
                    act.wait_ge(mag_ready, t + 1)
                    wait(act, log_ready, t)
                    nc.scalar.activation(dec[:], mag[:], ACT.Exp, scale=-1.0).then_inc(dec_ready, 1)
                    act.wait_ge(dec_ready, t + 1)
                    wait(act, qk_ready, t - 1)
                    nc.scalar.activation(log[:, par, :], dec[:], ACT.Ln, bias=1.0).then_inc(log_ready, 1)

            pipelined(act, step)
            for par in range(2):
                act.wait_ge(lat_stored[par], 16 * B // 2)
                act.wait_ge(ctx_stored[par], 16 * B // 2)

        @block.vector
        def _(dve):
            dve.wait_ge(b_loaded, 64)

            def moments(k, rows, source, rows_ready, s, par):
                wait_apart(dve, b_loaded, rows_ready, (mom_ready[k], s))
                nc.vector.bn_stats(stat[0:rows, k, :], source).then_inc(stat_ready[k], 1)
                wait_apart(dve, b_loaded, (stat_ready[k], s + 1))
                nc.vector.bn_aggr(mom[0:rows, k, par, :], stat[0:rows, k, :]).then_inc(mom_ready[k], 1)

            def step(t, par):
                s2, s1 = t - 2, t - 1
                if there(s2):
                    Xs = X[:, bass.ds(s2 * D, D)]
                    dve.wait_ge(y_psum, s2 + 1)
                    dve.wait_ge(res_ready, s2 + 1)
                    nc.vector.tensor_tensor(Xs, ps_y[:, par, 0:D], Xs, ALU.add).then_inc(sum_ready, 1)
                    moments(0, P, Xs, (sum_ready, s2 + 1), s2, par)
                if there(t):
                    dve.wait_ge(qkv_psum, t + 1)
                    wait(dve, kv_ready, t - 1)
                    nc.vector.tensor_tensor(z[:, par, :], ps_qkv[:, 0:3 * D], b_qkv[:], ALU.add).then_inc(z_ready, 1)
                if there(s1):
                    dve.wait_ge(cum_psum, s1 + 1)
                    wait(dve, numden_ready, s1)
                    q = qk[:, 1 - par, 0:D].rearrange("p (o f) -> p o f", o=1).broadcast_to([P, NE, D])
                    nc.vector.tensor_tensor(prod[:].rearrange("p e h d -> p e (h d)"),
                                            ps_cum[:, 0:NE * D].rearrange("p (e f) -> p e f", e=NE), q,
                                            ALU.mult).then_inc(prod_ready, 1)
                    dve.wait_ge(prod_ready, s1 + 1)
                    wait(dve, att_ready, s1)
                    nc.vector.tensor_reduce(numden[:], prod[:], AX, ALU.add).then_inc(numden_ready, 1)
                    dve.wait_ge(numden_ready, s1 + 1)
                    nc.vector.reciprocal(inv[:], numden[:, E, :]).then_inc(inv_ready, 1)
                    dve.wait_ge(inv_ready, s1 + 1)
                    wait(dve, aT_psum, s1 - 1)
                    nc.vector.tensor_tensor(att[:, 1 - par].rearrange("p h e -> p e h"), numden[:, 0:E, :],
                                            inv[:].unsqueeze(1).broadcast_to([P, E, H]), ALU.mult
                                            ).then_inc(att_ready, 1)
                if there(s2):
                    dve.wait_ge(rstd_ready[0], s2 + 1)
                    nc.vector.tensor_scalar(Xs, Xs, mom[:, 0, par, 0:1], rstd[:, 0, par:par + 1], ALU.subtract,
                                            ALU.mult).then_inc(x1_ready, 1)
                    moments(1, P, Xs, (x1_ready, s2 + 1), s2, par)
                if there(t):
                    moments(2, C, c_rows[:, par, :], (c_loaded[par], landed(t, par)), t, par)
                    dve.wait_ge(log_ready, t + 1)
                    wait(dve, cum_psum, t - 1)
                    nc.vector.scalar_tensor_tensor(qk[:, par, :], z[:, par, 0:QK], 0.0, log[:, par, :], ALU.max,
                                                   ALU.add).then_inc(qk_ready, 1)
                if there(s2):
                    dve.wait_ge(rstd_ready[1], s2 + 1)
                    wait(dve, lat_stored[par], landed(s2, par) - 16)
                    nc.vector.tensor_scalar(nlat[:, par, :], Xs, mom[:, 1, par, 0:1], rstd[:, 1, par:par + 1],
                                            ALU.subtract, ALU.mult).then_inc(nlat_ready, 1)
                if there(t):
                    dve.wait_ge(rstd_ready[2], t + 1)
                    wait(dve, ctx_stored[par], landed(t, par) - 16)
                    nc.vector.tensor_scalar(nctx[:, par, :], c_rows[:, par, :], mom[0:C, 2, par, 0:1],
                                            rstd[0:C, 2, par:par + 1], ALU.subtract, ALU.mult
                                            ).then_inc(nctx_ready, 1)

            pipelined(dve, step)

        @block.tensor
        def _(pe):
            pe.wait_ge(w_loaded, 64)
            for n in range(4):
                nc.tensor.transpose(ps_xT[:, n * D:(n + 1) * D], w_rows[:, n, :], ident[:]).then_inc(wT_psum, 1)
            pe.wait_ge(wT_ready, 4)

            def step(t, par):
                s2, s1 = t - 2, t - 1
                if there(t):
                    pe.wait_ge(x_loaded[par], landed(t, par))
                    wait(pe, xT_ready, t)
                    nc.tensor.transpose(ps_xT[:, 0:S], x_rows[:, par, :], ident[:]).then_inc(xT_psum, 1)
                if there(s2):
                    pe.wait_ge(att_ready, s2 + 1)
                    wait(pe, aT_ready, s2)
                    nc.tensor.transpose(ps_aT[:, 0:S], att[:, par].rearrange("p h e -> p (h e)"), ident[:]
                                        ).then_inc(aT_psum, 1)
                if there(t):
                    pe.wait_ge(xT_ready, t + 1)
                    wait(pe, z_ready, t)
                    nc.tensor.matmul(ps_qkv[:, 0:3 * D], xT[:, par, :], w_qkv[:], start=True, stop=True
                                     ).then_inc(qkv_psum, 1)
                if there(s2):
                    pe.wait_ge(aT_ready, s2 + 1)
                    wait(pe, sum_ready, s2 - 1)
                    nc.tensor.matmul(ps_y[:, par, 0:D], attT[:, par, :], w_o[:], start=True, stop=True
                                     ).then_inc(y_psum, 1)
                if there(s1):
                    pe.wait_ge(kv_ready, s1 + 1)
                    wait(pe, prod_ready, s1)
                    flat = kv[:, 1 - par].rearrange("p e h d -> p (e h d)")
                    for n in range(2):
                        nc.tensor.matmul(ps_cum[:, n * 512:(n + 1) * 512], tri[:], flat[:, n * 512:(n + 1) * 512],
                                         start=True, stop=True)
                    nc.tensor.matmul(ps_cum[:, 1024:1024 + D], tri[:], qk[:, 1 - par, D:QK], start=True, stop=True
                                     ).then_inc(cum_psum, 1)

            pipelined(pe, step)


def split_product(nc, out, stationary, moving, last=True):
    nc.tensor.matmul(out, stationary[0], moving[1], start=True, stop=False)
    nc.tensor.matmul(out, stationary[1], moving[0], start=False, stop=False)
    return nc.tensor.matmul(out, stationary[0], moving[0], start=False, stop=True)


def cross_attention(nc, X, nkv, ident, gains, w_q, w_kv, w_out):
    DH = 64
    I = H * DH
    K = C + S
    KT = K // 2
    PAIRS = H // 2
    UNITS = 2 * PAIRS
    ROUNDS = B // 2
    with ExitStack() as stack:
        room = Room(nc, stack, "x")
        wq = room.sbuf("wq", [P, I])
        wkv = room.sbuf("wkv", [P, 2 * I])
        wqT = room.sbuf("wqT", [P, PAIRS, D])
        wkT = room.sbuf("wkT", [P, PAIRS, D])
        M_part = [room.sbuf(f"M_{n}", [P, H, D], F32R) for n in ("hi", "lo")]
        wv_part = [room.sbuf(f"wv_{n}", [P, I], F32R) for n in ("hi", "lo")]
        wo = room.sbuf("wo", [P, PAIRS, D])
        gain = room.sbuf("gain", [P, 4])
        nk = room.sbuf("nk", [KT, 2, 2, 2, D])
        kT_full = room.sbuf("kT_full", [P, 2, K])
        kT_part = [room.sbuf(f"kT_{n}", [P, 2, 2, K], F32R) for n in ("hi", "lo")]
        G_part = [room.sbuf(f"G_{n}", [P, 2, 2, 2, S], F32R) for n in ("hi", "lo")]
        V = room.sbuf("V", [KT, 2, 2, 2, I // 2])
        nmax = room.sbuf("nmax", [P, 2, 2])
        total = room.sbuf("total", [P, 2, 2])
        inv = room.sbuf("inv", [P, 2, 2])
        prob = room.sbuf("prob", [P, 2, 2, K])
        probT = room.sbuf("probT", [KT, 2, 2, 2, S])
        outT = room.sbuf("outT", [P, 2, 2, PAIRS // 2, S])
        hsum = room.sbuf("hsum", [P, 2, D])
        stat = room.sbuf("stat", [P, 2, 6])
        mom = room.sbuf("mom", [P, 2, 2])
        vare = room.sbuf("vare", [P, 2])
        rstd = room.sbuf("rstd", [P, 2])
        half = room.sbuf("half", [P, 1])
        xnew = room.sbuf("xnew", [P, 2, D])
        ps_S = room.psum("ps_S", [P, 2, 512])
        ps_T = room.psum("ps_T", [P, 2, 512])
        ps_O = room.psum("ps_O", [P, 2, 512])
        ps_G = room.psum("ps_G", [P, 512])
        ps_V = room.psum("ps_V", [P, 512])

        w_loaded, g_loaded = room.sem("w_loaded"), room.sem("g_loaded")
        nk_loaded = [room.sem(f"nk_loaded{n}") for n in range(2)]
        wT_psum, wT_ready = room.sem("wT_psum"), room.sem("wT_ready")
        M_psum, M_hi_ready, M_lo_ready = room.sem("M_psum"), room.sem("M_hi_ready"), room.sem("M_lo_ready")
        wv_hi_ready, wv_lo_ready = room.sem("wv_hi_ready"), room.sem("wv_lo_ready")
        kT_psum, kT_ready = room.sem("kT_psum"), room.sem("kT_ready")
        kT_hi_ready, kT_lo_ready = room.sem("kT_hi_ready"), room.sem("kT_lo_ready")
        G_psum, G_hi_ready, G_lo_ready = room.sem("G_psum"), room.sem("G_hi_ready"), room.sem("G_lo_ready")
        V_psum, V_ready = room.sem("V_psum"), room.sem("V_ready")
        S_psum, max_ready, exp_ready = room.sem("S_psum"), room.sem("max_ready"), room.sem("exp_ready")
        inv_ready, prob_ready = room.sem("inv_ready"), room.sem("prob_ready")
        T_psum, probT_ready, O_psum = room.sem("T_psum"), room.sem("probT_ready"), room.sem("O_psum")
        outT_ready, y_psum = room.sem("outT_ready"), room.sem("y_psum")
        sum_ready, stat_ready, mom_ready = room.sem("sum_ready"), room.sem("stat_ready"), room.sem("mom_ready")
        half_ready, vare_ready, rstd_ready = room.sem("half_ready"), room.sem("vare_ready"), room.sem("rstd_ready")
        xnew_ready, x2_ready = room.sem("xnew_ready"), room.sem("x2_ready")
        block = stack.enter_context(nc.Block())

        def rounds(engine, body):
            with engine.Fori(0, ROUNDS // 2) as i:
                for parity in range(2):
                    body(i * 2 + parity, parity)

        @block.sync
        def _(sp):
            sp.dma_start(wq[:], w_q).then_inc(w_loaded, 16)
            sp.dma_start(wkv[:], w_kv).then_inc(w_loaded, 16)
            sp.dma_start(wo[:], w_out.rearrange("(j p) d -> p j d", p=P)).then_inc(w_loaded, 16)
            for n, g in enumerate(gains):
                sp.dma_start(gain[:, n:n + 1], g.rearrange("(d o) -> d o", o=1)).then_inc(g_loaded, 16)

            def load(r, b, par):
                for u in range(2):
                    sp.dma_start(nk[:, par, u], nkv[bass.ds(b + u, 1)].rearrange("o (t k) d -> k (o t) d", t=2)
                                 ).then_inc(nk_loaded[par], 16)

            load(0, 0, 0)
            load(1, 2, 1)
            with sp.Fori(1, ROUNDS // 2) as i:
                for par in range(2):
                    sp.wait_ge(kT_psum, i * 2 + par - 1)
                    load(i * 2 + par, i * 4 + par * 2, par)
            sp.wait_ge(kT_psum, ROUNDS - 1)
            load(ROUNDS, 0, 0)

        @block.gpsimd
        def _(pool):
            nc.gpsimd.memset(half[:], -0.5).then_inc(half_ready, 1)
            pool.wait_ge(half_ready, 1)
            pool.sem_inc(x2_ready, 2)

            def split_keys(n, par):
                wait_apart(pool, half_ready, (kT_ready, n + 1))
                nc.gpsimd.tensor_copy(kT_part[0][:, par], kT_full[:]).then_inc(kT_hi_ready, 1)
                pool.wait_ge(kT_hi_ready, n + 1)
                nc.gpsimd.tensor_tensor(kT_part[1][:, par], kT_full[:], kT_part[0][:, par].bitcast(F32), ALU.subtract
                                        ).then_inc(kT_lo_ready, 1)

            def normalise(r, u):
                n = r * 2 + u
                wait_apart(pool, half_ready, (mom_ready, n + 1))
                nc.gpsimd.tensor_scalar(vare[:, u:u + 1], mom[:, u, 1:2], EPS, None, ALU.add).then_inc(vare_ready, 1)
                pool.wait_ge(vare_ready, n + 1)
                nc.gpsimd.tensor_tensor(rstd[:, u:u + 1], vare[:, u:u + 1], half[:], ALU.pow).then_inc(rstd_ready, 1)
                wait_apart(pool, half_ready, (rstd_ready, n + 1))
                nc.gpsimd.tensor_scalar(xnew[:, u, :], hsum[:, u, :], mom[:, u, 0:1], rstd[:, u:u + 1], ALU.subtract,
                                        ALU.mult).then_inc(xnew_ready, 1)
                wait_apart(pool, half_ready, (xnew_ready, n + 1))
                nc.gpsimd.tensor_copy(X[:, bass.ds(n * D, D)], xnew[:, u, :]).then_inc(x2_ready, 1)

            def body(r, par):
                split_keys(r + 1, 1 - par)
                normalise(r, 0)
                normalise(r, 1)

            split_keys(0, 0)
            rounds(pool, body)

        @block.scalar
        def _(act):
            for n in range(4):
                act.wait_ge(wT_psum, n + 1)
                dst = (wqT, wkT)[n // 2]
                nc.scalar.copy(dst[:, n % 2 * 4:n % 2 * 4 + 4, :], ps_S[:, n % 2, :]).then_inc(wT_ready, 1)
            for n in range(4):
                act.wait_ge(M_psum, n + 1)
                nc.scalar.mul(M_part[0][:, n // 2 * 8 + n % 2:n // 2 * 8 + n % 2 + 7:2, :], ps_T[:, n % 2, :],
                              DH ** -0.5).then_inc(M_hi_ready, 1)
            act.wait_ge(w_loaded, 48)
            nc.scalar.copy(wv_part[0][:], wkv[:, I:2 * I]).then_inc(wv_hi_ready, 1)

            def G_hi(n, pair):
                act.wait_ge(G_psum, n + 1)
                nc.scalar.copy(G_part[0][:, pair], ps_G[:]).then_inc(G_hi_ready, 1)

            def V_copy(n, hf, u, tile):
                act.wait_ge(V_psum, n + 1)
                nc.scalar.copy(V[:, hf, u, tile, :], ps_V[0:KT, :]).then_inc(V_ready, 1)

            def exponentials(n, k):
                act.wait_ge(max_ready, n + 1)
                for h in range(2):
                    last = nc.scalar.activation(prob[:, k, h, :], ps_S[:, k, h * K:(h + 1) * K], ACT.Exp,
                                                bias=nmax[:, k, h:h + 1], accum_out=total[:, k, h:h + 1])
                last.then_inc(exp_ready, 1)

            def out_copy(n, u, hf, av):
                act.wait_ge(O_psum, av)
                nc.scalar.copy(outT[:, u, hf], ps_O[:, u, :]).then_inc(outT_ready, 1)

            def body(r, par):
                unit = r * UNITS
                for s in range(UNITS):
                    if s in (UNITS // 2 - 1, UNITS // 2, UNITS - 1):
                        out_copy(None, (s - 1) % 2, (s - 1) // (UNITS // 2), unit + s)
                    act.wait_ge(T_psum, unit + s + 1)
                    nc.scalar.copy(probT[:, s % 2], ps_T[0:KT, s % 2, :]).then_inc(probT_ready, 1)
                    if s % 2 == 0:
                        G_hi(r * PAIRS + s // 2 + 2, s // 2 % 2)
                    elif s < UNITS - 1:
                        k = s // 2
                        V_copy(r * 8 + 4 + k, 1 - k // 4, k % 4 // 2, k % 2)
                    exponentials(unit + s + 2, s % 2)
                out_copy(None, 1, 1, unit + UNITS)
                V_copy(r * 8 + 4 + 7, 0, 1, 1)

            for k in range(4):
                V_copy(k, 0, k // 2, k % 2)
            for j in range(2):
                G_hi(j, j)
            for k in range(2):
                exponentials(k, k)
            rounds(act, body)

        @block.vector
        def _(dve):
            for n in range(4):
                dve.wait_ge(M_hi_ready, n + 1)
                heads = slice(n // 2 * 8 + n % 2, n // 2 * 8 + n % 2 + 7, 2)
                nc.vector.scalar_tensor_tensor(M_part[1][:, heads, :], ps_T[:, n % 2, :].rearrange("p (h d) -> p h d", h=4),
                                               DH ** -0.5, M_part[0][:, heads, :].bitcast(F32), ALU.mult, ALU.subtract
                                               ).then_inc(M_lo_ready, 1)
            dve.wait_ge(wv_hi_ready, 1)
            nc.vector.tensor_tensor(wv_part[1][:], wkv[:, I:2 * I], wv_part[0][:].bitcast(F32), ALU.subtract
                                    ).then_inc(wv_lo_ready, 1)
            dve.wait_ge(g_loaded, 64)

            def keys(n):
                dve.wait_ge(kT_psum, n + 1)
                wait(dve, kT_lo_ready, n)
                rows = ps_V[:, 0:2 * K].rearrange("p (u k) -> p u k", u=2)
                nc.vector.tensor_scalar(kT_full[:, :, 0:C], rows[:, :, 0:C], gain[:, 0:1], gain[:, 1:2], ALU.mult, ALU.add)
                nc.vector.tensor_scalar(kT_full[:, :, C:K], rows[:, :, C:K], gain[:, 2:3], gain[:, 3:4], ALU.mult, ALU.add
                                        ).then_inc(kT_ready, 1)

            def G_lo(n, pair):
                dve.wait_ge(G_hi_ready, n + 1)
                nc.vector.tensor_tensor(G_part[1][:, pair].rearrange("p h u q -> p (h u q)"), ps_G[:],
                                        G_part[0][:, pair].bitcast(F32).rearrange("p h u q -> p (h u q)"), ALU.subtract
                                        ).then_inc(G_lo_ready, 1)

            def maxima(n, k):
                dve.wait_ge(S_psum, n + 1)
                nc.vector.tensor_reduce(nmax[:, k, :], ps_S[:, k, 0:2 * K].rearrange("p (h k) -> p h k", h=2), AX,
                                        ALU.max, negate=True).then_inc(max_ready, 1)

            def normal(n, k):
                dve.wait_ge(exp_ready, n + 1)
                nc.vector.reciprocal(inv[:, k, :], total[:, k, :]).then_inc(inv_ready, 1)
                dve.wait_ge(inv_ready, n + 1)
                for h in range(2):
                    last = nc.vector.tensor_scalar(prob[:, k, h, :], prob[:, k, h, :], inv[:, k, h:h + 1], None, ALU.mult)
                last.then_inc(prob_ready, 1)

            def residual(r, u):
                n = r * 2 + u
                dve.wait_ge(y_psum, n + 1)
                dve.wait_ge(x2_ready, n + 1)
                nc.vector.tensor_tensor(hsum[:, u, :], ps_G[:, 0:D], X[:, bass.ds(n * D, D)], ALU.add).then_inc(sum_ready, 1)
                dve.wait_ge(sum_ready, n + 2)
                nc.vector.bn_stats(stat[:, u, :], hsum[:, u, :]).then_inc(stat_ready, 1)
                wait_apart(dve, wv_hi_ready, (stat_ready, n + 1))
                nc.vector.bn_aggr(mom[:, u, :], stat[:, u, :]).then_inc(mom_ready, 1)

            def body(r, par):
                unit = r * UNITS
                for s in range(UNITS):
                    normal(unit + s + 1, (s + 1) % 2)
                    maxima(unit + s + 2, s % 2)
                    if s % 2 == 0:
                        G_lo(r * PAIRS + s // 2 + 2, s // 2 % 2)
                    if s == 4:
                        keys(r + 1)
                residual(r, 0)
                residual(r, 1)

            keys(0)
            for j in range(2):
                G_lo(j, j)
            dve.wait_ge(G_lo_ready, 2)
            dve.sem_inc(sum_ready, 1)
            maxima(0, 0)
            normal(0, 0)
            maxima(1, 1)
            rounds(dve, body)

        @block.tensor
        def _(pe):
            pe.wait_ge(w_loaded, 48)
            for n in range(4):
                if n >= 2:
                    pe.wait_ge(wT_ready, n - 1)
                src = (wq, wkv)[n // 2]
                for j in range(4):
                    jj = n % 2 * 4 + j
                    last = nc.tensor.transpose(ps_S[:, n % 2, j * D:(j + 1) * D], src[:, jj * D:(jj + 1) * D], ident[:])
                last.then_inc(wT_psum, 1)
            pe.wait_ge(wT_ready, 4)
            for n in range(4):
                if n >= 2:
                    pe.wait_ge(M_lo_ready, n - 1)
                odd = n % 2 * DH
                for j in range(4):
                    jj = n // 2 * 4 + j
                    last = nc.tensor.matmul(ps_T[:, n % 2, j * D:(j + 1) * D], wqT[odd:odd + DH, jj, :],
                                            wkT[odd:odd + DH, jj, :], start=True, stop=True)
                last.then_inc(M_psum, 1)
            pe.wait_ge(M_lo_ready, 4)
            pe.wait_ge(wv_lo_ready, 1)

            def keys(n, par):
                pe.wait_ge(nk_loaded[par], (n - par) * 16 + 32)
                for u in range(2):
                    for tile in range(2):
                        at = u * K + tile * KT
                        last = nc.tensor.transpose(ps_V[:, at:at + KT], nk[:, par, u, tile, :], ident[0:KT, 0:KT])
                last.then_inc(kT_psum, 1)

            def make_G(pair, keys_par, j):
                for h in range(2):
                    last = split_product(nc, ps_G[:, h * 256:(h + 1) * 256], [m[:, 2 * j + h, :] for m in M_part],
                                         [k[:, keys_par, :, C:K] for k in kT_part])
                last.then_inc(G_psum, 1)

            def make_V(keys_par, hf, u, tile):
                split_product(nc, ps_V[0:KT, :], [k[:, keys_par, u, tile * KT:(tile + 1) * KT] for k in kT_part],
                              [w[:, hf * 512:(hf + 1) * 512] for w in wv_part]).then_inc(V_psum, 1)

            def scores(n, k, keys_par, pair):
                for h in range(2):
                    last = split_product(nc, ps_S[:, k, h * K:(h + 1) * K], [g[:, pair, h, k, :] for g in G_part],
                                         [t[:, keys_par, k, :] for t in kT_part])
                last.then_inc(S_psum, 1)

            def output(n, u):
                for j in range(PAIRS):
                    last = nc.tensor.matmul(ps_G[:, 0:D], outT[:, u, j // 4, j % 4, :], wo[:, j, :], start=(j == 0),
                                            stop=(j == PAIRS - 1))
                last.then_inc(y_psum, 1)

            def body(r, par):
                unit = r * UNITS
                for s in range(UNITS):
                    j, u = s // 2, s % 2
                    pe.wait_ge(prob_ready, unit + s + 1)
                    for h in range(2):
                        for tile in range(2):
                            at = (h * 2 + tile) * S
                            last = nc.tensor.transpose(ps_T[0:KT, u, at:at + S], prob[:, u, h, tile * KT:(tile + 1) * KT],
                                                       ident[:])
                    last.then_inc(T_psum, 1)
                    ahead = j + 1
                    if u == 0:
                        pe.wait_ge(G_lo_ready, r * PAIRS + ahead + 1)
                    scores(unit + s + 2, u, par if ahead < PAIRS else 1 - par, ahead % 2)
                    if u == 0:
                        if s == 0:
                            pe.wait_ge(sum_ready, r * 2 + 1)
                        if s == 12:
                            pe.wait_ge(kT_lo_ready, r + 2)
                        make_G(j % 2, par if j + 2 < PAIRS else 1 - par, (j + 2) % PAIRS)
                    elif s < UNITS - 1:
                        if s != 5:
                            pe.wait_ge(V_ready, r * 8 + 4 + j)
                        else:
                            pe.wait_ge(kT_ready, r + 2)
                        if s == 9:
                            pe.wait_ge(kT_lo_ready, r + 2)
                        make_V(par if j < 4 else 1 - par, 1 - j // 4, j % 4 // 2, j % 2)
                    else:
                        pe.wait_ge(outT_ready, r * 4 + 3)
                        pe.wait_ge(G_lo_ready, r * PAIRS + 10)
                        output(None, 0)
                    if s == 4:
                        pe.wait_ge(V_ready, r * 8 + 4 + 2)
                        keys(r + 1, 1 - par)
                    pe.wait_ge(probT_ready, unit + s + 1)
                    if s in (0, 8):
                        pe.wait_ge(V_ready, r * 8 + 4 + s // 2)
                    if s in (8, 9):
                        pe.wait_ge(outT_ready, r * 4 + s - 7)
                    for tile in range(2):
                        for h in range(2):
                            last = nc.tensor.matmul(ps_O[h * DH:(h + 1) * DH, u, j % 4 * S:(j % 4 + 1) * S],
                                                    V[:, j // 4, u, tile, (j % 4 * 2 + h) * DH:(j % 4 * 2 + h + 1) * DH],
                                                    probT[:, u, h, tile, :], start=(tile == 0), stop=(tile == 1))
                    last.then_inc(O_psum, 1)
                pe.wait_ge(V_ready, r * 8 + 4 + 7)
                make_V(1 - par, 0, 1, 1)
                pe.wait_ge(outT_ready, r * 4 + 4)
                pe.wait_ge(sum_ready, r * 2 + 2)
                output(None, 1)

            keys(0, 0)
            pe.wait_ge(kT_lo_ready, 1)
            for k in range(4):
                if k:
                    pe.wait_ge(V_ready, k)
                make_V(0, 0, k // 2, k % 2)
            for j in range(2):
                if j:
                    pe.wait_ge(G_lo_ready, j)
                make_G(j, 0, j)
            for k in range(2):
                if k == 0:
                    pe.wait_ge(G_lo_ready, 1)
                scores(k, k, 0, 0)
            rounds(pe, body)


EXPERTS = 8
GROUP = 4
TOKENS = GROUP * S
GROUPS = B // GROUP
ROUTE_SCALE = 2.5


def router(nc, X, ident, gate_w, combine):
    TOP = -16.0
    with ExitStack() as stack:
        room = Room(nc, stack, "r")
        gw_rows = room.sbuf("gw_rows", [EXPERTS, D])
        gw_part = [room.sbuf(f"gw_{n}", [P, EXPERTS], F32R) for n in ("hi", "lo")]
        x_rows = room.sbuf("x_rows", [P, 2, TOKENS])
        xT_part = [room.sbuf(f"xT_{n}", [P, 2, TOKENS], F32R) for n in ("hi", "lo")]
        logitT = room.sbuf("logitT", [EXPERTS, 2, TOKENS])
        logit = room.sbuf("logit", [P, B, EXPERTS])
        index = room.sbuf("index", [P, EXPERTS])
        shifted = room.sbuf("shifted", [P, B, EXPERTS])
        score = room.sbuf("score", [P, B, EXPERTS])
        rest = room.sbuf("rest", [P, B, EXPERTS])
        equal = room.sbuf("equal", [P, B, EXPERTS])
        order = room.sbuf("order", [P, B, EXPERTS])
        first = room.sbuf("first", [P, B, EXPERTS])
        second = room.sbuf("second", [P, B, EXPERTS])
        col = room.sbuf("col", [P, 10, B])
        ps_x = room.psum("ps_x", [P, 2, 512])
        ps_l = room.psum("ps_l", [P, 2, 512])
        ps_t = room.psum("ps_t", [P, 2, 512])
        gw_loaded, gw_psum = room.sem("gw_loaded"), room.sem("gw_psum")
        gw_hi_ready, gw_lo_ready = room.sem("gw_hi_ready"), room.sem("gw_lo_ready")
        x_ready, x_psum, hi_ready, lo_ready = (room.sem(n) for n in ("x_ready", "x_psum", "hi_ready", "lo_ready"))
        l_psum, logitT_ready = room.sem("l_psum"), room.sem("logitT_ready")
        t_psum, logit_ready = room.sem("t_psum"), room.sem("logit_ready")
        index_ready, shifted_ready, exp_ready = room.sem("index_ready"), room.sem("shifted_ready"), room.sem("exp_ready")
        done = room.sem("done")
        block = stack.enter_context(nc.Block())

        @block.sync
        def _(sp):
            sp.dma_start(gw_rows[:], gate_w).then_inc(gw_loaded, 16)

        @block.gpsimd
        def _(pool):
            for e in range(EXPERTS):
                nc.gpsimd.memset(index[:, e:e + 1], float(e)).then_inc(index_ready, 1)

        @block.scalar
        def _(act):
            act.wait_ge(gw_psum, 1)
            nc.scalar.copy(gw_part[0][:], ps_t[:, 0, 0:EXPERTS]).then_inc(gw_hi_ready, 1)

            def step(t, par):
                s1 = t - 1
                if there(t, GROUPS):
                    act.wait_ge(x_psum, t + 1)
                    nc.scalar.copy(xT_part[0][:, par, :], ps_x[:, par, :]).then_inc(hi_ready, 1)
                if there(s1, GROUPS):
                    act.wait_ge(l_psum, s1 + 1)
                    nc.scalar.copy(logitT[:, 1 - par, :], ps_l[0:EXPERTS, 1 - par, :]).then_inc(logitT_ready, 1)

            pipelined(act, step, GROUPS, 4, 2)
            act.wait_ge(shifted_ready, 1)
            nc.scalar.activation(score[:], shifted[:], ACT.Exp).then_inc(exp_ready, 1)

        @block.tensor
        def _(pe):
            pe.wait_ge(gw_loaded, 16)
            nc.tensor.transpose(ps_t[:, 0, 0:EXPERTS], gw_rows[:], ident[0:EXPERTS, 0:EXPERTS]).then_inc(gw_psum, 1)
            pe.wait_ge(gw_lo_ready, 1)

            def step(t, par):
                s1, s2 = t - 1, t - 2
                if there(t, GROUPS):
                    pe.wait_ge(x_ready, t + 1)
                    wait(pe, lo_ready, t - 1)
                    for n in range(GROUP):
                        last = nc.tensor.transpose(ps_x[:, par, n * S:(n + 1) * S], x_rows[:, par, n * S:(n + 1) * S],
                                                   ident[:])
                    last.then_inc(x_psum, 1)
                if there(s1, GROUPS):
                    pe.wait_ge(lo_ready, s1 + 1)
                    wait(pe, logitT_ready, s1 - 1)
                    split_product(nc, ps_l[0:EXPERTS, 1 - par, :], [g[:] for g in gw_part],
                                  [x[:, 1 - par, :] for x in xT_part]).then_inc(l_psum, 1)
                if there(s2, GROUPS):
                    wait_apart(pe, gw_lo_ready, (logitT_ready, s2 + 1), (logit_ready, s2 - 1))
                    for n in range(GROUP):
                        last = nc.tensor.transpose(ps_t[:, par, n * EXPERTS:(n + 1) * EXPERTS],
                                                   logitT[:, par, n * S:(n + 1) * S], ident[0:EXPERTS, 0:EXPERTS])
                    last.then_inc(t_psum, 1)

            pipelined(pe, step, GROUPS, 4, 2)

        @block.vector
        def _(dve):
            dve.wait_ge(gw_hi_ready, 1)
            nc.vector.tensor_tensor(gw_part[1][:], ps_t[:, 0, 0:EXPERTS], gw_part[0][:].bitcast(F32), ALU.subtract
                                    ).then_inc(gw_lo_ready, 1)

            def step(t, par):
                s2 = t - 2
                if there(t, GROUPS):
                    wait(dve, x_psum, t - 1)
                    nc.vector.tensor_copy(x_rows[:, par, :], X[:, bass.ds(t * TOKENS, TOKENS)]).then_inc(x_ready, 1)
                    dve.wait_ge(hi_ready, t + 1)
                    nc.vector.tensor_tensor(xT_part[1][:, par, :], ps_x[:, par, :], xT_part[0][:, par, :].bitcast(F32),
                                            ALU.subtract).then_inc(lo_ready, 1)
                if there(s2, GROUPS):
                    dve.wait_ge(t_psum, s2 + 1)
                    nc.vector.tensor_copy(logit[:].rearrange("p b e -> p (b e)")[:, bass.ds(s2 * GROUP * EXPERTS, GROUP * EXPERTS)],
                                          ps_t[:, par, 0:GROUP * EXPERTS]).then_inc(logit_ready, 1)

            pipelined(dve, step, GROUPS, 4, 2)

            count = [0]

            def then(instruction):
                count[0] += 1
                instruction.then_inc(done, 1)
                dve.wait_ge(done, count[0])

            def across(column):
                return column.unsqueeze(2).broadcast_to([P, B, EXPERTS])

            top, z, inv_z, max1, at1, max2, at2, den, inv_den, w = (col[:, n, :] for n in range(10))
            indices = index[:].unsqueeze(1).broadcast_to([P, B, EXPERTS])
            dve.wait_ge(logit_ready, GROUPS)
            dve.wait_ge(index_ready, EXPERTS)
            then(nc.vector.tensor_reduce(top, logit[:], AX, ALU.max))
            nc.vector.tensor_tensor(shifted[:], logit[:], across(top), ALU.subtract).then_inc(shifted_ready, 1)
            dve.wait_ge(exp_ready, 1)
            then(nc.vector.tensor_reduce(z, score[:], AX, ALU.add))
            then(nc.vector.reciprocal(inv_z, z))
            then(nc.vector.tensor_tensor(score[:], score[:], across(inv_z), ALU.mult))

            def pick(values, largest, at, chosen):
                then(nc.vector.tensor_reduce(largest, values[:], AX, ALU.max))
                then(nc.vector.tensor_tensor(equal[:], values[:], across(largest), ALU.is_equal))
                then(nc.vector.scalar_tensor_tensor(order[:], equal[:], TOP, indices, ALU.mult, ALU.add))
                then(nc.vector.tensor_reduce(at, order[:], AX, ALU.min))
                then(nc.vector.tensor_tensor(chosen[:], order[:], across(at), ALU.is_equal))

            pick(score, max1, at1, first)
            then(nc.vector.scalar_tensor_tensor(rest[:], first[:], -4.0, score[:], ALU.mult, ALU.add))
            pick(rest, max2, at2, second)
            then(nc.vector.scalar_tensor_tensor(den, max1, 1e-20, max2, ALU.add, ALU.add))
            then(nc.vector.reciprocal(inv_den, den))
            then(nc.vector.tensor_scalar(inv_den, inv_den, ROUTE_SCALE, None, ALU.mult))
            then(nc.vector.tensor_tensor(w, max1, inv_den, ALU.mult))
            then(nc.vector.tensor_tensor(first[:], first[:], across(w), ALU.mult))
            then(nc.vector.tensor_tensor(w, max2, inv_den, ALU.mult))
            then(nc.vector.tensor_tensor(second[:], second[:], across(w), ALU.mult))
            then(nc.vector.tensor_tensor(first[:], first[:], second[:], ALU.add))
            then(nc.vector.tensor_copy(combine[:, :, 0:EXPERTS], first[:]))
            then(nc.vector.tensor_tensor(combine[:, :, EXPERTS:2 * EXPERTS], first[:],
                                         combine[:, :, 0:EXPERTS].bitcast(F32), ALU.subtract))


def experts(nc, X, ident, combine, w_gate, w_up, w_down, sw_gate, sw_up, sw_down, out):
    F = w_gate.shape[2]
    FS = sw_gate.shape[1]
    FE = EXPERTS * F
    FA = FE + FS
    NB = -(-FA // P)
    NE = FE // P
    RING = 7
    assert FE % P == 0 and NB % 2 == 0 and NB % RING == 0
    rows_of = [min(P, FA - n * P) for n in range(NB)]
    with ExitStack() as stack:
        room = Room(nc, stack, "e")
        w_rows = room.sbuf("w_rows", [P, 2, FA])
        gate_part = [room.sbuf(f"gate_{n}", [P, FA], F32R) for n in ("hi", "lo")]
        up_part = [room.sbuf(f"up_{n}", [P, FA], F32R) for n in ("hi", "lo")]
        down = room.sbuf("down", [P, NB, D])
        spread = room.sbuf("spread", [P, FE], F32R)
        x_rows = room.sbuf("x_rows", [P, 2, TOKENS])
        xT_part = [room.sbuf(f"xT_{n}", [P, 2, TOKENS], F32R) for n in ("hi", "lo")]
        c_rows = room.sbuf("c_rows", [P, 2, GROUP, 2 * EXPERTS])
        cT = room.sbuf("cT", [P, 2, TOKENS], F32R)
        silu = room.sbuf("silu", [P, 2, TOKENS])
        act_up = room.sbuf("act_up", [P, 2, TOKENS])
        hidden = room.sbuf("hidden", [P, RING, TOKENS])
        yT = room.sbuf("yT", [P, TOKENS])
        hsum = room.sbuf("hsum", [P, GROUP, D])
        stat = room.sbuf("stat", [P, GROUP, 6])
        mom = room.sbuf("mom", [P, GROUP, 2])
        vare = room.sbuf("vare", [P, GROUP])
        rstd = room.sbuf("rstd", [P, GROUP])
        half = room.sbuf("half", [P, GROUP])
        result = room.sbuf("result", [P, 2, GROUP, D])
        ps_gate = room.psum("ps_gate", [P, 2, 512])
        ps_up = room.psum("ps_up", [P, 2, 512])
        ps_c = room.psum("ps_c", [P, 2, 512])
        ps_y = room.psum("ps_y", [P, 512])
        ps_m = room.psum("ps_m", [P, 512])

        w_loaded, down_loaded = room.sem("w_loaded"), room.sem("down_loaded")
        ones_ready, spread_ready = room.sem("ones_ready"), room.sem("spread_ready")
        zero_ready, w_hi_ready, w_lo_ready = room.sem("zero_ready"), room.sem("w_hi_ready"), room.sem("w_lo_ready")
        half_ready = room.sem("half_ready")
        x_ready, x_psum, hi_ready, lo_ready = (room.sem(n) for n in ("x_ready", "x_psum", "hi_ready", "lo_ready"))
        c_ready, c_psum, cT_ready = room.sem("c_ready"), room.sem("c_psum"), room.sem("cT_ready")
        gate_psum, up_psum, spread_psum = room.sem("gate_psum"), room.sem("up_psum"), room.sem("spread_psum")
        silu_ready, act_ready, hidden_ready = room.sem("silu_ready"), room.sem("act_ready"), room.sem("hidden_ready")
        scaled_ready = room.sem("scaled_ready")
        y_psum, yT_ready, back_psum = room.sem("y_psum"), room.sem("yT_ready"), room.sem("back_psum")
        sum_ready, stat_ready, mom_ready = room.sem("sum_ready"), room.sem("stat_ready"), room.sem("mom_ready")
        vare_ready, rstd_ready, result_ready = room.sem("vare_ready"), room.sem("rstd_ready"), room.sem("result_ready")
        stored = [room.sem(f"stored{n}") for n in range(2)]
        block = stack.enter_context(nc.Block())

        def run(engine, step):
            pipelined(engine, step, GROUPS, 2, 2)

        def here(s):
            return there(s, GROUPS)

        @block.sync
        def _(sp):
            for n, (w, sw) in enumerate(((w_gate, sw_gate), (w_up, sw_up))):
                sp.dma_start(w_rows[:, n, 0:FE].rearrange("p (e f) -> p e f", f=F), w.rearrange("e d f -> d e f")
                             ).then_inc(w_loaded, 16)
                sp.dma_start(w_rows[:, n, FE:FA], sw).then_inc(w_loaded, 16)
            sp.dma_start(down[:, 0:NE, :], w_down.rearrange("e f d -> (e f) d").rearrange("(n p) d -> p n d", p=P)
                         ).then_inc(down_loaded, 16)
            full = FS // P
            sp.dma_start(down[:, NE:NE + full, :], sw_down[0:full * P].rearrange("(n p) d -> p n d", p=P)
                         ).then_inc(down_loaded, 16)
            sp.dma_start(down[0:FS - full * P, NE + full, :], sw_down[full * P:FS]).then_inc(down_loaded, 16)

            def step(t, par):
                s2 = t - 2
                if here(s2):
                    sp.wait_ge(result_ready, (s2 + 1) * GROUP)
                    sp.dma_start(out[bass.ds(s2 * GROUP, GROUP)].rearrange("b s d -> s b d"), result[:, par]
                                 ).then_inc(stored[par], 16)

            run(sp, step)
            for par in range(2):
                sp.wait_ge(stored[par], GROUPS // 2 * 16)

        @block.gpsimd
        def _(pool):
            nc.gpsimd.memset(half[:], -0.5).then_inc(half_ready, 1)
            built = hidden[:].rearrange("p r t -> p (r t)")[:, 0:FE]
            nc.gpsimd.memset(built, 0.0).then_inc(ones_ready, 1)
            for k in range(2):
                pool.wait_ge(ones_ready, k + 1)
                view = built.rearrange("p (e f) -> p e f", f=F)
                nc.gpsimd.affine_select(out=view, in_=view, compare_op=ALU.not_equal, fill=1.0, base=-k * EXPERTS,
                                        pattern=[[-1, EXPERTS], [0, F]], channel_multiplier=1).then_inc(ones_ready, 1)
            pool.wait_ge(ones_ready, 3)
            nc.gpsimd.tensor_copy(spread[:], built).then_inc(spread_ready, 1)
            nc.gpsimd.memset(cT[:].bitcast(F32), 0.0).then_inc(zero_ready, 1)
            pool.wait_ge(half_ready, 1)

            def step(t, par):
                s2 = t - 2
                if here(s2):
                    wait_apart(pool, half_ready, (mom_ready, (s2 + 1) * GROUP))
                    nc.gpsimd.tensor_scalar(vare[:], mom[:, :, 1], EPS, None, ALU.add).then_inc(vare_ready, 1)
                    pool.wait_ge(vare_ready, s2 + 1)
                    nc.gpsimd.tensor_tensor(rstd[:], vare[:], half[:], ALU.pow).then_inc(rstd_ready, 1)
                    wait_apart(pool, half_ready, (rstd_ready, s2 + 1), (stored[par], landed(s2, par) - 16))
                    for n in range(GROUP):
                        nc.gpsimd.tensor_scalar(result[:, par, n, :], hsum[:, n, :], mom[:, n, 0:1], rstd[:, n:n + 1],
                                                ALU.subtract, ALU.mult).then_inc(result_ready, 1)

            run(pool, step)

        @block.scalar
        def _(act):
            act.wait_ge(w_loaded, 64)
            for n, part in enumerate((gate_part, up_part)):
                nc.scalar.copy(part[0][:], w_rows[:, n, :]).then_inc(w_hi_ready, 1)
            act.wait_ge(zero_ready, 1)

            def step(t, par):
                s1, s2 = t - 1, t - 2
                for n in range(NB):
                    if here(s1):
                        act.wait_ge(gate_psum, s1 * NB + n + 1)
                        wait(act, act_ready, s1 * NB + n - 1)
                        nc.scalar.activation(silu[0:rows_of[n], n % 2, :], ps_gate[0:rows_of[n], n % 2, :], ACT.Silu
                                             ).then_inc(silu_ready, 1)
                    if n == 1 and here(s2):
                        act.wait_ge(y_psum, s2 + 1)
                        nc.scalar.copy(yT[:], ps_y[:]).then_inc(yT_ready, 1)
                    if n == 5 and here(t):
                        act.wait_ge(x_psum, t + 1)
                        nc.scalar.copy(xT_part[0][:, par, :], ps_m[:]).then_inc(hi_ready, 1)
                    if n == 7 and here(t):
                        act.wait_ge(c_psum, t + 1)
                        nc.scalar.copy(cT[0:2 * EXPERTS, par, :], ps_m[0:2 * EXPERTS, :]).then_inc(cT_ready, 1)

            run(act, step)

        @block.vector
        def _(dve):
            for n, part in enumerate((gate_part, up_part)):
                dve.wait_ge(w_hi_ready, n + 1)
                nc.vector.tensor_tensor(part[1][:], w_rows[:, n, :], part[0][:].bitcast(F32), ALU.subtract
                                        ).then_inc(w_lo_ready, 1)
            dve.wait_ge(spread_ready, 1)

            def step(t, par):
                s1, s2 = t - 1, t - 2
                for n in range(NB):
                    if here(s1):
                        rows = rows_of[n]
                        dve.wait_ge(silu_ready, s1 * NB + n + 1)
                        dve.wait_ge(up_psum, s1 * NB + n + 1)
                        first = act_up if n < NE else hidden
                        at = n % 2 if n < NE else n % RING
                        nc.vector.tensor_tensor(first[0:rows, at, :], silu[0:rows, n % 2, :], ps_up[0:rows, n % 2, :],
                                                ALU.mult).then_inc(act_ready, 1)
                        if n < NE:
                            dve.wait_ge(act_ready, s1 * NB + n + 1)
                            dve.wait_ge(spread_psum, s1 * NE + n + 1)
                            nc.vector.tensor_tensor(hidden[:, n % RING, :], act_up[:, n % 2, :],
                                                    ps_c[:, n % 2, :], ALU.mult).then_inc(scaled_ready, 1)
                    if n == 3 and here(s2):
                        dve.wait_ge(back_psum, s2 + 1)
                        wait(dve, result_ready, s2 * GROUP)
                        nc.vector.tensor_tensor(hsum[:].rearrange("p n d -> p (n d)"), ps_m[:], x_rows[:, par, :], ALU.add
                                                ).then_inc(sum_ready, 1)
                        dve.wait_ge(sum_ready, s2 + 1)
                        for k in range(GROUP):
                            nc.vector.bn_stats(stat[:, k, :], hsum[:, k, :]).then_inc(stat_ready, 1)
                        for k in range(GROUP):
                            wait_apart(dve, w_hi_ready, (stat_ready, s2 * GROUP + k + 1))
                            nc.vector.bn_aggr(mom[:, k, :], stat[:, k, :]).then_inc(mom_ready, 1)
                    if n == 4 and here(t):
                        nc.vector.tensor_copy(x_rows[:, par, :], X[:, bass.ds(t * TOKENS, TOKENS)]).then_inc(x_ready, 1)
                        wait(dve, c_psum, t - 1)
                        nc.vector.tensor_copy(c_rows[:, par].rearrange("p b e -> p (b e)"),
                                              combine[:].bitcast(F32).rearrange("p b e -> p (b e)")[
                                                  :, bass.ds(t * GROUP * 2 * EXPERTS, GROUP * 2 * EXPERTS)]
                                              ).then_inc(c_ready, 1)
                    if n == 6 and here(t):
                        dve.wait_ge(hi_ready, t + 1)
                        nc.vector.tensor_tensor(xT_part[1][:, par, :], ps_m[:], xT_part[0][:, par, :].bitcast(F32),
                                                ALU.subtract).then_inc(lo_ready, 1)

            run(dve, step)

        @block.tensor
        def _(pe):
            pe.wait_ge(w_lo_ready, 2)
            pe.wait_ge(spread_ready, 1)
            pe.wait_ge(down_loaded, 48)

            def project_down(s, n):
                if n < NE:
                    pe.wait_ge(scaled_ready, s * NE + n + 1)
                else:
                    pe.wait_ge(act_ready, s * NB + n + 1)
                last = nc.tensor.matmul(ps_y[:], down[0:rows_of[n], n, :], hidden[0:rows_of[n], n % RING, :],
                                        start=(n == 0), stop=(n == NB - 1))
                if n == NB - 1:
                    last.then_inc(y_psum, 1)

            def step(t, par):
                s1, s2 = t - 1, t - 2
                if here(s1):
                    pe.wait_ge(lo_ready, s1 + 1)
                    pe.wait_ge(cT_ready, s1 + 1)
                for n in range(NB):
                    if here(s1):
                        rows = rows_of[n]
                        xT = [x[:, 1 - par, :] for x in xT_part]
                        wait(pe, silu_ready, s1 * NB + n - 1)
                        split_product(nc, ps_gate[0:rows, n % 2, :], [g[:, n * P:n * P + rows] for g in gate_part], xT
                                      ).then_inc(gate_psum, 1)
                        wait(pe, act_ready, s1 * NB + n - 1)
                        split_product(nc, ps_up[0:rows, n % 2, :], [u[:, n * P:n * P + rows] for u in up_part], xT
                                      ).then_inc(up_psum, 1)
                        if n < NE:
                            wait(pe, scaled_ready, s1 * NE + n - 1 if n else s1 * NE)
                            nc.tensor.matmul(ps_c[:, n % 2, :], spread[:, n * P:(n + 1) * P], cT[:, 1 - par, :],
                                             start=True, stop=True).then_inc(spread_psum, 1)
                    if n < 2 and here(s2):
                        project_down(s2, NB - 2 + n)
                    if n == 2 and here(s1):
                        wait(pe, yT_ready, s1)
                    if n >= 2 and here(s1):
                        project_down(s1, n - 2)
                    if n == 2 and here(s2):
                        pe.wait_ge(yT_ready, s2 + 1)
                        wait(pe, cT_ready, s2 + 2 if not isinstance(s2, int) else min(s2 + 2, GROUPS))
                        for k in range(GROUP):
                            last = nc.tensor.transpose(ps_m[:, k * D:(k + 1) * D], yT[:, k * S:(k + 1) * S], ident[:])
                        last.then_inc(back_psum, 1)
                    if n == 5 and here(t):
                        pe.wait_ge(x_ready, t + 1)
                        wait(pe, sum_ready, t - 1)
                        for k in range(GROUP):
                            last = nc.tensor.transpose(ps_m[:, k * S:(k + 1) * S], x_rows[:, par, k * S:(k + 1) * S],
                                                       ident[:])
                        last.then_inc(x_psum, 1)
                    if n == 7 and here(t):
                        pe.wait_ge(c_ready, t + 1)
                        pe.wait_ge(lo_ready, t + 1)
                        for k in range(GROUP):
                            last = nc.tensor.transpose(ps_m[0:2 * EXPERTS, k * S:(k + 1) * S], c_rows[:, par, k, :],
                                                       ident[:])
                        last.then_inc(c_psum, 1)

            run(pe, step)


def decoder(nc, x, ctx, Wq, bq, Wk, bk, Wv, bv, Wo, bo, m_g, m_b, l_g, l_b, xWq, xWkv, xWout,
            gate_w, w_gate, w_up, w_down, sw_gate, sw_up, sw_down, out):
    nkv = nc.dram_tensor("normalised_keys", (B, C + S, D), F32, kind="Internal").ap()
    with ExitStack() as stack:
        X = stack.enter_context(nc.sbuf_tensor("X", [P, B * D], F32))
        ident = stack.enter_context(nc.sbuf_tensor("ident", [P, P], F32))
        tri = stack.enter_context(nc.sbuf_tensor("tri", [P, P], F32))
        combine = stack.enter_context(nc.sbuf_tensor("combine", [P, B, 2 * EXPERTS], F32R))
        constants(nc, ident, tri)
        linear_attention(nc, X, nkv, ident, tri, x, ctx, (Wq, Wk, Wv, Wo), (bq, bk, bv, bo))
        cross_attention(nc, X, nkv, ident, (m_g, m_b, l_g, l_b), xWq, xWkv, xWout)
        router(nc, X, ident, gate_w, combine)
        experts(nc, X, ident, combine, w_gate, w_up, w_down, sw_gate, sw_up, sw_down, out)


INPUTS = ["x", "ctx_1024", "L0_attn_Wq", "L0_attn_bq", "L0_attn_Wk", "L0_attn_bk", "L0_attn_Wv", "L0_attn_bv",
          "L0_attn_Wo", "L0_attn_bo", "L0_xattn_ln_m_g", "L0_xattn_ln_m_b", "L0_xattn_ln_l_g", "L0_xattn_ln_l_b",
          "L0_xattn_Wq", "L0_xattn_Wkv", "L0_xattn_Wout", "L0_ffn_gate_w", "L0_ffn_w_gate", "L0_ffn_w_up",
          "L0_ffn_w_down", "L0_ffn_sw_gate", "L0_ffn_sw_up", "L0_ffn_sw_down"]


def kernel(**inputs):
    import numpy as np
    import concourse.bacc as bacc
    from concourse.bass_utils import run_bass_kernel_spmd

    nc = bacc.Bacc("TRN2", target_bir_lowering=False, num_devices=1)
    arrays, args = {}, []
    for name in INPUTS:
        a = np.ascontiguousarray(inputs[name])
        arrays[f"in_{name}"] = a
        args.append(nc.dram_tensor(f"in_{name}", a.shape, mybir.dt.from_np(a.dtype), kind="ExternalInput").ap())
    args.append(nc.dram_tensor("out_dram", (B, S, D), F32, kind="ExternalOutput").ap())
    decoder(nc, *args)
    result = run_bass_kernel_spmd(nc, [arrays], core_ids=[0])
    return result.results[0]["out_dram"]
```

```python
from contextlib import ExitStack

import concourse.bass as bass
from concourse import mybir

F32 = mybir.dt.float32
F32R = mybir.dt.float32r
ALU = mybir.AluOpType
ACT = mybir.ActivationFunctionType
AX = mybir.AxisListType.X

P = 128
B = 64
S = 128
D = 128
C = 120
H = 16
EPS = 1e-5


def wait(engine, semaphore, count):
    if not isinstance(count, int) or count > 0:
        engine.wait_ge(semaphore, count)


def wait_apart(engine, opened, *waits):
    waits = [(semaphore, count if isinstance(count, int) else engine.to_reg(count)) for semaphore, count in waits]
    engine.wait_ge(opened, 1)
    for semaphore, count in waits:
        wait(engine, semaphore, count)


def pipelined(engine, step, count=B, head=4, tail=4):
    for t in range(head):
        step(t, t % 2)
    with engine.Fori(head // 2, count // 2) as i:
        for parity in range(2):
            step(i * 2 + parity, parity)
    for t in range(count, count + tail):
        step(t, t % 2)


def there(s, count=B):
    return not isinstance(s, int) or 0 <= s < count


def landed(s, parity):
    return (s - parity) * 8 + 16


class Room:

    def __init__(self, nc, stack, tag):
        self.nc, self.stack, self.tag = nc, stack, tag

    def sbuf(self, name, shape, dtype=F32):
        return self.stack.enter_context(self.nc.sbuf_tensor(f"{self.tag}_{name}", shape, dtype))

    def psum(self, name, shape):
        return self.stack.enter_context(self.nc.psum_tensor(f"{self.tag}_{name}", shape, F32))

    def sem(self, name):
        return self.stack.enter_context(self.nc.semaphore(f"{self.tag}_{name}"))


def constants(nc, ident, tri):
    with ExitStack() as stack:
        room = Room(nc, stack, "const")
        filled = room.sem("filled")
        shaped = room.sem("shaped")
        block = stack.enter_context(nc.Block())

        @block.gpsimd
        def _(pool):
            nc.gpsimd.memset(ident[:], 0.0).then_inc(filled, 1)
            nc.gpsimd.memset(tri[:], 1.0).then_inc(filled, 1)
            pool.wait_ge(filled, 2)
            nc.gpsimd.affine_select(out=ident[:], in_=ident[:], compare_op=ALU.not_equal, fill=1.0, base=0,
                                    pattern=[[-1, P]], channel_multiplier=1).then_inc(shaped, 1)
            nc.gpsimd.affine_select(out=tri[:], in_=tri[:], compare_op=ALU.is_ge, fill=0.0, base=0,
                                    pattern=[[1, P]], channel_multiplier=-1).then_inc(shaped, 1)
            pool.wait_ge(shaped, 2)


def linear_attention(nc, X, nkv, ident, tri, x, ctx, weights, biases):
    E = D // H
    NE = E + 1
    QK = 2 * D
    PAIRS = B // 2
    with ExitStack() as stack:
        room = Room(nc, stack, "lin")
        w_rows = room.sbuf("w_rows", [P, 4, D])
        w = room.sbuf("w", [P, 4 * D])
        b_qkv = room.sbuf("b_qkv", [P, 3 * D])
        b_o = room.sbuf("b_o", [P, D])
        x_rows = room.sbuf("x_rows", [P, 2, 2, D])
        c_rows = room.sbuf("c_rows", [C, 2, 2, D])
        turned = room.sbuf("turned", [P, 4, S])
        z = room.sbuf("z", [P, 2, 2, QK])
        v = room.sbuf("v", [P, 2, 2, D])
        mag = room.sbuf("mag", [P, 2, QK])
        dec = room.sbuf("dec", [P, 2, QK])
        log = room.sbuf("log", [P, 2, QK])
        qk = room.sbuf("qk", [P, 2, 2, QK])
        kv = room.sbuf("kv", [P, 2, E, H, E])
        prod = room.sbuf("prod", [P, 2, NE, H, E])
        numden = room.sbuf("numden", [P, 2, NE, H])
        inv = room.sbuf("inv", [P, 2, H])
        att = room.sbuf("att", [P, 2, H, E])
        res = room.sbuf("res", [P, 2, 2, D])
        stat = room.sbuf("stat", [P, 4, 6])
        mom = room.sbuf("mom", [P, 2, 4, 2])
        square = room.sbuf("square", [P, 2, 6])
        scale = room.sbuf("scale", [P, 2, 6])
        shift = room.sbuf("shift", [P, 2, 6])
        half = room.sbuf("half", [P, 6])
        nlat = room.sbuf("nlat", [P, 2, 2, D])
        nctx = room.sbuf("nctx", [C, 2, 2, D])
        ps_t = room.psum("ps_t", [P, 512])
        ps_qk = room.psum("ps_qk", [P, 512])
        ps_vy = room.psum("ps_vy", [P, 512])
        ps_cum = room.psum("ps_cum", [P, 2, 1024])
        ps_den = room.psum("ps_den", [P, 512])

        w_loaded, bqkv_loaded, bo_loaded = room.sem("w_loaded"), room.sem("bqkv_loaded"), room.sem("bo_loaded")
        res_loaded = [room.sem(f"res_loaded{n}") for n in range(4)]
        x_loaded = [room.sem(f"x_loaded{n}") for n in range(2)]
        c_loaded = [room.sem(f"c_loaded{n}") for n in range(2)]
        lat_stored = [room.sem(f"lat_stored{n}") for n in range(2)]
        ctx_stored = [room.sem(f"ctx_stored{n}") for n in range(2)]
        wT_psum, wT_ready = room.sem("wT_psum"), room.sem("wT_ready")
        half_ready, mom_ready = room.sem("half_ready"), room.sem("mom_ready")
        t_psum, turned_ready = room.sem("t_psum"), room.sem("turned_ready")
        qk_psum, vy_psum = room.sem("qk_psum"), room.sem("vy_psum")
        z_ready, v_ready = room.sem("z_ready"), room.sem("v_ready")
        mag_ready, dec_ready, log_ready = room.sem("mag_ready"), room.sem("dec_ready"), room.sem("log_ready")
        qk_ready, kv_ready = room.sem("qk_ready"), room.sem("kv_ready")
        den_psum, cum_psum = room.sem("den_psum"), room.sem("cum_psum")
        den_taken, cum_taken = room.sem("den_taken"), room.sem("cum_taken")
        numden_ready, inv_ready, att_ready = room.sem("numden_ready"), room.sem("inv_ready"), room.sem("att_ready")
        bias_added, sum_ready = room.sem("bias_added"), room.sem("sum_ready")
        stat_ready = room.sem("stat_ready")
        cstat_ready = room.sem("cstat_ready")
        square_ready, scale_ready, shift_ready = (room.sem(n) for n in ("square_ready", "scale_ready", "shift_ready"))
        x1_ready, nlat_ready, nctx_ready = room.sem("x1_ready"), room.sem("nlat_ready"), room.sem("nctx_ready")
        ymom_ready, cmom_ready = room.sem("ymom_ready"), room.sem("cmom_ready")
        block = stack.enter_context(nc.Block())
        QUART = B // 4
        STEPS = PAIRS + 3

        def here(s):
            return there(s, PAIRS)

        def rows_of(dram, s, rows):
            return dram[bass.ds(s * 2, 2), rows, :].rearrange("b s d -> s b d")

        @block.sync
        def _(sp):
            for n, weight in enumerate(weights):
                sp.dma_start(w_rows[:, n, :], weight).then_inc(w_loaded, 16)

            def step(t, par):
                s2, s5 = t - 2, t - 5
                if here(s2):
                    sp.wait_ge(nctx_ready, s2 * 2 + 2)
                    sp.dma_start(rows_of(nkv, s2, slice(0, C)), nctx[:, par]).then_inc(ctx_stored[par], 16)
                if here(s5):
                    sp.wait_ge(nlat_ready, s5 * 2 + 2)
                    sp.dma_start(rows_of(nkv, s5, slice(C, C + S)), nlat[:, 1 - par]).then_inc(lat_stored[1 - par], 16)
                if here(t):
                    wait(sp, t_psum, t - 1)
                    sp.dma_start(x_rows[:, par], rows_of(x, t, slice(0, S))).then_inc(x_loaded[par], 16)
                    wait(sp, nctx_ready, t * 2 - 2)
                    sp.dma_start(c_rows[:, par], rows_of(ctx, t, slice(0, C))).then_inc(c_loaded[par], 16)

            pipelined(sp, step, PAIRS, 6, 6)
            for par in range(2):
                sp.wait_ge(lat_stored[par], 16 * PAIRS // 2)
                sp.wait_ge(ctx_stored[par], 16 * PAIRS // 2)

        @block.gpsimd
        def _(pool):
            nc.gpsimd.memset(half[:], -0.5).then_inc(half_ready, 1)
            nc.gpsimd.memset(mom[:], 1.0).then_inc(half_ready, 1)
            pool.wait_ge(half_ready, 2)
            pool.wait_ge(bo_loaded, 16)
            for n in range(4):
                pool.wait_ge(res_loaded[n], 16)

            def step(t, par):
                s1 = t - 1
                if there(s1, STEPS):
                    pool.wait_ge(square_ready, s1 * 2 + 2)
                    wait(pool, shift_ready, s1 * 2 - 2)
                    wait(pool, x1_ready, (s1 - 4) * 2)
                    nc.gpsimd.tensor_tensor(scale[:, 1 - par, :], square[:, 1 - par, :], half[:], ALU.pow
                                            ).then_inc(scale_ready, 1)
                if here(s1):
                    pair = X[:, bass.ds(s1 * 2 * D, 2 * D)]
                    nc.gpsimd.tensor_tensor(pair.rearrange("p (b d) -> p b d", b=2), pair.rearrange("p (b d) -> p b d", b=2),
                                            b_o[:].unsqueeze(1).broadcast_to([P, 2, D]), ALU.add).then_inc(bias_added, 1)
                    pool.wait_ge(v_ready, s1 + 1)
                    pool.wait_ge(qk_ready, s1 + 1)
                    for u in range(2):
                        wait(pool, cum_psum, s1 * 2 - 1 + u)
                        k_u = qk[:, 1 - par, u, D:QK].rearrange("p (h d) -> p h d", h=H)
                        v_u = v[:, 1 - par, u].rearrange("p (h e) -> p e h", h=H)
                        nc.gpsimd.tensor_tensor(kv[:, u], k_u.unsqueeze(1).broadcast_to([P, E, H, E]),
                                                v_u.unsqueeze(3).broadcast_to([P, E, H, E]), ALU.mult
                                                ).then_inc(kv_ready, 1)

            pipelined(pool, step, PAIRS, 6, 4)

        @block.scalar
        def _(act):
            for n in range(3):
                act.dma_start(b_qkv[:, n * D:(n + 1) * D],
                              biases[n].rearrange("(o d) -> o d", o=1).broadcast_to([P, D])).then_inc(bqkv_loaded, 16)
            act.dma_start(b_o[:], biases[3].rearrange("(o d) -> o d", o=1).broadcast_to([P, D])).then_inc(bo_loaded, 16)
            for n in range(4):
                act.dma_start(X[:, n * QUART * D:(n + 1) * QUART * D].rearrange("s (b d) -> s b d", d=D),
                              x[n * QUART:(n + 1) * QUART].rearrange("b s d -> s b d")).then_inc(res_loaded[n], 16)
            act.wait_ge(wT_psum, 1)
            nc.scalar.copy(w[:], ps_t[:]).then_inc(wT_ready, 1)

            def step(t, par):
                s1, s3, s4 = t - 1, t - 3, t - 4
                if there(t, STEPS):
                    first, last = (0 if here(t) else 2), (4 if here(s3) else 2)
                    act.wait_ge(t_psum, t + 1)
                    nc.scalar.copy(turned[:, first:last, :], ps_t[:, first * S:last * S]).then_inc(turned_ready, 1)
                if there(s1, STEPS):
                    act.wait_ge(shift_ready, s1 * 2 + 2)

                def normalise(out, rows, column, ready):
                    height = C if column in (2, 3) else P
                    nc.scalar.activation(out, rows, ACT.Identity, bias=shift[0:height, 1 - par, column:column + 1],
                                         scale=scale[0:height, 1 - par, column:column + 1]).then_inc(ready, 1)

                if here(s1):
                    wait(act, ctx_stored[1 - par], landed(s1, 1 - par) - 16)
                    for u in range(2):
                        normalise(nctx[:, 1 - par, u, :], c_rows[:, 1 - par, u, :], 2 + u, nctx_ready)
                if here(s4):
                    wait(act, lat_stored[par], landed(s4, par) - 16)
                    for u in range(2):
                        normalise(nlat[:, par, u, :], res[:, par, u, :], 4 + u, nlat_ready)
                    for u in range(2):
                        normalise(X[:, bass.ds((s4 * 2 + u) * D, D)], res[:, par, u, :], u, x1_ready)
                if here(t):
                    act.wait_ge(z_ready, t + 1)
                    wait(act, dec_ready, t)
                    nc.scalar.activation(mag[:], z[:, par], ACT.Abs).then_inc(mag_ready, 1)
                    act.wait_ge(mag_ready, t + 1)
                    wait(act, log_ready, t)
                    nc.scalar.activation(dec[:], mag[:], ACT.Exp, scale=-1.0).then_inc(dec_ready, 1)
                    act.wait_ge(dec_ready, t + 1)
                    wait(act, qk_ready, t)
                    nc.scalar.activation(log[:], dec[:], ACT.Ln, bias=1.0).then_inc(log_ready, 1)

            pipelined(act, step, PAIRS, 4, 4)

        @block.vector
        def _(dve):
            dve.wait_ge(bqkv_loaded, 48)
            dve.wait_ge(half_ready, 2)

            def stats(rows, source, first, ready):
                for u in range(2):
                    nc.vector.bn_stats(stat[0:rows, first + u, :], source(u)).then_inc(ready, 1)

            def moments(rows, par, first, ready, s, done):
                for u in range(2):
                    wait_apart(dve, half_ready, (ready, s * 2 + u + 1))
                    nc.vector.bn_aggr(mom[0:rows, par, first + u, :], stat[0:rows, first + u, :]).then_inc(done, 1)

            def step(t, par):
                s1, s2, s3 = t - 1, t - 2, t - 3
                if here(s2):
                    wait(dve, numden_ready, s2)
                    for u in range(2):
                        dve.wait_ge(cum_psum, s2 * 2 + u + 1)
                        q_u = qk[:, par, u, 0:D].rearrange("p (o f) -> p o f", o=1).broadcast_to([P, E, D])
                        nc.vector.tensor_tensor(prod[:, u, 0:E].rearrange("p e h d -> p e (h d)"),
                                                ps_cum[:, u, :].rearrange("p (e f) -> p e f", e=E), q_u, ALU.mult
                                                ).then_inc(cum_taken, 1)
                    nc.vector.tensor_tensor(prod[:, :, E].rearrange("p u h d -> p u (h d)"),
                                            ps_den[:, 0:2 * D].rearrange("p (u f) -> p u f", u=2), qk[:, par, :, 0:D],
                                            ALU.mult).then_inc(den_taken, 1)
                if there(s1, STEPS):
                    dve.wait_ge(scale_ready, s1 + 1)
                    wait(dve, x1_ready, (s1 - 4) * 2)
                    for columns, rows in ((slice(0, 4), slice(0, 4)), (slice(4, 6), slice(0, 2))):
                        nc.vector.scalar_tensor_tensor(shift[:, 1 - par, columns], mom[:, 1 - par, rows, 0], -1.0,
                                                       scale[:, 1 - par, columns], ALU.mult, ALU.mult
                                                       ).then_inc(shift_ready, 1)
                if here(s1):
                    dve.wait_ge(log_ready, s1 + 1)
                    wait(dve, den_psum, s1 - 1)
                    nc.vector.scalar_tensor_tensor(qk[:, 1 - par], z[:, 1 - par], 0.0, log[:], ALU.max, ALU.add
                                                   ).then_inc(qk_ready, 1)
                if here(t):
                    dve.wait_ge(qk_psum, t + 1)
                    nc.vector.tensor_tensor(z[:, par], ps_qk[:].rearrange("p (u f) -> p u f", u=2),
                                            b_qkv[:, 0:QK].unsqueeze(1).broadcast_to([P, 2, QK]), ALU.add
                                            ).then_inc(z_ready, 1)
                if here(s3):
                    dve.wait_ge(vy_psum, t + 1)
                    dve.wait_ge(bias_added, s3 + 1)
                    wait(dve, x1_ready, (s3 - 1) * 2)
                    nc.vector.tensor_tensor(res[:, 1 - par], ps_vy[:, 2 * D:4 * D].rearrange("p (u f) -> p u f", u=2),
                                            X[:, bass.ds(s3 * 2 * D, 2 * D)].rearrange("p (u f) -> p u f", u=2), ALU.add
                                            ).then_inc(sum_ready, 1)
                if here(t):
                    dve.wait_ge(vy_psum, t + 1)
                    wait(dve, kv_ready, t * 2 - 2)
                    nc.vector.tensor_tensor(v[:, par], ps_vy[:, 0:2 * D].rearrange("p (u f) -> p u f", u=2),
                                            b_qkv[:, QK:3 * D].unsqueeze(1).broadcast_to([P, 2, D]), ALU.add
                                            ).then_inc(v_ready, 1)
                if here(s3):
                    wait_apart(dve, half_ready, (sum_ready, s3 + 1), (ymom_ready, s3 * 2))
                    stats(P, lambda u: res[:, 1 - par, u, :], 0, stat_ready)
                if here(s2):
                    dve.wait_ge(den_taken, s2 + 1)
                    wait(dve, att_ready, s2)
                    nc.vector.tensor_reduce(numden[:], prod[:], AX, ALU.add).then_inc(numden_ready, 1)
                if here(s3):
                    moments(P, par, 0, stat_ready, s3, ymom_ready)
                if here(t):
                    wait_apart(dve, half_ready, (c_loaded[par], landed(t, par)), (cmom_ready, t * 2))
                    stats(C, lambda u: c_rows[:, par, u, :], 2, cstat_ready)
                if here(s2):
                    dve.wait_ge(numden_ready, s2 + 1)
                    nc.vector.reciprocal(inv[:], numden[:, :, E, :]).then_inc(inv_ready, 1)
                if here(t):
                    moments(C, par, 2, cstat_ready, t, cmom_ready)
                if here(s2):
                    dve.wait_ge(inv_ready, s2 + 1)
                    wait(dve, t_psum, t)
                    nc.vector.tensor_tensor(att[:].rearrange("p u h e -> p u e h"), numden[:, :, 0:E, :],
                                            inv[:].unsqueeze(2).broadcast_to([P, 2, E, H]), ALU.mult
                                            ).then_inc(att_ready, 1)
                if there(t, STEPS):
                    if here(s3):
                        dve.wait_ge(ymom_ready, s3 * 2 + 2)
                    if here(t):
                        dve.wait_ge(cmom_ready, t * 2 + 2)
                    nc.vector.tensor_scalar(square[:, par, 0:4], mom[:, par, :, 1], EPS, None, ALU.add
                                            ).then_inc(square_ready, 1)
                    nc.vector.tensor_scalar(square[:, par, 4:6], mom[:, par, 0:2, 1], 1.0 + EPS, EPS * EPS, ALU.mult,
                                            ALU.add).then_inc(square_ready, 1)

            pipelined(dve, step, PAIRS, 6, 4)

        @block.tensor
        def _(pe):
            pe.wait_ge(w_loaded, 64)
            for n in range(4):
                last = nc.tensor.transpose(ps_t[:, n * D:(n + 1) * D], w_rows[:, n, :], ident[:])
            last.then_inc(wT_psum, 1)
            pe.wait_ge(wT_ready, 1)

            def step(t, par):
                s1, s3 = t - 1, t - 3
                if there(t, STEPS):
                    wait(pe, turned_ready, t)
                if here(t):
                    pe.wait_ge(x_loaded[par], landed(t, par))
                    for u in range(2):
                        last = nc.tensor.transpose(ps_t[:, u * S:(u + 1) * S], x_rows[:, par, u, :], ident[:])
                if here(s3):
                    pe.wait_ge(att_ready, s3 + 1)
                    for u in range(2):
                        last = nc.tensor.transpose(ps_t[:, (2 + u) * S:(3 + u) * S],
                                                   att[:, u].rearrange("p h e -> p (h e)"), ident[:])
                if there(t, STEPS):
                    last.then_inc(t_psum, 1)
                    pe.wait_ge(turned_ready, t + 1)
                if here(t):
                    wait(pe, z_ready, t)
                    for u in range(2):
                        last = nc.tensor.matmul(ps_qk[:, u * QK:(u + 1) * QK], turned[:, u, :], w[:, 0:QK],
                                                start=True, stop=True)
                    last.then_inc(qk_psum, 1)
                    wait(pe, v_ready, t)
                if there(s3 - 1, PAIRS):
                    pe.wait_ge(sum_ready, s3)
                if here(t):
                    for u in range(2):
                        last = nc.tensor.matmul(ps_vy[:, u * D:(u + 1) * D], turned[:, u, :], w[:, QK:3 * D],
                                                start=True, stop=True)
                if here(s3):
                    for u in range(2):
                        last = nc.tensor.matmul(ps_vy[:, (2 + u) * D:(3 + u) * D], turned[:, 2 + u, :], w[:, 3 * D:4 * D],
                                                start=True, stop=True)
                if there(t, STEPS):
                    last.then_inc(vy_psum, 1)
                if here(s1):
                    pe.wait_ge(qk_ready, s1 + 1)
                    wait(pe, den_taken, s1)
                    nc.tensor.matmul(ps_den[:, 0:2 * D], tri[:], qk[:, 1 - par, :, D:QK], start=True, stop=True
                                     ).then_inc(den_psum, 1)
                    for u in range(2):
                        pe.wait_ge(kv_ready, s1 * 2 + u + 1)
                        wait(pe, cum_taken, s1 * 2 - 1 + u)
                        flat = kv[:, u].rearrange("p e h d -> p (e h d)")
                        for n in range(2):
                            last = nc.tensor.matmul(ps_cum[:, u, n * 512:(n + 1) * 512], tri[:],
                                                    flat[:, n * 512:(n + 1) * 512], start=True, stop=True)
                        last.then_inc(cum_psum, 1)

            pipelined(pe, step, PAIRS, 4, 4)


def split_product(nc, out, stationary, moving, last=True):
    nc.tensor.matmul(out, stationary[0], moving[1], start=True, stop=False)
    nc.tensor.matmul(out, stationary[1], moving[0], start=False, stop=False)
    return nc.tensor.matmul(out, stationary[0], moving[0], start=False, stop=True)


def cross_attention(nc, X, nkv, ident, gains, w_q, w_kv, w_out):
    DH = 64
    I = H * DH
    K = C + S
    KT = K // 2
    PAIRS = H // 2
    UNITS = 2 * PAIRS
    ROUNDS = B // 2
    with ExitStack() as stack:
        room = Room(nc, stack, "x")
        wq = room.sbuf("wq", [P, I])
        wkv = room.sbuf("wkv", [P, 2 * I])
        wqT = room.sbuf("wqT", [P, PAIRS, D])
        wkT = room.sbuf("wkT", [P, PAIRS, D])
        M_part = [room.sbuf(f"M_{n}", [P, H, D], F32R) for n in ("hi", "lo")]
        wv_part = [room.sbuf(f"wv_{n}", [P, I], F32R) for n in ("hi", "lo")]
        wo = room.sbuf("wo", [P, PAIRS, D])
        gain = room.sbuf("gain", [P, 4])
        nk = room.sbuf("nk", [KT, 2, 2, 2, D])
        kT_full = room.sbuf("kT_full", [P, 2, K])
        kT_part = [room.sbuf(f"kT_{n}", [P, 2, 2, K], F32R) for n in ("hi", "lo")]
        G_part = [room.sbuf(f"G_{n}", [P, 2, 2, 2, S], F32R) for n in ("hi", "lo")]
        V = room.sbuf("V", [KT, 2, 2, 2, I // 2])
        nmax = room.sbuf("nmax", [P, 2, 2])
        total = room.sbuf("total", [P, 2, 2])
        inv = room.sbuf("inv", [P, 2, 2])
        prob = room.sbuf("prob", [P, 2, 2, K])
        probT = room.sbuf("probT", [KT, 2, 2, 2, S])
        outT = room.sbuf("outT", [P, 2, 2, PAIRS // 2, S])
        hsum = room.sbuf("hsum", [P, 2, D])
        stat = room.sbuf("stat", [P, 2, 6])
        mom = room.sbuf("mom", [P, 2, 2])
        vare = room.sbuf("vare", [P, 2])
        rstd = room.sbuf("rstd", [P, 2])
        half = room.sbuf("half", [P, 1])
        xnew = room.sbuf("xnew", [P, 2, D])
        ps_S = room.psum("ps_S", [P, 2, 512])
        ps_T = room.psum("ps_T", [P, 2, 512])
        ps_O = room.psum("ps_O", [P, 2, 512])
        ps_G = room.psum("ps_G", [P, 512])
        ps_V = room.psum("ps_V", [P, 512])

        w_loaded, g_loaded = room.sem("w_loaded"), room.sem("g_loaded")
        nk_loaded = [room.sem(f"nk_loaded{n}") for n in range(2)]
        wT_psum, wT_ready = room.sem("wT_psum"), room.sem("wT_ready")
        M_psum, M_hi_ready, M_lo_ready = room.sem("M_psum"), room.sem("M_hi_ready"), room.sem("M_lo_ready")
        wv_hi_ready, wv_lo_ready = room.sem("wv_hi_ready"), room.sem("wv_lo_ready")
        kT_psum, kT_ready = room.sem("kT_psum"), room.sem("kT_ready")
        kT_hi_ready, kT_lo_ready = room.sem("kT_hi_ready"), room.sem("kT_lo_ready")
        G_psum, G_hi_ready, G_lo_ready = room.sem("G_psum"), room.sem("G_hi_ready"), room.sem("G_lo_ready")
        V_psum, V_ready = room.sem("V_psum"), room.sem("V_ready")
        S_psum, max_ready, exp_ready = room.sem("S_psum"), room.sem("max_ready"), room.sem("exp_ready")
        inv_ready, prob_ready = room.sem("inv_ready"), room.sem("prob_ready")
        T_psum, probT_ready, O_psum = room.sem("T_psum"), room.sem("probT_ready"), room.sem("O_psum")
        outT_ready, y_psum = room.sem("outT_ready"), room.sem("y_psum")
        sum_ready, stat_ready, mom_ready = room.sem("sum_ready"), room.sem("stat_ready"), room.sem("mom_ready")
        half_ready, vare_ready, rstd_ready = room.sem("half_ready"), room.sem("vare_ready"), room.sem("rstd_ready")
        xnew_ready, x2_ready = room.sem("xnew_ready"), room.sem("x2_ready")
        block = stack.enter_context(nc.Block())

        def rounds(engine, body):
            with engine.Fori(0, ROUNDS // 2) as i:
                for parity in range(2):
                    body(i * 2 + parity, parity)

        @block.sync
        def _(sp):
            sp.dma_start(wq[:], w_q).then_inc(w_loaded, 16)
            sp.dma_start(wkv[:], w_kv).then_inc(w_loaded, 16)
            sp.dma_start(wo[:], w_out.rearrange("(j p) d -> p j d", p=P)).then_inc(w_loaded, 16)
            for n, g in enumerate(gains):
                sp.dma_start(gain[:, n:n + 1], g.rearrange("(d o) -> d o", o=1)).then_inc(g_loaded, 16)

            def load(r, b, par):
                for u in range(2):
                    sp.dma_start(nk[:, par, u], nkv[bass.ds(b + u, 1)].rearrange("o (t k) d -> k (o t) d", t=2)
                                 ).then_inc(nk_loaded[par], 16)

            load(0, 0, 0)
            load(1, 2, 1)
            with sp.Fori(1, ROUNDS // 2) as i:
                for par in range(2):
                    sp.wait_ge(kT_psum, i * 2 + par - 1)
                    load(i * 2 + par, i * 4 + par * 2, par)
            sp.wait_ge(kT_psum, ROUNDS - 1)
            load(ROUNDS, 0, 0)

        @block.gpsimd
        def _(pool):
            nc.gpsimd.memset(half[:], -0.5).then_inc(half_ready, 1)
            pool.wait_ge(half_ready, 1)
            pool.sem_inc(x2_ready, 2)

            def split_keys(n, par):
                wait_apart(pool, half_ready, (kT_ready, n + 1))
                nc.gpsimd.tensor_copy(kT_part[0][:, par], kT_full[:]).then_inc(kT_hi_ready, 1)
                pool.wait_ge(kT_hi_ready, n + 1)
                nc.gpsimd.tensor_tensor(kT_part[1][:, par], kT_full[:], kT_part[0][:, par].bitcast(F32), ALU.subtract
                                        ).then_inc(kT_lo_ready, 1)

            def normalise(r, u):
                n = r * 2 + u
                wait_apart(pool, half_ready, (mom_ready, n + 1))
                nc.gpsimd.tensor_scalar(vare[:, u:u + 1], mom[:, u, 1:2], EPS, None, ALU.add).then_inc(vare_ready, 1)
                pool.wait_ge(vare_ready, n + 1)
                nc.gpsimd.tensor_tensor(rstd[:, u:u + 1], vare[:, u:u + 1], half[:], ALU.pow).then_inc(rstd_ready, 1)
                wait_apart(pool, half_ready, (rstd_ready, n + 1))
                nc.gpsimd.tensor_scalar(xnew[:, u, :], hsum[:, u, :], mom[:, u, 0:1], rstd[:, u:u + 1], ALU.subtract,
                                        ALU.mult).then_inc(xnew_ready, 1)
                wait_apart(pool, half_ready, (xnew_ready, n + 1))
                nc.gpsimd.tensor_copy(X[:, bass.ds(n * D, D)], xnew[:, u, :]).then_inc(x2_ready, 1)

            def body(r, par):
                split_keys(r + 1, 1 - par)
                normalise(r, 0)
                normalise(r, 1)

            split_keys(0, 0)
            rounds(pool, body)

        @block.scalar
        def _(act):
            for n in range(4):
                act.wait_ge(wT_psum, n + 1)
                dst = (wqT, wkT)[n // 2]
                nc.scalar.copy(dst[:, n % 2 * 4:n % 2 * 4 + 4, :], ps_S[:, n % 2, :]).then_inc(wT_ready, 1)
            for n in range(4):
                act.wait_ge(M_psum, n + 1)
                nc.scalar.mul(M_part[0][:, n // 2 * 8 + n % 2:n // 2 * 8 + n % 2 + 7:2, :], ps_T[:, n % 2, :],
                              DH ** -0.5).then_inc(M_hi_ready, 1)
            act.wait_ge(w_loaded, 48)
            nc.scalar.copy(wv_part[0][:], wkv[:, I:2 * I]).then_inc(wv_hi_ready, 1)

            def G_hi(n, pair):
                act.wait_ge(G_psum, n + 1)
                nc.scalar.copy(G_part[0][:, pair], ps_G[:]).then_inc(G_hi_ready, 1)

            def V_copy(n, hf, u, tile):
                act.wait_ge(V_psum, n + 1)
                nc.scalar.copy(V[:, hf, u, tile, :], ps_V[0:KT, :]).then_inc(V_ready, 1)

            def exponentials(n, k):
                act.wait_ge(max_ready, n + 1)
                for h in range(2):
                    last = nc.scalar.activation(prob[:, k, h, :], ps_S[:, k, h * K:(h + 1) * K], ACT.Exp,
                                                bias=nmax[:, k, h:h + 1], accum_out=total[:, k, h:h + 1])
                last.then_inc(exp_ready, 1)

            def out_copy(n, u, hf, av):
                act.wait_ge(O_psum, av)
                nc.scalar.copy(outT[:, u, hf], ps_O[:, u, :]).then_inc(outT_ready, 1)

            def body(r, par):
                unit = r * UNITS
                for s in range(UNITS):
                    if s in (UNITS // 2 - 1, UNITS // 2, UNITS - 1):
                        out_copy(None, (s - 1) % 2, (s - 1) // (UNITS // 2), unit + s)
                    act.wait_ge(T_psum, unit + s + 1)
                    nc.scalar.copy(probT[:, s % 2], ps_T[0:KT, s % 2, :]).then_inc(probT_ready, 1)
                    if s % 2 == 0:
                        G_hi(r * PAIRS + s // 2 + 2, s // 2 % 2)
                    elif s < UNITS - 1:
                        k = s // 2
                        V_copy(r * 8 + 4 + k, 1 - k // 4, k % 4 // 2, k % 2)
                    exponentials(unit + s + 2, s % 2)
                out_copy(None, 1, 1, unit + UNITS)
                V_copy(r * 8 + 4 + 7, 0, 1, 1)

            for k in range(4):
                V_copy(k, 0, k // 2, k % 2)
            for j in range(2):
                G_hi(j, j)
            for k in range(2):
                exponentials(k, k)
            rounds(act, body)

        @block.vector
        def _(dve):
            for n in range(4):
                dve.wait_ge(M_hi_ready, n + 1)
                heads = slice(n // 2 * 8 + n % 2, n // 2 * 8 + n % 2 + 7, 2)
                nc.vector.scalar_tensor_tensor(M_part[1][:, heads, :], ps_T[:, n % 2, :].rearrange("p (h d) -> p h d", h=4),
                                               DH ** -0.5, M_part[0][:, heads, :].bitcast(F32), ALU.mult, ALU.subtract
                                               ).then_inc(M_lo_ready, 1)
            dve.wait_ge(wv_hi_ready, 1)
            nc.vector.tensor_tensor(wv_part[1][:], wkv[:, I:2 * I], wv_part[0][:].bitcast(F32), ALU.subtract
                                    ).then_inc(wv_lo_ready, 1)
            dve.wait_ge(g_loaded, 64)

            def keys(n):
                dve.wait_ge(kT_psum, n + 1)
                wait(dve, kT_lo_ready, n)
                rows = ps_V[:, 0:2 * K].rearrange("p (u k) -> p u k", u=2)
                nc.vector.tensor_scalar(kT_full[:, :, 0:C], rows[:, :, 0:C], gain[:, 0:1], gain[:, 1:2], ALU.mult, ALU.add)
                nc.vector.tensor_scalar(kT_full[:, :, C:K], rows[:, :, C:K], gain[:, 2:3], gain[:, 3:4], ALU.mult, ALU.add
                                        ).then_inc(kT_ready, 1)

            def G_lo(n, pair):
                dve.wait_ge(G_hi_ready, n + 1)
                nc.vector.tensor_tensor(G_part[1][:, pair].rearrange("p h u q -> p (h u q)"), ps_G[:],
                                        G_part[0][:, pair].bitcast(F32).rearrange("p h u q -> p (h u q)"), ALU.subtract
                                        ).then_inc(G_lo_ready, 1)

            def maxima(n, k):
                dve.wait_ge(S_psum, n + 1)
                nc.vector.tensor_reduce(nmax[:, k, :], ps_S[:, k, 0:2 * K].rearrange("p (h k) -> p h k", h=2), AX,
                                        ALU.max, negate=True).then_inc(max_ready, 1)

            def normal(n, k):
                dve.wait_ge(exp_ready, n + 1)
                nc.vector.reciprocal(inv[:, k, :], total[:, k, :]).then_inc(inv_ready, 1)
                dve.wait_ge(inv_ready, n + 1)
                for h in range(2):
                    last = nc.vector.tensor_scalar(prob[:, k, h, :], prob[:, k, h, :], inv[:, k, h:h + 1], None, ALU.mult)
                last.then_inc(prob_ready, 1)

            def residual(r, u):
                n = r * 2 + u
                dve.wait_ge(y_psum, n + 1)
                dve.wait_ge(x2_ready, n + 1)
                nc.vector.tensor_tensor(hsum[:, u, :], ps_G[:, 0:D], X[:, bass.ds(n * D, D)], ALU.add).then_inc(sum_ready, 1)
                dve.wait_ge(sum_ready, n + 2)
                nc.vector.bn_stats(stat[:, u, :], hsum[:, u, :]).then_inc(stat_ready, 1)
                wait_apart(dve, wv_hi_ready, (stat_ready, n + 1))
                nc.vector.bn_aggr(mom[:, u, :], stat[:, u, :]).then_inc(mom_ready, 1)

            def body(r, par):
                unit = r * UNITS
                for s in range(UNITS):
                    normal(unit + s + 1, (s + 1) % 2)
                    maxima(unit + s + 2, s % 2)
                    if s % 2 == 0:
                        G_lo(r * PAIRS + s // 2 + 2, s // 2 % 2)
                    if s == 4:
                        keys(r + 1)
                residual(r, 0)
                residual(r, 1)

            keys(0)
            for j in range(2):
                G_lo(j, j)
            dve.wait_ge(G_lo_ready, 2)
            dve.sem_inc(sum_ready, 1)
            maxima(0, 0)
            normal(0, 0)
            maxima(1, 1)
            rounds(dve, body)

        @block.tensor
        def _(pe):
            pe.wait_ge(w_loaded, 48)
            for n in range(4):
                if n >= 2:
                    pe.wait_ge(wT_ready, n - 1)
                src = (wq, wkv)[n // 2]
                for j in range(4):
                    jj = n % 2 * 4 + j
                    last = nc.tensor.transpose(ps_S[:, n % 2, j * D:(j + 1) * D], src[:, jj * D:(jj + 1) * D], ident[:])
                last.then_inc(wT_psum, 1)
            pe.wait_ge(wT_ready, 4)
            for n in range(4):
                if n >= 2:
                    pe.wait_ge(M_lo_ready, n - 1)
                odd = n % 2 * DH
                for j in range(4):
                    jj = n // 2 * 4 + j
                    last = nc.tensor.matmul(ps_T[:, n % 2, j * D:(j + 1) * D], wqT[odd:odd + DH, jj, :],
                                            wkT[odd:odd + DH, jj, :], start=True, stop=True)
                last.then_inc(M_psum, 1)
            pe.wait_ge(M_lo_ready, 4)
            pe.wait_ge(wv_lo_ready, 1)

            def keys(n, par):
                pe.wait_ge(nk_loaded[par], (n - par) * 16 + 32)
                for u in range(2):
                    for tile in range(2):
                        at = u * K + tile * KT
                        last = nc.tensor.transpose(ps_V[:, at:at + KT], nk[:, par, u, tile, :], ident[0:KT, 0:KT])
                last.then_inc(kT_psum, 1)

            def make_G(pair, keys_par, j):
                for h in range(2):
                    last = split_product(nc, ps_G[:, h * 256:(h + 1) * 256], [m[:, 2 * j + h, :] for m in M_part],
                                         [k[:, keys_par, :, C:K] for k in kT_part])
                last.then_inc(G_psum, 1)

            def make_V(keys_par, hf, u, tile):
                split_product(nc, ps_V[0:KT, :], [k[:, keys_par, u, tile * KT:(tile + 1) * KT] for k in kT_part],
                              [w[:, hf * 512:(hf + 1) * 512] for w in wv_part]).then_inc(V_psum, 1)

            def scores(n, k, keys_par, pair):
                for h in range(2):
                    last = split_product(nc, ps_S[:, k, h * K:(h + 1) * K], [g[:, pair, h, k, :] for g in G_part],
                                         [t[:, keys_par, k, :] for t in kT_part])
                last.then_inc(S_psum, 1)

            def output(n, u):
                for j in range(PAIRS):
                    last = nc.tensor.matmul(ps_G[:, 0:D], outT[:, u, j // 4, j % 4, :], wo[:, j, :], start=(j == 0),
                                            stop=(j == PAIRS - 1))
                last.then_inc(y_psum, 1)

            def body(r, par):
                unit = r * UNITS
                for s in range(UNITS):
                    j, u = s // 2, s % 2
                    pe.wait_ge(prob_ready, unit + s + 1)
                    for h in range(2):
                        for tile in range(2):
                            at = (h * 2 + tile) * S
                            last = nc.tensor.transpose(ps_T[0:KT, u, at:at + S], prob[:, u, h, tile * KT:(tile + 1) * KT],
                                                       ident[:])
                    last.then_inc(T_psum, 1)
                    ahead = j + 1
                    if u == 0:
                        pe.wait_ge(G_lo_ready, r * PAIRS + ahead + 1)
                    scores(unit + s + 2, u, par if ahead < PAIRS else 1 - par, ahead % 2)
                    if u == 0:
                        if s == 0:
                            pe.wait_ge(sum_ready, r * 2 + 1)
                        if s == 12:
                            pe.wait_ge(kT_lo_ready, r + 2)
                        make_G(j % 2, par if j + 2 < PAIRS else 1 - par, (j + 2) % PAIRS)
                    elif s < UNITS - 1:
                        if s != 5:
                            pe.wait_ge(V_ready, r * 8 + 4 + j)
                        else:
                            pe.wait_ge(kT_ready, r + 2)
                        if s == 9:
                            pe.wait_ge(kT_lo_ready, r + 2)
                        make_V(par if j < 4 else 1 - par, 1 - j // 4, j % 4 // 2, j % 2)
                    else:
                        pe.wait_ge(outT_ready, r * 4 + 3)
                        pe.wait_ge(G_lo_ready, r * PAIRS + 10)
                        output(None, 0)
                    if s == 4:
                        pe.wait_ge(V_ready, r * 8 + 4 + 2)
                        keys(r + 1, 1 - par)
                    pe.wait_ge(probT_ready, unit + s + 1)
                    if s in (0, 8):
                        pe.wait_ge(V_ready, r * 8 + 4 + s // 2)
                    if s in (8, 9):
                        pe.wait_ge(outT_ready, r * 4 + s - 7)
                    for tile in range(2):
                        for h in range(2):
                            last = nc.tensor.matmul(ps_O[h * DH:(h + 1) * DH, u, j % 4 * S:(j % 4 + 1) * S],
                                                    V[:, j // 4, u, tile, (j % 4 * 2 + h) * DH:(j % 4 * 2 + h + 1) * DH],
                                                    probT[:, u, h, tile, :], start=(tile == 0), stop=(tile == 1))
                    last.then_inc(O_psum, 1)
                pe.wait_ge(V_ready, r * 8 + 4 + 7)
                make_V(1 - par, 0, 1, 1)
                pe.wait_ge(outT_ready, r * 4 + 4)
                pe.wait_ge(sum_ready, r * 2 + 2)
                output(None, 1)

            keys(0, 0)
            pe.wait_ge(kT_lo_ready, 1)
            for k in range(4):
                if k:
                    pe.wait_ge(V_ready, k)
                make_V(0, 0, k // 2, k % 2)
            for j in range(2):
                if j:
                    pe.wait_ge(G_lo_ready, j)
                make_G(j, 0, j)
            for k in range(2):
                if k == 0:
                    pe.wait_ge(G_lo_ready, 1)
                scores(k, k, 0, 0)
            rounds(pe, body)


EXPERTS = 8
GROUP = 4
TOKENS = GROUP * S
GROUPS = B // GROUP
ROUTE_SCALE = 2.5


def router(nc, X, ident, gate_w, combine):
    TOP = -16.0
    with ExitStack() as stack:
        room = Room(nc, stack, "r")
        gw_rows = room.sbuf("gw_rows", [EXPERTS, D])
        gw_part = [room.sbuf(f"gw_{n}", [P, EXPERTS], F32R) for n in ("hi", "lo")]
        x_rows = room.sbuf("x_rows", [P, 2, TOKENS])
        xT_part = [room.sbuf(f"xT_{n}", [P, 2, TOKENS], F32R) for n in ("hi", "lo")]
        logitT = room.sbuf("logitT", [EXPERTS, 2, TOKENS])
        logit = room.sbuf("logit", [P, B, EXPERTS])
        index = room.sbuf("index", [P, EXPERTS])
        shifted = room.sbuf("shifted", [P, B, EXPERTS])
        score = room.sbuf("score", [P, B, EXPERTS])
        rest = room.sbuf("rest", [P, B, EXPERTS])
        equal = room.sbuf("equal", [P, B, EXPERTS])
        order = room.sbuf("order", [P, B, EXPERTS])
        first = room.sbuf("first", [P, B, EXPERTS])
        second = room.sbuf("second", [P, B, EXPERTS])
        col = room.sbuf("col", [P, 10, B])
        ps_x = room.psum("ps_x", [P, 2, 512])
        ps_l = room.psum("ps_l", [P, 2, 512])
        ps_t = room.psum("ps_t", [P, 2, 512])
        gw_loaded, gw_psum = room.sem("gw_loaded"), room.sem("gw_psum")
        gw_hi_ready, gw_lo_ready = room.sem("gw_hi_ready"), room.sem("gw_lo_ready")
        x_ready, x_psum, hi_ready, lo_ready = (room.sem(n) for n in ("x_ready", "x_psum", "hi_ready", "lo_ready"))
        l_psum, logitT_ready = room.sem("l_psum"), room.sem("logitT_ready")
        t_psum, logit_ready = room.sem("t_psum"), room.sem("logit_ready")
        index_ready, shifted_ready, exp_ready = room.sem("index_ready"), room.sem("shifted_ready"), room.sem("exp_ready")
        done = room.sem("done")
        block = stack.enter_context(nc.Block())

        @block.sync
        def _(sp):
            sp.dma_start(gw_rows[:], gate_w).then_inc(gw_loaded, 16)

        @block.gpsimd
        def _(pool):
            for e in range(EXPERTS):
                nc.gpsimd.memset(index[:, e:e + 1], float(e)).then_inc(index_ready, 1)

        @block.scalar
        def _(act):
            act.wait_ge(gw_psum, 1)
            nc.scalar.copy(gw_part[0][:], ps_t[:, 0, 0:EXPERTS]).then_inc(gw_hi_ready, 1)

            def step(t, par):
                s1 = t - 1
                if there(t, GROUPS):
                    act.wait_ge(x_psum, t + 1)
                    nc.scalar.copy(xT_part[0][:, par, :], ps_x[:, par, :]).then_inc(hi_ready, 1)
                if there(s1, GROUPS):
                    act.wait_ge(l_psum, s1 + 1)
                    nc.scalar.copy(logitT[:, 1 - par, :], ps_l[0:EXPERTS, 1 - par, :]).then_inc(logitT_ready, 1)

            pipelined(act, step, GROUPS, 4, 2)
            act.wait_ge(shifted_ready, 1)
            nc.scalar.activation(score[:], shifted[:], ACT.Exp).then_inc(exp_ready, 1)

        @block.tensor
        def _(pe):
            pe.wait_ge(gw_loaded, 16)
            nc.tensor.transpose(ps_t[:, 0, 0:EXPERTS], gw_rows[:], ident[0:EXPERTS, 0:EXPERTS]).then_inc(gw_psum, 1)
            pe.wait_ge(gw_lo_ready, 1)

            def step(t, par):
                s1, s2 = t - 1, t - 2
                if there(t, GROUPS):
                    pe.wait_ge(x_ready, t + 1)
                    wait(pe, lo_ready, t - 1)
                    for n in range(GROUP):
                        last = nc.tensor.transpose(ps_x[:, par, n * S:(n + 1) * S], x_rows[:, par, n * S:(n + 1) * S],
                                                   ident[:])
                    last.then_inc(x_psum, 1)
                if there(s1, GROUPS):
                    pe.wait_ge(lo_ready, s1 + 1)
                    wait(pe, logitT_ready, s1 - 1)
                    split_product(nc, ps_l[0:EXPERTS, 1 - par, :], [g[:] for g in gw_part],
                                  [x[:, 1 - par, :] for x in xT_part]).then_inc(l_psum, 1)
                if there(s2, GROUPS):
                    wait_apart(pe, gw_lo_ready, (logitT_ready, s2 + 1), (logit_ready, s2 - 1))
                    for n in range(GROUP):
                        last = nc.tensor.transpose(ps_t[:, par, n * EXPERTS:(n + 1) * EXPERTS],
                                                   logitT[:, par, n * S:(n + 1) * S], ident[0:EXPERTS, 0:EXPERTS])
                    last.then_inc(t_psum, 1)

            pipelined(pe, step, GROUPS, 4, 2)

        @block.vector
        def _(dve):
            dve.wait_ge(gw_hi_ready, 1)
            nc.vector.tensor_tensor(gw_part[1][:], ps_t[:, 0, 0:EXPERTS], gw_part[0][:].bitcast(F32), ALU.subtract
                                    ).then_inc(gw_lo_ready, 1)

            def step(t, par):
                s2 = t - 2
                if there(t, GROUPS):
                    wait(dve, x_psum, t - 1)
                    nc.vector.tensor_copy(x_rows[:, par, :], X[:, bass.ds(t * TOKENS, TOKENS)]).then_inc(x_ready, 1)
                    dve.wait_ge(hi_ready, t + 1)
                    nc.vector.tensor_tensor(xT_part[1][:, par, :], ps_x[:, par, :], xT_part[0][:, par, :].bitcast(F32),
                                            ALU.subtract).then_inc(lo_ready, 1)
                if there(s2, GROUPS):
                    dve.wait_ge(t_psum, s2 + 1)
                    nc.vector.tensor_copy(logit[:].rearrange("p b e -> p (b e)")[:, bass.ds(s2 * GROUP * EXPERTS, GROUP * EXPERTS)],
                                          ps_t[:, par, 0:GROUP * EXPERTS]).then_inc(logit_ready, 1)

            pipelined(dve, step, GROUPS, 4, 2)

            count = [0]

            def then(instruction):
                count[0] += 1
                instruction.then_inc(done, 1)
                dve.wait_ge(done, count[0])

            def across(column):
                return column.unsqueeze(2).broadcast_to([P, B, EXPERTS])

            top, z, inv_z, max1, at1, max2, at2, den, inv_den, w = (col[:, n, :] for n in range(10))
            indices = index[:].unsqueeze(1).broadcast_to([P, B, EXPERTS])
            dve.wait_ge(logit_ready, GROUPS)
            dve.wait_ge(index_ready, EXPERTS)
            then(nc.vector.tensor_reduce(top, logit[:], AX, ALU.max))
            nc.vector.tensor_tensor(shifted[:], logit[:], across(top), ALU.subtract).then_inc(shifted_ready, 1)
            dve.wait_ge(exp_ready, 1)
            then(nc.vector.tensor_reduce(z, score[:], AX, ALU.add))
            then(nc.vector.reciprocal(inv_z, z))
            then(nc.vector.tensor_tensor(score[:], score[:], across(inv_z), ALU.mult))

            def pick(values, largest, at, chosen):
                then(nc.vector.tensor_reduce(largest, values[:], AX, ALU.max))
                then(nc.vector.tensor_tensor(equal[:], values[:], across(largest), ALU.is_equal))
                then(nc.vector.scalar_tensor_tensor(order[:], equal[:], TOP, indices, ALU.mult, ALU.add))
                then(nc.vector.tensor_reduce(at, order[:], AX, ALU.min))
                then(nc.vector.tensor_tensor(chosen[:], order[:], across(at), ALU.is_equal))

            pick(score, max1, at1, first)
            then(nc.vector.scalar_tensor_tensor(rest[:], first[:], -4.0, score[:], ALU.mult, ALU.add))
            pick(rest, max2, at2, second)
            then(nc.vector.scalar_tensor_tensor(den, max1, 1e-20, max2, ALU.add, ALU.add))
            then(nc.vector.reciprocal(inv_den, den))
            then(nc.vector.tensor_scalar(inv_den, inv_den, ROUTE_SCALE, None, ALU.mult))
            then(nc.vector.tensor_tensor(w, max1, inv_den, ALU.mult))
            then(nc.vector.tensor_tensor(first[:], first[:], across(w), ALU.mult))
            then(nc.vector.tensor_tensor(w, max2, inv_den, ALU.mult))
            then(nc.vector.tensor_tensor(second[:], second[:], across(w), ALU.mult))
            then(nc.vector.tensor_tensor(first[:], first[:], second[:], ALU.add))
            then(nc.vector.tensor_copy(combine[:, :, 0:EXPERTS], first[:]))
            then(nc.vector.tensor_tensor(combine[:, :, EXPERTS:2 * EXPERTS], first[:],
                                         combine[:, :, 0:EXPERTS].bitcast(F32), ALU.subtract))


def experts(nc, X, ident, combine, w_gate, w_up, w_down, sw_gate, sw_up, sw_down, out):
    F = w_gate.shape[2]
    FS = sw_gate.shape[1]
    FE = EXPERTS * F
    FA = FE + FS
    NB = -(-FA // P)
    NE = FE // P
    RING = 7
    assert FE % P == 0 and NB % 2 == 0 and NB % RING == 0
    rows_of = [min(P, FA - n * P) for n in range(NB)]
    with ExitStack() as stack:
        room = Room(nc, stack, "e")
        w_rows = room.sbuf("w_rows", [P, 2, FA])
        gate_part = [room.sbuf(f"gate_{n}", [P, FA], F32R) for n in ("hi", "lo")]
        up_part = [room.sbuf(f"up_{n}", [P, FA], F32R) for n in ("hi", "lo")]
        down = room.sbuf("down", [P, NB, D])
        spread = room.sbuf("spread", [P, FE], F32R)
        x_rows = room.sbuf("x_rows", [P, 2, TOKENS])
        xT_part = [room.sbuf(f"xT_{n}", [P, 2, TOKENS], F32R) for n in ("hi", "lo")]
        c_rows = room.sbuf("c_rows", [P, 2, GROUP, 2 * EXPERTS])
        cT = room.sbuf("cT", [P, 2, TOKENS], F32R)
        silu = room.sbuf("silu", [P, 2, TOKENS])
        act_up = room.sbuf("act_up", [P, 2, TOKENS])
        hidden = room.sbuf("hidden", [P, RING, TOKENS])
        yT = room.sbuf("yT", [P, TOKENS])
        hsum = room.sbuf("hsum", [P, GROUP, D])
        stat = room.sbuf("stat", [P, GROUP, 6])
        mom = room.sbuf("mom", [P, GROUP, 2])
        vare = room.sbuf("vare", [P, GROUP])
        rstd = room.sbuf("rstd", [P, GROUP])
        half = room.sbuf("half", [P, GROUP])
        result = room.sbuf("result", [P, 2, GROUP, D])
        ps_gate = room.psum("ps_gate", [P, 2, 512])
        ps_up = room.psum("ps_up", [P, 2, 512])
        ps_c = room.psum("ps_c", [P, 2, 512])
        ps_y = room.psum("ps_y", [P, 512])
        ps_m = room.psum("ps_m", [P, 512])

        w_loaded, down_loaded = room.sem("w_loaded"), room.sem("down_loaded")
        ones_ready, spread_ready = room.sem("ones_ready"), room.sem("spread_ready")
        zero_ready, w_hi_ready, w_lo_ready = room.sem("zero_ready"), room.sem("w_hi_ready"), room.sem("w_lo_ready")
        half_ready = room.sem("half_ready")
        x_ready, x_psum, hi_ready, lo_ready = (room.sem(n) for n in ("x_ready", "x_psum", "hi_ready", "lo_ready"))
        c_ready, c_psum, cT_ready = room.sem("c_ready"), room.sem("c_psum"), room.sem("cT_ready")
        gate_psum, up_psum, spread_psum = room.sem("gate_psum"), room.sem("up_psum"), room.sem("spread_psum")
        silu_ready, act_ready, hidden_ready = room.sem("silu_ready"), room.sem("act_ready"), room.sem("hidden_ready")
        scaled_ready = room.sem("scaled_ready")
        y_psum, yT_ready, back_psum = room.sem("y_psum"), room.sem("yT_ready"), room.sem("back_psum")
        sum_ready, stat_ready, mom_ready = room.sem("sum_ready"), room.sem("stat_ready"), room.sem("mom_ready")
        vare_ready, rstd_ready, result_ready = room.sem("vare_ready"), room.sem("rstd_ready"), room.sem("result_ready")
        stored = [room.sem(f"stored{n}") for n in range(2)]
        block = stack.enter_context(nc.Block())

        def run(engine, step):
            pipelined(engine, step, GROUPS, 2, 2)

        def here(s):
            return there(s, GROUPS)

        @block.sync
        def _(sp):
            for n, (w, sw) in enumerate(((w_gate, sw_gate), (w_up, sw_up))):
                sp.dma_start(w_rows[:, n, 0:FE].rearrange("p (e f) -> p e f", f=F), w.rearrange("e d f -> d e f")
                             ).then_inc(w_loaded, 16)
                sp.dma_start(w_rows[:, n, FE:FA], sw).then_inc(w_loaded, 16)
            sp.dma_start(down[:, 0:NE, :], w_down.rearrange("e f d -> (e f) d").rearrange("(n p) d -> p n d", p=P)
                         ).then_inc(down_loaded, 16)
            full = FS // P
            sp.dma_start(down[:, NE:NE + full, :], sw_down[0:full * P].rearrange("(n p) d -> p n d", p=P)
                         ).then_inc(down_loaded, 16)
            sp.dma_start(down[0:FS - full * P, NE + full, :], sw_down[full * P:FS]).then_inc(down_loaded, 16)

            def step(t, par):
                s2 = t - 2
                if here(s2):
                    sp.wait_ge(result_ready, (s2 + 1) * GROUP)
                    sp.dma_start(out[bass.ds(s2 * GROUP, GROUP)].rearrange("b s d -> s b d"), result[:, par]
                                 ).then_inc(stored[par], 16)

            run(sp, step)
            for par in range(2):
                sp.wait_ge(stored[par], GROUPS // 2 * 16)

        @block.gpsimd
        def _(pool):
            nc.gpsimd.memset(half[:], -0.5).then_inc(half_ready, 1)
            built = hidden[:].rearrange("p r t -> p (r t)")[:, 0:FE]
            nc.gpsimd.memset(built, 0.0).then_inc(ones_ready, 1)
            for k in range(2):
                pool.wait_ge(ones_ready, k + 1)
                view = built.rearrange("p (e f) -> p e f", f=F)
                nc.gpsimd.affine_select(out=view, in_=view, compare_op=ALU.not_equal, fill=1.0, base=-k * EXPERTS,
                                        pattern=[[-1, EXPERTS], [0, F]], channel_multiplier=1).then_inc(ones_ready, 1)
            pool.wait_ge(ones_ready, 3)
            nc.gpsimd.tensor_copy(spread[:], built).then_inc(spread_ready, 1)
            nc.gpsimd.memset(cT[:].bitcast(F32), 0.0).then_inc(zero_ready, 1)
            pool.wait_ge(half_ready, 1)

            def step(t, par):
                s2 = t - 2
                if here(s2):
                    wait_apart(pool, half_ready, (mom_ready, (s2 + 1) * GROUP))
                    nc.gpsimd.tensor_scalar(vare[:], mom[:, :, 1], EPS, None, ALU.add).then_inc(vare_ready, 1)
                    pool.wait_ge(vare_ready, s2 + 1)
                    nc.gpsimd.tensor_tensor(rstd[:], vare[:], half[:], ALU.pow).then_inc(rstd_ready, 1)
                    wait_apart(pool, half_ready, (rstd_ready, s2 + 1), (stored[par], landed(s2, par) - 16))
                    for n in range(GROUP):
                        nc.gpsimd.tensor_scalar(result[:, par, n, :], hsum[:, n, :], mom[:, n, 0:1], rstd[:, n:n + 1],
                                                ALU.subtract, ALU.mult).then_inc(result_ready, 1)

            run(pool, step)

        @block.scalar
        def _(act):
            act.wait_ge(w_loaded, 64)
            for n, part in enumerate((gate_part, up_part)):
                nc.scalar.copy(part[0][:], w_rows[:, n, :]).then_inc(w_hi_ready, 1)
            act.wait_ge(zero_ready, 1)

            def step(t, par):
                s1, s2 = t - 1, t - 2
                for n in range(NB):
                    if here(s1):
                        act.wait_ge(gate_psum, s1 * NB + n + 1)
                        wait(act, act_ready, s1 * NB + n - 1)
                        nc.scalar.activation(silu[0:rows_of[n], n % 2, :], ps_gate[0:rows_of[n], n % 2, :], ACT.Silu
                                             ).then_inc(silu_ready, 1)
                    if n == 1 and here(s2):
                        act.wait_ge(y_psum, s2 + 1)
                        nc.scalar.copy(yT[:], ps_y[:]).then_inc(yT_ready, 1)
                    if n == 5 and here(t):
                        act.wait_ge(x_psum, t + 1)
                        nc.scalar.copy(xT_part[0][:, par, :], ps_m[:]).then_inc(hi_ready, 1)
                    if n == 7 and here(t):
                        act.wait_ge(c_psum, t + 1)
                        nc.scalar.copy(cT[0:2 * EXPERTS, par, :], ps_m[0:2 * EXPERTS, :]).then_inc(cT_ready, 1)

            run(act, step)

        @block.vector
        def _(dve):
            for n, part in enumerate((gate_part, up_part)):
                dve.wait_ge(w_hi_ready, n + 1)
                nc.vector.tensor_tensor(part[1][:], w_rows[:, n, :], part[0][:].bitcast(F32), ALU.subtract
                                        ).then_inc(w_lo_ready, 1)
            dve.wait_ge(spread_ready, 1)

            def step(t, par):
                s1, s2 = t - 1, t - 2
                for n in range(NB):
                    if here(s1):
                        rows = rows_of[n]
                        dve.wait_ge(silu_ready, s1 * NB + n + 1)
                        dve.wait_ge(up_psum, s1 * NB + n + 1)
                        first = act_up if n < NE else hidden
                        at = n % 2 if n < NE else n % RING
                        nc.vector.tensor_tensor(first[0:rows, at, :], silu[0:rows, n % 2, :], ps_up[0:rows, n % 2, :],
                                                ALU.mult).then_inc(act_ready, 1)
                        if n < NE:
                            dve.wait_ge(act_ready, s1 * NB + n + 1)
                            dve.wait_ge(spread_psum, s1 * NE + n + 1)
                            nc.vector.tensor_tensor(hidden[:, n % RING, :], act_up[:, n % 2, :],
                                                    ps_c[:, n % 2, :], ALU.mult).then_inc(scaled_ready, 1)
                    if n == 3 and here(s2):
                        dve.wait_ge(back_psum, s2 + 1)
                        wait(dve, result_ready, s2 * GROUP)
                        nc.vector.tensor_tensor(hsum[:].rearrange("p n d -> p (n d)"), ps_m[:], x_rows[:, par, :], ALU.add
                                                ).then_inc(sum_ready, 1)
                        dve.wait_ge(sum_ready, s2 + 1)
                        for k in range(GROUP):
                            nc.vector.bn_stats(stat[:, k, :], hsum[:, k, :]).then_inc(stat_ready, 1)
                        for k in range(GROUP):
                            wait_apart(dve, w_hi_ready, (stat_ready, s2 * GROUP + k + 1))
                            nc.vector.bn_aggr(mom[:, k, :], stat[:, k, :]).then_inc(mom_ready, 1)
                    if n == 4 and here(t):
                        nc.vector.tensor_copy(x_rows[:, par, :], X[:, bass.ds(t * TOKENS, TOKENS)]).then_inc(x_ready, 1)
                        wait(dve, c_psum, t - 1)
                        nc.vector.tensor_copy(c_rows[:, par].rearrange("p b e -> p (b e)"),
                                              combine[:].bitcast(F32).rearrange("p b e -> p (b e)")[
                                                  :, bass.ds(t * GROUP * 2 * EXPERTS, GROUP * 2 * EXPERTS)]
                                              ).then_inc(c_ready, 1)
                    if n == 6 and here(t):
                        dve.wait_ge(hi_ready, t + 1)
                        nc.vector.tensor_tensor(xT_part[1][:, par, :], ps_m[:], xT_part[0][:, par, :].bitcast(F32),
                                                ALU.subtract).then_inc(lo_ready, 1)

            run(dve, step)

        @block.tensor
        def _(pe):
            pe.wait_ge(w_lo_ready, 2)
            pe.wait_ge(spread_ready, 1)
            pe.wait_ge(down_loaded, 48)

            def project_down(s, n):
                if n < NE:
                    pe.wait_ge(scaled_ready, s * NE + n + 1)
                else:
                    pe.wait_ge(act_ready, s * NB + n + 1)
                last = nc.tensor.matmul(ps_y[:], down[0:rows_of[n], n, :], hidden[0:rows_of[n], n % RING, :],
                                        start=(n == 0), stop=(n == NB - 1))
                if n == NB - 1:
                    last.then_inc(y_psum, 1)

            def step(t, par):
                s1, s2 = t - 1, t - 2
                if here(s1):
                    pe.wait_ge(lo_ready, s1 + 1)
                    pe.wait_ge(cT_ready, s1 + 1)
                for n in range(NB):
                    if here(s1):
                        rows = rows_of[n]
                        xT = [x[:, 1 - par, :] for x in xT_part]
                        wait(pe, silu_ready, s1 * NB + n - 1)
                        split_product(nc, ps_gate[0:rows, n % 2, :], [g[:, n * P:n * P + rows] for g in gate_part], xT
                                      ).then_inc(gate_psum, 1)
                        wait(pe, act_ready, s1 * NB + n - 1)
                        split_product(nc, ps_up[0:rows, n % 2, :], [u[:, n * P:n * P + rows] for u in up_part], xT
                                      ).then_inc(up_psum, 1)
                        if n < NE:
                            wait(pe, scaled_ready, s1 * NE + n - 1 if n else s1 * NE)
                            nc.tensor.matmul(ps_c[:, n % 2, :], spread[:, n * P:(n + 1) * P], cT[:, 1 - par, :],
                                             start=True, stop=True).then_inc(spread_psum, 1)
                    if n < 2 and here(s2):
                        project_down(s2, NB - 2 + n)
                    if n == 2 and here(s1):
                        wait(pe, yT_ready, s1)
                    if n >= 2 and here(s1):
                        project_down(s1, n - 2)
                    if n == 2 and here(s2):
                        pe.wait_ge(yT_ready, s2 + 1)
                        wait(pe, cT_ready, s2 + 2 if not isinstance(s2, int) else min(s2 + 2, GROUPS))
                        for k in range(GROUP):
                            last = nc.tensor.transpose(ps_m[:, k * D:(k + 1) * D], yT[:, k * S:(k + 1) * S], ident[:])
                        last.then_inc(back_psum, 1)
                    if n == 5 and here(t):
                        pe.wait_ge(x_ready, t + 1)
                        wait(pe, sum_ready, t - 1)
                        for k in range(GROUP):
                            last = nc.tensor.transpose(ps_m[:, k * S:(k + 1) * S], x_rows[:, par, k * S:(k + 1) * S],
                                                       ident[:])
                        last.then_inc(x_psum, 1)
                    if n == 7 and here(t):
                        pe.wait_ge(c_ready, t + 1)
                        pe.wait_ge(lo_ready, t + 1)
                        for k in range(GROUP):
                            last = nc.tensor.transpose(ps_m[0:2 * EXPERTS, k * S:(k + 1) * S], c_rows[:, par, k, :],
                                                       ident[:])
                        last.then_inc(c_psum, 1)

            run(pe, step)


def decoder(nc, x, ctx, Wq, bq, Wk, bk, Wv, bv, Wo, bo, m_g, m_b, l_g, l_b, xWq, xWkv, xWout,
            gate_w, w_gate, w_up, w_down, sw_gate, sw_up, sw_down, out):
    nkv = nc.dram_tensor("normalised_keys", (B, C + S, D), F32, kind="Internal").ap()
    with ExitStack() as stack:
        X = stack.enter_context(nc.sbuf_tensor("X", [P, B * D], F32))
        ident = stack.enter_context(nc.sbuf_tensor("ident", [P, P], F32))
        tri = stack.enter_context(nc.sbuf_tensor("tri", [P, P], F32))
        combine = stack.enter_context(nc.sbuf_tensor("combine", [P, B, 2 * EXPERTS], F32R))
        constants(nc, ident, tri)
        linear_attention(nc, X, nkv, ident, tri, x, ctx, (Wq, Wk, Wv, Wo), (bq, bk, bv, bo))
        cross_attention(nc, X, nkv, ident, (m_g, m_b, l_g, l_b), xWq, xWkv, xWout)
        router(nc, X, ident, gate_w, combine)
        experts(nc, X, ident, combine, w_gate, w_up, w_down, sw_gate, sw_up, sw_down, out)


INPUTS = ["x", "ctx_1024", "L0_attn_Wq", "L0_attn_bq", "L0_attn_Wk", "L0_attn_bk", "L0_attn_Wv", "L0_attn_bv",
          "L0_attn_Wo", "L0_attn_bo", "L0_xattn_ln_m_g", "L0_xattn_ln_m_b", "L0_xattn_ln_l_g", "L0_xattn_ln_l_b",
          "L0_xattn_Wq", "L0_xattn_Wkv", "L0_xattn_Wout", "L0_ffn_gate_w", "L0_ffn_w_gate", "L0_ffn_w_up",
          "L0_ffn_w_down", "L0_ffn_sw_gate", "L0_ffn_sw_up", "L0_ffn_sw_down"]


def kernel(**inputs):
    import numpy as np
    import concourse.bacc as bacc
    from concourse.bass_utils import run_bass_kernel_spmd

    nc = bacc.Bacc("TRN2", target_bir_lowering=False, num_devices=1)
    arrays, args = {}, []
    for name in INPUTS:
        a = np.ascontiguousarray(inputs[name])
        arrays[f"in_{name}"] = a
        args.append(nc.dram_tensor(f"in_{name}", a.shape, mybir.dt.from_np(a.dtype), kind="ExternalInput").ap())
    args.append(nc.dram_tensor("out_dram", (B, S, D), F32, kind="ExternalOutput").ap())
    decoder(nc, *args)
    result = run_bass_kernel_spmd(nc, [arrays], core_ids=[0])
    return result.results[0]["out_dram"]
```

```python
from contextlib import ExitStack

import concourse.bass as bass
from concourse import mybir

F32 = mybir.dt.float32
F32R = mybir.dt.float32r
ALU = mybir.AluOpType
ACT = mybir.ActivationFunctionType
AX = mybir.AxisListType.X

P = 128
EXPERTS = 8
B = 64
S = 128
D = 128
C = 120
H = 16
EPS = 1e-5


def wait(engine, semaphore, count):
    if not isinstance(count, int) or count > 0:
        engine.wait_ge(semaphore, count)


def wait_apart(engine, opened, *waits):
    waits = [(semaphore, count if isinstance(count, int) else engine.to_reg(count)) for semaphore, count in waits]
    engine.wait_ge(opened, 1)
    for semaphore, count in waits:
        wait(engine, semaphore, count)


def pipelined(engine, step, count=B, head=4, tail=4):
    for t in range(head):
        step(t, t % 2)
    with engine.Fori(head // 2, count // 2) as i:
        for parity in range(2):
            step(i * 2 + parity, parity)
    for t in range(count, count + tail):
        step(t, t % 2)


def there(s, count=B):
    return not isinstance(s, int) or 0 <= s < count


def landed(s, parity):
    return (s - parity) * 8 + 16


class Room:

    def __init__(self, nc, stack, tag):
        self.nc, self.stack, self.tag = nc, stack, tag

    def sbuf(self, name, shape, dtype=F32):
        return self.stack.enter_context(self.nc.sbuf_tensor(f"{self.tag}_{name}", shape, dtype))

    def psum(self, name, shape):
        return self.stack.enter_context(self.nc.psum_tensor(f"{self.tag}_{name}", shape, F32))

    def sem(self, name):
        return self.stack.enter_context(self.nc.semaphore(f"{self.tag}_{name}"))


def constants(nc, ident, tri):
    with ExitStack() as stack:
        room = Room(nc, stack, "const")
        filled = room.sem("filled")
        shaped = room.sem("shaped")
        block = stack.enter_context(nc.Block())

        @block.gpsimd
        def _(pool):
            nc.gpsimd.memset(ident[:], 0.0).then_inc(filled, 1)
            nc.gpsimd.memset(tri[:], 1.0).then_inc(filled, 1)
            pool.wait_ge(filled, 2)
            nc.gpsimd.affine_select(out=ident[:], in_=ident[:], compare_op=ALU.not_equal, fill=1.0, base=0,
                                    pattern=[[-1, P]], channel_multiplier=1).then_inc(shaped, 1)
            nc.gpsimd.affine_select(out=tri[:], in_=tri[:], compare_op=ALU.is_ge, fill=0.0, base=0,
                                    pattern=[[1, P]], channel_multiplier=-1).then_inc(shaped, 1)
            pool.wait_ge(shaped, 2)


class LaterWeights:

    def __init__(self, nc, stack, gains, w_q, w_kv, w_out, gate_w, w_gate, w_up, w_down, sw_gate, sw_up, sw_down):
        room = Room(nc, stack, "w")
        I = w_q.shape[1]
        F, FS = w_gate.shape[2], sw_gate.shape[1]
        FE = EXPERTS * F
        FA = FE + FS
        self.blocks, self.expert_blocks = -(-FA // P), FE // P
        self.F, self.FE, self.FA, self.FS = F, FE, FA, FS
        self.wq = room.sbuf("wq", [P, I])
        self.wkv = room.sbuf("wkv", [P, 2 * I])
        self.wo = room.sbuf("wo", [P, I // P, D])
        self.gain = room.sbuf("gain", [P, 4])
        self.gw_rows = room.sbuf("gw_rows", [EXPERTS, D])
        self.rows = room.sbuf("rows", [P, 2, FA])
        self.down = room.sbuf("down", [P, self.blocks, D])
        self.gate_part = [room.sbuf(f"gate_{n}", [P, FA], F32R) for n in ("hi", "lo")]
        self.up_part = [room.sbuf(f"up_{n}", [P, FA], F32R) for n in ("hi", "lo")]
        self.spread = room.sbuf("spread", [P, FE], F32R)
        self.attention_loaded, self.gains_loaded = room.sem("attention_loaded"), room.sem("gains_loaded")
        self.gate_loaded, self.mlps_loaded = room.sem("gate_loaded"), room.sem("mlps_loaded")
        self.down_loaded = room.sem("down_loaded")
        self.sources = gains, w_q, w_kv, w_out, gate_w, w_gate, w_up, w_down, sw_gate, sw_up, sw_down

    def load(self, sp):
        gains, w_q, w_kv, w_out, gate_w, w_gate, w_up, w_down, sw_gate, sw_up, sw_down = self.sources
        sp.dma_start(self.wq[:], w_q).then_inc(self.attention_loaded, 16)
        sp.dma_start(self.wkv[:], w_kv).then_inc(self.attention_loaded, 16)
        sp.dma_start(self.wo[:], w_out.rearrange("(j p) d -> p j d", p=P)).then_inc(self.attention_loaded, 16)
        for n, g in enumerate(gains):
            sp.dma_start(self.gain[:, n:n + 1], g.rearrange("(d o) -> d o", o=1)).then_inc(self.gains_loaded, 16)
        sp.dma_start(self.gw_rows[:], gate_w).then_inc(self.gate_loaded, 16)
        for n, (w, sw) in enumerate(((w_gate, sw_gate), (w_up, sw_up))):
            sp.dma_start(self.rows[:, n, 0:self.FE].rearrange("p (e f) -> p e f", f=self.F),
                         w.rearrange("e d f -> d e f")).then_inc(self.mlps_loaded, 16)
            sp.dma_start(self.rows[:, n, self.FE:self.FA], sw).then_inc(self.mlps_loaded, 16)
        full, at = self.FS // P, self.expert_blocks
        sp.dma_start(self.down[:, 0:at, :], w_down.rearrange("e f d -> (e f) d").rearrange("(n p) d -> p n d", p=P)
                     ).then_inc(self.down_loaded, 16)
        sp.dma_start(self.down[:, at:at + full, :], sw_down[0:full * P].rearrange("(n p) d -> p n d", p=P)
                     ).then_inc(self.down_loaded, 16)
        sp.dma_start(self.down[0:self.FS - full * P, at + full, :], sw_down[full * P:self.FS]
                     ).then_inc(self.down_loaded, 16)


def linear_attention(nc, X, lat, ident, tri, x, weights, biases, later):
    E = D // H
    NE = E + 1
    QK = 2 * D
    PAIRS = B // 2
    with ExitStack() as stack:
        room = Room(nc, stack, "lin")
        w_rows = room.sbuf("w_rows", [P, 4, D])
        w = room.sbuf("w", [P, 4 * D])
        b_qk = room.sbuf("b_qk", [1, QK])
        b_qk_part = [room.sbuf(f"b_qk_{n}", [1, QK], F32R) for n in ("hi", "lo")]
        b_v = room.sbuf("b_v", [P, D])
        ones = room.sbuf("ones", [1, P], F32R)
        b_o = room.sbuf("b_o", [P, D])
        x_rows = room.sbuf("x_rows", [P, 2, 2, D])
        turned = room.sbuf("turned", [P, 4, S])
        pos = room.sbuf("pos", [P, 2, 2 * QK])
        v = room.sbuf("v", [P, 2, 2, D])
        mag = room.sbuf("mag", [P, 2 * QK])
        dec = room.sbuf("dec", [P, 2 * QK])
        log = room.sbuf("log", [P, 2 * QK])
        qk = room.sbuf("qk", [P, 2, 2, QK])
        kv = room.sbuf("kv", [P, 2, E, H, E])
        prod = room.sbuf("prod", [P, 2, NE, H, E])
        numden = room.sbuf("numden", [P, 2, NE, H])
        inv = room.sbuf("inv", [P, 2, H])
        att = room.sbuf("att", [P, 2, H, E])
        res = room.sbuf("res", [P, 2, 2, D])
        stat = room.sbuf("stat", [P, 2, 6])
        mom = room.sbuf("mom", [P, 2, 2, 2])
        square = room.sbuf("square", [P, 2, 4])
        scale = room.sbuf("scale", [P, 2, 4])
        shift = room.sbuf("shift", [P, 2, 4])
        half = room.sbuf("half", [P, 4])
        nlat = room.sbuf("nlat", [P, 2, 2, D])
        ps_t = room.psum("ps_t", [P, 512])
        ps_qk = room.psum("ps_qk", [P, 512])
        ps_vy = room.psum("ps_vy", [P, 512])
        ps_cum = room.psum("ps_cum", [P, 2, 1024])
        ps_den = room.psum("ps_den", [P, 512])

        w_loaded, bqk_loaded, bvo_loaded = room.sem("w_loaded"), room.sem("bqk_loaded"), room.sem("bvo_loaded")
        res_loaded = [room.sem(f"res_loaded{n}") for n in range(4)]
        x_loaded = [room.sem(f"x_loaded{n}") for n in range(2)]
        lat_stored = [room.sem(f"lat_stored{n}") for n in range(2)]
        wT_psum, wT_ready = room.sem("wT_psum"), room.sem("wT_ready")
        half_ready, ones_ready = room.sem("half_ready"), room.sem("ones_ready")
        b_hi_ready, b_lo_ready = room.sem("b_hi_ready"), room.sem("b_lo_ready")
        xT_psum, xT_ready = room.sem("xT_psum"), room.sem("xT_ready")
        aT_psum, aT_ready = room.sem("aT_psum"), room.sem("aT_ready")
        qk_psum, vy_psum = room.sem("qk_psum"), room.sem("vy_psum")
        pos_ready, v_ready, vb_ready = room.sem("pos_ready"), room.sem("v_ready"), room.sem("vb_ready")
        mag_ready, dec_ready, log_ready = room.sem("mag_ready"), room.sem("dec_ready"), room.sem("log_ready")
        qk_ready, kv_ready = room.sem("qk_ready"), room.sem("kv_ready")
        den_psum, cum_psum = room.sem("den_psum"), room.sem("cum_psum")
        den_taken, cum_taken = room.sem("den_taken"), room.sem("cum_taken")
        numden_ready, inv_ready, att_ready = room.sem("numden_ready"), room.sem("inv_ready"), room.sem("att_ready")
        bias_added, sum_ready = room.sem("bias_added"), room.sem("sum_ready")
        stat_ready, mom_ready = room.sem("stat_ready"), room.sem("mom_ready")
        square_ready, scale_ready, shift_ready = (room.sem(n) for n in ("square_ready", "scale_ready", "shift_ready"))
        x1_ready, nlat_ready = room.sem("x1_ready"), room.sem("nlat_ready")
        block = stack.enter_context(nc.Block())
        QUART = B // 4

        def here(s):
            return there(s, PAIRS)

        def rows_of(dram, s, rows):
            return dram[bass.ds(s * 2, 2), rows, :].rearrange("b s d -> s b d")

        @block.sync
        def _(sp):
            for n, weight in enumerate(weights):
                sp.dma_start(w_rows[:, n, :], weight).then_inc(w_loaded, 16)

            def step(t, par):
                s5 = t - 5
                if here(s5):
                    sp.wait_ge(nlat_ready, s5 * 2 + 2)
                    sp.dma_start(rows_of(lat, s5, slice(0, S)), nlat[:, 1 - par]).then_inc(lat_stored[1 - par], 16)
                if here(t):
                    wait(sp, xT_psum, t - 1)
                    sp.dma_start(x_rows[:, par], rows_of(x, t, slice(0, S))).then_inc(x_loaded[par], 16)
                if isinstance(t, int) and t == 5:
                    later.load(sp)

            pipelined(sp, step, PAIRS, 6, 6)
            for par in range(2):
                sp.wait_ge(lat_stored[par], 16 * PAIRS // 2)

        @block.gpsimd
        def _(pool):
            nc.gpsimd.memset(half[:], -0.5).then_inc(half_ready, 1)
            nc.gpsimd.memset(ones[:].bitcast(F32), 1.0).then_inc(ones_ready, 1)
            pool.wait_ge(half_ready, 1)
            pool.wait_ge(bvo_loaded, 32)
            for n in range(4):
                pool.wait_ge(res_loaded[n], 16)

            def step(t, par):
                s1, s4 = t - 1, t - 4
                if here(s4):
                    pool.wait_ge(square_ready, s4 * 2 + 2)
                    wait(pool, x1_ready, s4 * 2 - 2)
                    nc.gpsimd.tensor_tensor(scale[:, par, :], square[:, par, :], half[:], ALU.pow
                                            ).then_inc(scale_ready, 1)
                if here(s1):
                    pair = X[:, bass.ds(s1 * 2 * D, 2 * D)]
                    nc.gpsimd.tensor_tensor(pair.rearrange("p (b d) -> p b d", b=2), pair.rearrange("p (b d) -> p b d", b=2),
                                            b_o[:].unsqueeze(1).broadcast_to([P, 2, D]), ALU.add).then_inc(bias_added, 1)
                    pool.wait_ge(v_ready, s1 + 1)
                    nc.gpsimd.tensor_tensor(v[:, 1 - par], v[:, 1 - par], b_v[:].unsqueeze(1).broadcast_to([P, 2, D]),
                                            ALU.add).then_inc(vb_ready, 1)
                    pool.wait_ge(vb_ready, s1 + 1)
                    pool.wait_ge(qk_ready, s1 + 1)
                    for u in range(2):
                        wait(pool, cum_psum, s1 * 2 - 1 + u)
                        k_u = qk[:, 1 - par, u, D:QK].rearrange("p (h d) -> p h d", h=H)
                        v_u = v[:, 1 - par, u].rearrange("p (h e) -> p e h", h=H)
                        nc.gpsimd.tensor_tensor(kv[:, u], k_u.unsqueeze(1).broadcast_to([P, E, H, E]),
                                                v_u.unsqueeze(3).broadcast_to([P, E, H, E]), ALU.mult
                                                ).then_inc(kv_ready, 1)

            pipelined(pool, step, PAIRS, 6, 4)

        @block.scalar
        def _(act):
            for n in range(2):
                act.dma_start(b_qk[:, n * D:(n + 1) * D], biases[n].rearrange("(o d) -> o d", o=1)
                              ).then_inc(bqk_loaded, 16)
            for b, n in ((b_v, 2), (b_o, 3)):
                act.dma_start(b[:], biases[n].rearrange("(o d) -> o d", o=1).broadcast_to([P, D])
                              ).then_inc(bvo_loaded, 16)
            for n in range(4):
                act.dma_start(X[:, n * QUART * D:(n + 1) * QUART * D].rearrange("s (b d) -> s b d", d=D),
                              x[n * QUART:(n + 1) * QUART].rearrange("b s d -> s b d")).then_inc(res_loaded[n], 16)
            act.wait_ge(wT_psum, 1)
            nc.scalar.copy(w[:], ps_t[:]).then_inc(wT_ready, 1)

            def step(t, par):
                s3, s4 = t - 3, t - 4
                if here(t):
                    act.wait_ge(xT_psum, t + 1)
                    nc.scalar.copy(turned[:, 0:2, :], ps_t[:, 0:2 * S]).then_inc(xT_ready, 1)

                def normalise(out, rows, column, ready):
                    nc.scalar.activation(out, rows, ACT.Identity, bias=shift[:, par, column:column + 1],
                                         scale=scale[:, par, column:column + 1]).then_inc(ready, 1)

                if here(s4):
                    act.wait_ge(shift_ready, s4 + 1)
                    wait(act, lat_stored[par], landed(s4, par) - 16)
                    for u in range(2):
                        normalise(nlat[:, par, u, :], res[:, par, u, :], 2 + u, nlat_ready)
                    for u in range(2):
                        normalise(X[:, bass.ds((s4 * 2 + u) * D, D)], res[:, par, u, :], u, x1_ready)
                if here(s3):
                    act.wait_ge(aT_psum, s3 + 1)
                    nc.scalar.copy(turned[:, 2:4, :], ps_t[:, 2 * S:4 * S]).then_inc(aT_ready, 1)
                if here(t):
                    act.wait_ge(qk_psum, t + 1)
                    wait(act, dec_ready, t)
                    nc.scalar.activation(mag[:], ps_qk[:], ACT.Abs).then_inc(mag_ready, 1)
                    act.wait_ge(mag_ready, t + 1)
                    wait(act, log_ready, t)
                    nc.scalar.activation(dec[:], mag[:], ACT.Exp, scale=-1.0).then_inc(dec_ready, 1)
                    wait(act, qk_ready, t - 1)
                    nc.scalar.activation(pos[:, par], ps_qk[:], ACT.Relu).then_inc(pos_ready, 1)
                    act.wait_ge(dec_ready, t + 1)
                    wait(act, qk_ready, t)
                    nc.scalar.activation(log[:], dec[:], ACT.Ln, bias=1.0).then_inc(log_ready, 1)
                    act.wait_ge(vy_psum, t + 1)
                    wait(act, sum_ready, s3 + 1)
                    wait(act, kv_ready, t * 2 - 2)
                    nc.scalar.copy(v[:, par].rearrange("p u d -> p (u d)"), ps_vy[:, 0:2 * D]).then_inc(v_ready, 1)

            pipelined(act, step, PAIRS, 4, 4)

        @block.vector
        def _(dve):
            dve.wait_ge(bqk_loaded, 32)
            nc.vector.tensor_copy(b_qk_part[0][:], b_qk[:]).then_inc(b_hi_ready, 1)
            dve.wait_ge(b_hi_ready, 1)
            nc.vector.tensor_tensor(b_qk_part[1][:], b_qk[:], b_qk_part[0][:].bitcast(F32), ALU.subtract
                                    ).then_inc(b_lo_ready, 1)

            def numerators(s, par, u):
                wait(dve, numden_ready, s)
                dve.wait_ge(cum_psum, s * 2 + u + 1)
                q = qk[:, par, u, 0:D].rearrange("p (o f) -> p o f", o=1).broadcast_to([P, E, D])
                nc.vector.tensor_tensor(prod[:, u, 0:E].rearrange("p e h d -> p e (h d)"),
                                        ps_cum[:, u, :].rearrange("p (e f) -> p e f", e=E), q, ALU.mult
                                        ).then_inc(cum_taken, 1)

            def step(t, par):
                s1, s2, s3, s4 = t - 1, t - 2, t - 3, t - 4
                if here(s2):
                    numerators(s2, par, 0)
                if here(s1):
                    dve.wait_ge(log_ready, s1 + 1)
                    wait(dve, den_psum, s1 - 1)
                    nc.vector.tensor_tensor(qk[:, 1 - par].rearrange("p u f -> p (u f)"), pos[:, 1 - par], log[:], ALU.add
                                            ).then_inc(qk_ready, 1)
                if here(s4):
                    dve.wait_ge(scale_ready, s4 + 1)
                    wait(dve, x1_ready, s4 * 2 - 2)
                    nc.vector.scalar_tensor_tensor(shift[:, par, :].rearrange("p (k u) -> p k u", k=2),
                                                   mom[:, par, :, 0].unsqueeze(1).broadcast_to([P, 2, 2]), -1.0,
                                                   scale[:, par, :].rearrange("p (k u) -> p k u", k=2), ALU.mult,
                                                   ALU.mult).then_inc(shift_ready, 1)
                if here(s2):
                    numerators(s2, par, 1)
                    nc.vector.tensor_tensor(prod[:, :, E].rearrange("p u h d -> p u (h d)"),
                                            ps_den[:, 0:2 * D].rearrange("p (u f) -> p u f", u=2), qk[:, par, :, 0:D],
                                            ALU.mult).then_inc(den_taken, 1)
                    dve.wait_ge(den_taken, s2 + 1)
                    wait(dve, att_ready, s2)
                    nc.vector.tensor_reduce(numden[:], prod[:], AX, ALU.add).then_inc(numden_ready, 1)
                if here(s3):
                    dve.wait_ge(vy_psum, t + 1)
                    dve.wait_ge(bias_added, s3 + 1)
                    wait(dve, x1_ready, (s3 - 1) * 2)
                    nc.vector.tensor_tensor(res[:, 1 - par], ps_vy[:, 2 * D:4 * D].rearrange("p (u f) -> p u f", u=2),
                                            X[:, bass.ds(s3 * 2 * D, 2 * D)].rearrange("p (u f) -> p u f", u=2), ALU.add
                                            ).then_inc(sum_ready, 1)
                if here(s2):
                    dve.wait_ge(numden_ready, s2 + 1)
                    nc.vector.reciprocal(inv[:], numden[:, :, E, :]).then_inc(inv_ready, 1)
                if here(s3):
                    wait_apart(dve, b_lo_ready, (sum_ready, s3 + 1), (mom_ready, s3 * 2))
                    for u in range(2):
                        nc.vector.bn_stats(stat[:, u, :], res[:, 1 - par, u, :]).then_inc(stat_ready, 1)
                if here(s2):
                    dve.wait_ge(inv_ready, s2 + 1)
                    wait(dve, aT_psum, s2)
                    nc.vector.tensor_tensor(att[:].rearrange("p u h e -> p u e h"), numden[:, :, 0:E, :],
                                            inv[:].unsqueeze(2).broadcast_to([P, 2, E, H]), ALU.mult
                                            ).then_inc(att_ready, 1)
                if here(s3):
                    for u in range(2):
                        wait_apart(dve, b_lo_ready, (stat_ready, s3 * 2 + u + 1))
                        nc.vector.bn_aggr(mom[:, 1 - par, u, :], stat[:, u, :]).then_inc(mom_ready, 1)
                if here(s3):
                    dve.wait_ge(mom_ready, s3 * 2 + 2)
                    nc.vector.tensor_scalar(square[:, 1 - par, 0:2], mom[:, 1 - par, :, 1], EPS, None, ALU.add
                                            ).then_inc(square_ready, 1)
                    nc.vector.tensor_scalar(square[:, 1 - par, 2:4], mom[:, 1 - par, :, 1], 1.0 + EPS, EPS * EPS,
                                            ALU.mult, ALU.add).then_inc(square_ready, 1)

            pipelined(dve, step, PAIRS, 6, 4)

        @block.tensor
        def _(pe):
            pe.wait_ge(w_loaded, 64)
            for n in range(4):
                last = nc.tensor.transpose(ps_t[:, n * D:(n + 1) * D], w_rows[:, n, :], ident[:])
            last.then_inc(wT_psum, 1)
            pe.wait_ge(wT_ready, 1)
            pe.wait_ge(b_lo_ready, 1)
            pe.wait_ge(ones_ready, 1)

            def step(t, par):
                s1, s3 = t - 1, t - 3
                if here(t):
                    wait(pe, aT_ready, s3)
                    pe.wait_ge(x_loaded[par], landed(t, par))
                    for u in range(2):
                        last = nc.tensor.transpose(ps_t[:, u * S:(u + 1) * S], x_rows[:, par, u, :], ident[:])
                    last.then_inc(xT_psum, 1)
                    pe.wait_ge(xT_ready, t + 1)
                    wait(pe, pos_ready, t)
                    for u in range(2):
                        out = ps_qk[:, u * QK:(u + 1) * QK]
                        nc.tensor.matmul(out, ones[:], b_qk_part[1][:], start=True, stop=False)
                        nc.tensor.matmul(out, ones[:], b_qk_part[0][:], start=False, stop=False)
                        last = nc.tensor.matmul(out, turned[:, u, :], w[:, 0:QK], start=False, stop=True)
                    last.then_inc(qk_psum, 1)
                if here(s3):
                    pe.wait_ge(att_ready, s3 + 1)
                    wait(pe, aT_ready, s3)
                    for u in range(2):
                        last = nc.tensor.transpose(ps_t[:, (2 + u) * S:(3 + u) * S],
                                                   att[:, u].rearrange("p h e -> p (h e)"), ident[:])
                    last.then_inc(aT_psum, 1)
                if here(t):
                    wait(pe, v_ready, t)
                if here(s3 - 1):
                    pe.wait_ge(sum_ready, s3)
                if here(t):
                    for u in range(2):
                        last = nc.tensor.matmul(ps_vy[:, u * D:(u + 1) * D], turned[:, u, :], w[:, QK:3 * D],
                                                start=True, stop=True)
                if here(s3):
                    pe.wait_ge(aT_ready, s3 + 1)
                    for u in range(2):
                        last = nc.tensor.matmul(ps_vy[:, (2 + u) * D:(3 + u) * D], turned[:, 2 + u, :], w[:, 3 * D:4 * D],
                                                start=True, stop=True)
                if here(t) or here(s3):
                    last.then_inc(vy_psum, 1)
                if here(s1):
                    pe.wait_ge(qk_ready, s1 + 1)
                    wait(pe, den_taken, s1)
                    nc.tensor.matmul(ps_den[:, 0:2 * D], tri[:], qk[:, 1 - par, :, D:QK], start=True, stop=True
                                     ).then_inc(den_psum, 1)
                    for u in range(2):
                        pe.wait_ge(kv_ready, s1 * 2 + u + 1)
                        wait(pe, cum_taken, s1 * 2 - 1 + u)
                        flat = kv[:, u].rearrange("p e h d -> p (e h d)")
                        for n in range(2):
                            last = nc.tensor.matmul(ps_cum[:, u, n * 512:(n + 1) * 512], tri[:],
                                                    flat[:, n * 512:(n + 1) * 512], start=True, stop=True)
                        last.then_inc(cum_psum, 1)

            pipelined(pe, step, PAIRS, 4, 4)


def split_product(nc, out, stationary, moving, first=True, last=True):
    nc.tensor.matmul(out, stationary[0], moving[1], start=first, stop=False)
    nc.tensor.matmul(out, stationary[1], moving[0], start=False, stop=False)
    return nc.tensor.matmul(out, stationary[0], moving[0], start=False, stop=last)


def cross_attention(nc, X, lat, ctx, ident, later):
    DH = 64
    I = H * DH
    K = C + S
    KT = K // 2
    PAIRS = H // 2
    UNITS = 2 * PAIRS
    ROUNDS = B // 2
    with ExitStack() as stack:
        room = Room(nc, stack, "x")
        wq, wkv, wo, gain = later.wq, later.wkv, later.wo, later.gain
        wqT = room.sbuf("wqT", [P, PAIRS, D])
        wkT = room.sbuf("wkT", [P, PAIRS, D])
        M_part = [room.sbuf(f"M_{n}", [P, H, D], F32R) for n in ("hi", "lo")]
        wv_part = [room.sbuf(f"wv_{n}", [P, I], F32R) for n in ("hi", "lo")]
        nk = room.sbuf("nk", [KT, 2, 2, 2, D])
        kT_full = room.sbuf("kT_full", [P, 2, K])
        kT_part = [room.sbuf(f"kT_{n}", [P, 2, 2, K], F32R) for n in ("hi", "lo")]
        G_part = [room.sbuf(f"G_{n}", [P, 2, 2, 2, S], F32R) for n in ("hi", "lo")]
        V = room.sbuf("V", [KT, 2, 2, 2, I // 2])
        nmax = room.sbuf("nmax", [P, 2, 2])
        total = room.sbuf("total", [P, 2, 2])
        inv = room.sbuf("inv", [P, 2, 2])
        prob = room.sbuf("prob", [P, 2, 2, K])
        probT = room.sbuf("probT", [KT, 2, 2, 2, S])
        outT = room.sbuf("outT", [P, 2, 2, PAIRS // 2, S])
        hsum = room.sbuf("hsum", [P, 2, D])
        stat = room.sbuf("stat", [P, 2, 6])
        mom = room.sbuf("mom", [P, 2, 2])
        vare = room.sbuf("vare", [P, 2])
        rstd = room.sbuf("rstd", [P, 2])
        cstat = room.sbuf("cstat", [C, 2, 6])
        cmom = room.sbuf("cmom", [C, 2, 2])
        cvare = room.sbuf("cvare", [C, 2])
        crstd = room.sbuf("crstd", [C, 2])
        half = room.sbuf("half", [P, 2])
        xnew = room.sbuf("xnew", [P, 2, D])
        ps_S = room.psum("ps_S", [P, 2, 512])
        ps_T = room.psum("ps_T", [P, 2, 512])
        ps_O = room.psum("ps_O", [P, 2, 512])
        ps_G = room.psum("ps_G", [P, 512])
        ps_V = room.psum("ps_V", [P, 512])

        ones_ready, spread_ready = room.sem("ones_ready"), room.sem("spread_ready")
        part_ready = room.sem("part_ready")
        ctx_loaded = [room.sem(f"ctx_loaded{n}") for n in range(2)]
        lat_loaded = [room.sem(f"lat_loaded{n}") for n in range(2)]
        cstat_ready, cmom_ready, cvare_ready = room.sem("cstat_ready"), room.sem("cmom_ready"), room.sem("cvare_ready")
        crstd_ready, ctx_ready = room.sem("crstd_ready"), room.sem("ctx_ready")
        wT_psum, wT_ready = room.sem("wT_psum"), room.sem("wT_ready")
        M_psum, M_hi_ready, M_lo_ready = room.sem("M_psum"), room.sem("M_hi_ready"), room.sem("M_lo_ready")
        wv_hi_ready, wv_lo_ready = room.sem("wv_hi_ready"), room.sem("wv_lo_ready")
        kT_psum, kT_ready = room.sem("kT_psum"), room.sem("kT_ready")
        kT_hi_ready, kT_lo_ready = room.sem("kT_hi_ready"), room.sem("kT_lo_ready")
        G_psum, G_hi_ready, G_lo_ready = room.sem("G_psum"), room.sem("G_hi_ready"), room.sem("G_lo_ready")
        V_psum, V_ready = room.sem("V_psum"), room.sem("V_ready")
        S_psum, max_ready, exp_ready = room.sem("S_psum"), room.sem("max_ready"), room.sem("exp_ready")
        inv_ready, prob_ready = room.sem("inv_ready"), room.sem("prob_ready")
        T_psum, probT_ready, O_psum = room.sem("T_psum"), room.sem("probT_ready"), room.sem("O_psum")
        outT_ready, y_psum = room.sem("outT_ready"), room.sem("y_psum")
        sum_ready, stat_ready, mom_ready = room.sem("sum_ready"), room.sem("stat_ready"), room.sem("mom_ready")
        half_ready, vare_ready, rstd_ready = room.sem("half_ready"), room.sem("vare_ready"), room.sem("rstd_ready")
        xnew_ready, x2_ready = room.sem("xnew_ready"), room.sem("x2_ready")
        block = stack.enter_context(nc.Block())

        def rounds(engine, body):
            with engine.Fori(0, ROUNDS // 2) as i:
                for parity in range(2):
                    body(i * 2 + parity, parity)

        @block.sync
        def _(sp):
            def load(b, par):
                pair = bass.ds(b, 2)
                sp.dma_start(nk[0:C, par, :, 0, :], ctx[pair].rearrange("b s d -> s b d")).then_inc(ctx_loaded[par], 16)
                sp.dma_start(nk[C:KT, par, :, 0, :], lat[pair, 0:KT - C, :].rearrange("b s d -> s b d")
                             ).then_inc(lat_loaded[par], 16)
                sp.dma_start(nk[:, par, :, 1, :], lat[pair, KT - C:S, :].rearrange("b s d -> s b d")
                             ).then_inc(lat_loaded[par], 16)

            load(0, 0)
            load(2, 1)
            with sp.Fori(1, ROUNDS // 2) as i:
                for par in range(2):
                    sp.wait_ge(kT_psum, i * 2 + par - 1)
                    load(i * 4 + par * 2, par)
            for par in range(2):
                sp.wait_ge(kT_psum, ROUNDS - 1 + par)
                load(par * 2, par)
            for par in range(2):
                sp.wait_ge(ctx_loaded[par], (ROUNDS // 2 + 1) * 16)
                sp.wait_ge(lat_loaded[par], (ROUNDS // 2 + 1) * 32)

        @block.gpsimd
        def _(pool):
            nc.gpsimd.memset(half[:], -0.5).then_inc(half_ready, 1)
            pool.wait_ge(half_ready, 1)
            pool.sem_inc(x2_ready, 2)

            def split_keys(n, par):
                wait_apart(pool, half_ready, (kT_ready, n + 1))
                nc.gpsimd.tensor_copy(kT_part[0][:, par], kT_full[:]).then_inc(kT_hi_ready, 1)
                pool.wait_ge(kT_hi_ready, n + 1)
                nc.gpsimd.tensor_tensor(kT_part[1][:, par], kT_full[:], kT_part[0][:, par].bitcast(F32), ALU.subtract
                                        ).then_inc(kT_lo_ready, 1)

            def normalise_context(n, par):
                wait_apart(pool, half_ready, (cmom_ready, n * 2 + 2))
                nc.gpsimd.tensor_scalar(cvare[:], cmom[:, :, 1], EPS, None, ALU.add).then_inc(cvare_ready, 1)
                pool.wait_ge(cvare_ready, n + 1)
                nc.gpsimd.tensor_tensor(crstd[:], cvare[:], half[0:C, :], ALU.pow).then_inc(crstd_ready, 1)
                wait_apart(pool, half_ready, (crstd_ready, n + 1))
                for u in range(2):
                    rows = nk[0:C, par, u, 0, :]
                    nc.gpsimd.tensor_scalar(rows, rows, cmom[:, u, 0:1], crstd[:, u:u + 1], ALU.subtract, ALU.mult
                                            ).then_inc(ctx_ready, 1)

            def normalise(r, u):
                n = r * 2 + u
                wait_apart(pool, half_ready, (mom_ready, n + 1))
                nc.gpsimd.tensor_scalar(vare[:, u:u + 1], mom[:, u, 1:2], EPS, None, ALU.add).then_inc(vare_ready, 1)
                pool.wait_ge(vare_ready, n + 1)
                nc.gpsimd.tensor_tensor(rstd[:, u:u + 1], vare[:, u:u + 1], half[:, 0:1], ALU.pow).then_inc(rstd_ready, 1)
                wait_apart(pool, half_ready, (rstd_ready, n + 1))
                nc.gpsimd.tensor_scalar(xnew[:, u, :], hsum[:, u, :], mom[:, u, 0:1], rstd[:, u:u + 1], ALU.subtract,
                                        ALU.mult).then_inc(xnew_ready, 1)
                wait_apart(pool, half_ready, (xnew_ready, n + 1))
                nc.gpsimd.tensor_copy(X[:, bass.ds(n * D, D)], xnew[:, u, :]).then_inc(x2_ready, 1)

            def body(r, par):
                split_keys(r + 1, 1 - par)
                normalise_context(r + 2, par)
                normalise(r, 0)
                normalise(r, 1)

            normalise_context(0, 0)
            split_keys(0, 0)
            normalise_context(1, 1)
            built = outT[:].rearrange("p u n j q -> p (u n j q)")[:, 0:later.FE]
            view = built.rearrange("p (e f) -> p e f", f=later.F)
            nc.gpsimd.memset(built, 0.0).then_inc(ones_ready, 1)
            for k in range(2):
                pool.wait_ge(ones_ready, k + 1)
                nc.gpsimd.affine_select(out=view, in_=view, compare_op=ALU.not_equal, fill=1.0, base=-k * EXPERTS,
                                        pattern=[[-1, EXPERTS], [0, later.F]], channel_multiplier=1
                                        ).then_inc(ones_ready, 1)
            pool.wait_ge(ones_ready, 3)
            nc.gpsimd.tensor_copy(later.spread[:], built).then_inc(spread_ready, 1)
            pool.wait_ge(later.mlps_loaded, 64)
            for n, part in enumerate((later.gate_part, later.up_part)):
                nc.gpsimd.tensor_copy(part[0][:], later.rows[:, n, :]).then_inc(part_ready, 1)
                pool.wait_ge(part_ready, n * 2 + 1)
                nc.gpsimd.tensor_tensor(part[1][:], later.rows[:, n, :], part[0][:].bitcast(F32), ALU.subtract
                                        ).then_inc(part_ready, 1)
            rounds(pool, body)
            pool.wait_ge(part_ready, 4)
            pool.wait_ge(spread_ready, 1)

        @block.scalar
        def _(act):
            act.wait_ge(later.attention_loaded, 48)
            nc.scalar.copy(wv_part[0][:], wkv[:, I:2 * I]).then_inc(wv_hi_ready, 1)
            for n in range(4):
                act.wait_ge(wT_psum, n + 1)
                dst = (wqT, wkT)[n // 2]
                nc.scalar.copy(dst[:, n % 2 * 4:n % 2 * 4 + 4, :], ps_S[:, n % 2, :]).then_inc(wT_ready, 1)
            for n in range(4):
                act.wait_ge(M_psum, n + 1)
                nc.scalar.mul(M_part[0][:, n // 2 * 8 + n % 2:n // 2 * 8 + n % 2 + 7:2, :], ps_T[:, n % 2, :],
                              DH ** -0.5).then_inc(M_hi_ready, 1)

            def G_hi(n, pair):
                act.wait_ge(G_psum, n + 1)
                nc.scalar.copy(G_part[0][:, pair], ps_G[:]).then_inc(G_hi_ready, 1)

            def V_copy(n, hf, u, tile):
                act.wait_ge(V_psum, n + 1)
                nc.scalar.copy(V[:, hf, u, tile, :], ps_V[0:KT, :]).then_inc(V_ready, 1)

            def exponentials(n, k):
                act.wait_ge(max_ready, n + 1)
                for h in range(2):
                    nc.scalar.activation(prob[:, k, h, :], ps_S[:, k, h * K:(h + 1) * K], ACT.Exp,
                                         bias=nmax[:, k, h:h + 1], accum_out=total[:, k, h:h + 1]).then_inc(exp_ready, 1)

            def out_copy(u, hf, n):
                act.wait_ge(O_psum, n + 1)
                nc.scalar.copy(outT[:, u, hf], ps_O[:, u, :]).then_inc(outT_ready, 1)

            def body(r, par):
                unit = r * UNITS
                for s in range(UNITS):
                    act.wait_ge(T_psum, unit + s + 1)
                    nc.scalar.copy(probT[:, s % 2], ps_T[0:KT, s % 2, :]).then_inc(probT_ready, 1)
                    if s in (UNITS // 2 - 1, UNITS // 2, UNITS - 1):
                        out_copy((s - 1) % 2, (s - 1) // (UNITS // 2), unit + s - 1)
                    if s % 2 == 0:
                        G_hi(r * PAIRS + s // 2 + 2, s // 2 % 2)
                    else:
                        k = s // 2
                        V_copy(r * 8 + 4 + k, 1 - k // 4, k % 4 // 2, k % 2)
                    if s == UNITS - 1:
                        out_copy(1, 1, unit + s)
                    exponentials(unit + s + 2, s % 2)

            for k in range(4):
                V_copy(k, 0, k // 2, k % 2)
                if k < 2:
                    G_hi(k, k)
                else:
                    exponentials(k - 2, k - 2)
            act.wait_ge(spread_ready, 1)
            rounds(act, body)

        @block.vector
        def _(dve):
            dve.wait_ge(later.gains_loaded, 64)

            def keys(n):
                dve.wait_ge(kT_psum, n + 1)
                wait(dve, kT_lo_ready, n)
                rows = ps_V[:, 0:2 * K].rearrange("p (u k) -> p u k", u=2)
                nc.vector.tensor_scalar(kT_full[:, :, 0:C], rows[:, :, 0:C], gain[:, 0:1], gain[:, 1:2], ALU.mult, ALU.add)
                nc.vector.tensor_scalar(kT_full[:, :, C:K], rows[:, :, C:K], gain[:, 2:3], gain[:, 3:4], ALU.mult, ALU.add
                                        ).then_inc(kT_ready, 1)

            def context_moments(n, par):
                wait_apart(dve, later.gains_loaded, (ctx_loaded[par], landed(n, par)), (ctx_ready, n * 2))
                for u in range(2):
                    nc.vector.bn_stats(cstat[:, u, :], nk[0:C, par, u, 0, :]).then_inc(cstat_ready, 1)
                for u in range(2):
                    wait_apart(dve, later.gains_loaded, (cstat_ready, n * 2 + u + 1))
                    nc.vector.bn_aggr(cmom[:, u, :], cstat[:, u, :]).then_inc(cmom_ready, 1)

            def G_lo(n, pair):
                dve.wait_ge(G_hi_ready, n + 1)
                nc.vector.tensor_tensor(G_part[1][:, pair].rearrange("p h u q -> p (h u q)"), ps_G[:],
                                        G_part[0][:, pair].bitcast(F32).rearrange("p h u q -> p (h u q)"), ALU.subtract
                                        ).then_inc(G_lo_ready, 1)

            def maxima(n, k):
                dve.wait_ge(S_psum, n + 1)
                nc.vector.tensor_reduce(nmax[:, k, :], ps_S[:, k, 0:2 * K].rearrange("p (h k) -> p h k", h=2), AX,
                                        ALU.max, negate=True).then_inc(max_ready, 1)

            def normal(n, k):
                for h in range(2):
                    dve.wait_ge(exp_ready, n * 2 + h + 1)
                    nc.vector.reciprocal(inv[:, k, h:h + 1], total[:, k, h:h + 1]).then_inc(inv_ready, 1)
                    dve.wait_ge(inv_ready, n * 2 + h + 1)
                    nc.vector.tensor_scalar(prob[:, k, h, :], prob[:, k, h, :], inv[:, k, h:h + 1], None, ALU.mult
                                            ).then_inc(prob_ready, 1)

            def residual(r):
                dve.wait_ge(y_psum, r + 1)
                dve.wait_ge(x2_ready, r * 2 + 2)
                nc.vector.tensor_tensor(hsum[:].rearrange("p u d -> p (u d)"), ps_G[:, 0:2 * D],
                                        X[:, bass.ds(r * 2 * D, 2 * D)], ALU.add).then_inc(sum_ready, 1)
                dve.wait_ge(sum_ready, r + 2)
                for u in range(2):
                    nc.vector.bn_stats(stat[:, u, :], hsum[:, u, :]).then_inc(stat_ready, 1)
                for u in range(2):
                    wait_apart(dve, later.gains_loaded, (stat_ready, r * 2 + u + 1))
                    nc.vector.bn_aggr(mom[:, u, :], stat[:, u, :]).then_inc(mom_ready, 1)

            def body(r, par):
                unit = r * UNITS
                for s in range(UNITS):
                    if s:
                        normal(unit + s + 1, (s + 1) % 2)
                    maxima(unit + s + 2, s % 2)
                    if s == 4:
                        keys(r + 1)
                    if s == 5:
                        context_moments(r + 2, par)
                    if s % 2 == 0:
                        G_lo(r * PAIRS + s // 2 + 2, s // 2 % 2)
                normal(unit + UNITS + 1, 1)
                residual(r)

            def M_lo(n):
                dve.wait_ge(M_hi_ready, n + 1)
                heads = slice(n // 2 * 8 + n % 2, n // 2 * 8 + n % 2 + 7, 2)
                nc.vector.scalar_tensor_tensor(M_part[1][:, heads, :], ps_T[:, n % 2, :].rearrange("p (h d) -> p h d", h=4),
                                               DH ** -0.5, M_part[0][:, heads, :].bitcast(F32), ALU.mult, ALU.subtract
                                               ).then_inc(M_lo_ready, 1)

            context_moments(0, 0)
            dve.wait_ge(wv_hi_ready, 1)
            nc.vector.tensor_tensor(wv_part[1][:], wkv[:, I:2 * I], wv_part[0][:].bitcast(F32), ALU.subtract
                                    ).then_inc(wv_lo_ready, 1)
            M_lo(0)
            M_lo(1)
            keys(0)
            M_lo(2)
            M_lo(3)
            context_moments(1, 1)
            for j in range(2):
                G_lo(j, j)
            dve.wait_ge(G_lo_ready, 2)
            dve.sem_inc(sum_ready, 1)
            for k in range(2):
                maxima(k, k)
            for k in range(2):
                normal(k, k)
            rounds(dve, body)

        @block.tensor
        def _(pe):
            def keys(n, par):
                pe.wait_ge(ctx_ready, n * 2 + 2)
                pe.wait_ge(lat_loaded[par], (n - par) * 16 + 32)
                for u in range(2):
                    for tile in range(2):
                        at = u * K + tile * KT
                        last = nc.tensor.transpose(ps_V[:, at:at + KT], nk[:, par, u, tile, :], ident[0:KT, 0:KT])
                last.then_inc(kT_psum, 1)

            pe.wait_ge(later.attention_loaded, 48)
            for n in range(4):
                if n >= 2:
                    pe.wait_ge(wT_ready, n - 1)
                src = (wq, wkv)[n // 2]
                for j in range(4):
                    jj = n % 2 * 4 + j
                    last = nc.tensor.transpose(ps_S[:, n % 2, j * D:(j + 1) * D], src[:, jj * D:(jj + 1) * D], ident[:])
                last.then_inc(wT_psum, 1)
            pe.wait_ge(wT_ready, 4)
            for n in range(4):
                if n == 2:
                    keys(0, 0)
                if n >= 2:
                    pe.wait_ge(M_lo_ready, n - 1)
                odd = n % 2 * DH
                for j in range(4):
                    jj = n // 2 * 4 + j
                    last = nc.tensor.matmul(ps_T[:, n % 2, j * D:(j + 1) * D], wqT[odd:odd + DH, jj, :],
                                            wkT[odd:odd + DH, jj, :], start=True, stop=True)
                last.then_inc(M_psum, 1)
            pe.wait_ge(M_lo_ready, 4)
            pe.wait_ge(wv_lo_ready, 1)

            def make_G(pair, keys_par, j):
                for h in range(2):
                    last = split_product(nc, ps_G[:, h * 256:(h + 1) * 256], [m[:, 2 * j + h, :] for m in M_part],
                                         [k[:, keys_par, :, C:K] for k in kT_part])
                last.then_inc(G_psum, 1)

            def make_V(keys_par, hf, u, tile):
                split_product(nc, ps_V[0:KT, :], [k[:, keys_par, u, tile * KT:(tile + 1) * KT] for k in kT_part],
                              [w[:, hf * 512:(hf + 1) * 512] for w in wv_part]).then_inc(V_psum, 1)

            def scores(n, k, keys_par, pair):
                for h in range(2):
                    last = split_product(nc, ps_S[:, k, h * K:(h + 1) * K], [g[:, pair, h, k, :] for g in G_part],
                                         [t[:, keys_par, k, :] for t in kT_part])
                last.then_inc(S_psum, 1)

            def output(u):
                for j in range(PAIRS):
                    last = nc.tensor.matmul(ps_G[:, u * D:(u + 1) * D], outT[:, u, j // 4, j % 4, :], wo[:, j, :],
                                            start=(j == 0), stop=(j == PAIRS - 1))
                return last

            def body(r, par):
                unit = r * UNITS
                for s in range(UNITS):
                    j, u = s // 2, s % 2
                    for h in range(2):
                        pe.wait_ge(prob_ready, (unit + s) * 2 + h + 1)
                        for tile in range(2):
                            at = (h * 2 + tile) * S
                            last = nc.tensor.transpose(ps_T[0:KT, u, at:at + S], prob[:, u, h, tile * KT:(tile + 1) * KT],
                                                       ident[:])
                    last.then_inc(T_psum, 1)
                    ahead = j + 1
                    if u == 0:
                        pe.wait_ge(G_lo_ready, r * PAIRS + ahead + 1)
                    scores(unit + s + 2, u, par if ahead < PAIRS else 1 - par, ahead % 2)
                    if s == 4:
                        pe.wait_ge(V_ready, r * 8 + 4 + 2)
                        keys(r + 1, 1 - par)
                    if u == 0:
                        if s == 0:
                            pe.wait_ge(sum_ready, r + 1)
                        if s == 12:
                            pe.wait_ge(kT_lo_ready, r + 2)
                        make_G(j % 2, par if j + 2 < PAIRS else 1 - par, (j + 2) % PAIRS)
                    else:
                        if s != 5:
                            pe.wait_ge(V_ready, r * 8 + 4 + j)
                        else:
                            pe.wait_ge(kT_ready, r + 2)
                        if s == 9:
                            pe.wait_ge(kT_lo_ready, r + 2)
                        make_V(par if j < 4 else 1 - par, 1 - j // 4, j % 4 // 2, j % 2)
                    pe.wait_ge(probT_ready, unit + s + 1)
                    if s in (0, 8):
                        pe.wait_ge(V_ready, r * 8 + 4 + s // 2)
                    if s in (8, 9):
                        pe.wait_ge(outT_ready, r * 4 + s - 7)
                    for tile in range(2):
                        for h in range(2):
                            last = nc.tensor.matmul(ps_O[h * DH:(h + 1) * DH, u, j % 4 * S:(j % 4 + 1) * S],
                                                    V[:, j // 4, u, tile, (j % 4 * 2 + h) * DH:(j % 4 * 2 + h + 1) * DH],
                                                    probT[:, u, h, tile, :], start=(tile == 0), stop=(tile == 1))
                    last.then_inc(O_psum, 1)
                pe.wait_ge(G_lo_ready, r * PAIRS + 10)
                for u in range(2):
                    pe.wait_ge(outT_ready, r * 4 + 3 + u)
                    last = output(u)
                last.then_inc(y_psum, 1)

            pe.wait_ge(kT_lo_ready, 1)
            for k in range(4):
                if k:
                    pe.wait_ge(V_ready, k)
                make_V(0, 0, k // 2, k % 2)
                if k:
                    pe.wait_ge(G_lo_ready, min(k, 2))
                if k < 2:
                    make_G(k, 0, k)
                else:
                    scores(k - 2, k - 2, 0, 0)
            rounds(pe, body)


GROUP = 4
TOKENS = GROUP * S
GROUPS = B // GROUP
ROUTE_SCALE = 2.5


def experts(nc, X, ident, later, out):
    FE, FA = later.FE, later.FA
    NB = later.blocks
    NE = later.expert_blocks
    TOP = -16.0
    ROUTE_AT = 8
    STEPS = 21
    LAG = 3
    RING = 7
    assert FE % P == 0 and NB % 2 == 0 and NB % RING == 0
    rows_of = [min(P, FA - n * P) for n in range(NB)]
    with ExitStack() as stack:
        room = Room(nc, stack, "e")
        gate_part, up_part, spread = later.gate_part, later.up_part, later.spread
        down_part = [room.sbuf(f"down_{n}", [P, NB, D], F32R) for n in ("hi", "lo")]
        x_rows = room.sbuf("x_rows", [P, TOKENS])
        xT_part = [room.sbuf(f"xT_{n}", [P, 2, TOKENS], F32R) for n in ("hi", "lo")]
        gw_part = [room.sbuf(f"gw_{n}", [P, EXPERTS], F32R) for n in ("hi", "lo")]
        logitT = room.sbuf("logitT", [EXPERTS, TOKENS])
        index = room.sbuf("index", [P, EXPERTS])
        shifted, score, rest, equal, order, first, second, both, picked = (
            room.sbuf(n, [P, GROUP, EXPERTS])
            for n in ("shifted", "score", "rest", "equal", "order", "first", "second", "both", "picked"))
        col = room.sbuf("col", [P, 9, GROUP])
        c_rows = room.sbuf("c_rows", [P, GROUP, 2 * EXPERTS], F32R)
        cT = room.sbuf("cT", [P, 2, TOKENS], F32R)
        silu = room.sbuf("silu", [P, 2, TOKENS])
        act_up = room.sbuf("act_up", [P, 2, TOKENS])
        hidden = room.sbuf("hidden", [P, 2, TOKENS])
        hidden_part = [room.sbuf(f"hidden_{n}", [P, RING, TOKENS], F32R) for n in ("hi", "lo")]
        yT = room.sbuf("yT", [P, TOKENS])
        hsum = room.sbuf("hsum", [P, GROUP, D])
        stat = room.sbuf("stat", [P, GROUP, 6])
        mom = room.sbuf("mom", [P, GROUP, 2])
        vare = room.sbuf("vare", [P, GROUP])
        rstd = room.sbuf("rstd", [P, GROUP])
        half = room.sbuf("half", [P, GROUP])
        result = room.sbuf("result", [P, 2, GROUP, D])
        ps_gate = room.psum("ps_gate", [P, 2, 512])
        ps_up = room.psum("ps_up", [P, 2, 512])
        ps_c = room.psum("ps_c", [P, 2, 512])
        ps_y = room.psum("ps_y", [P, 512])
        ps_m = room.psum("ps_m", [P, 512])

        zero_ready, down_hi_ready, down_lo_ready = (room.sem(n) for n in ("zero_ready", "down_hi_ready", "down_lo_ready"))
        half_ready = room.sem("half_ready")
        x_ready, x_psum, hi_ready, lo_ready = (room.sem(n) for n in ("x_ready", "x_psum", "hi_ready", "lo_ready"))
        gw_psum, gw_hi_ready, gw_lo_ready = room.sem("gw_psum"), room.sem("gw_hi_ready"), room.sem("gw_lo_ready")
        logitT_psum, logitT_ready, logit_psum = room.sem("logitT_psum"), room.sem("logitT_ready"), room.sem("logit_psum")
        index_ready, shifted_ready, score_ready = room.sem("index_ready"), room.sem("shifted_ready"), room.sem("score_ready")
        routed = room.sem("routed")
        c_psum, cT_ready = room.sem("c_psum"), room.sem("cT_ready")
        gate_psum, up_psum, spread_psum = room.sem("gate_psum"), room.sem("up_psum"), room.sem("spread_psum")
        silu_ready, act_ready, scaled_ready = room.sem("silu_ready"), room.sem("act_ready"), room.sem("scaled_ready")
        hidden_hi_ready, hidden_lo_ready = room.sem("hidden_hi_ready"), room.sem("hidden_lo_ready")
        y_psum, yT_ready, back_psum = room.sem("y_psum"), room.sem("yT_ready"), room.sem("back_psum")
        sum_ready, stat_ready, mom_ready = room.sem("sum_ready"), room.sem("stat_ready"), room.sem("mom_ready")
        vare_ready, rstd_ready, result_ready = room.sem("vare_ready"), room.sem("rstd_ready"), room.sem("result_ready")
        stored = [room.sem(f"stored{n}") for n in range(2)]
        block = stack.enter_context(nc.Block())

        def run(engine, step):
            pipelined(engine, step, GROUPS, 2, 2)

        def here(s):
            return there(s, GROUPS)

        @block.sync
        def _(sp):
            def step(t, par):
                s2 = t - 2
                if here(s2):
                    sp.wait_ge(result_ready, (s2 + 1) * GROUP)
                    sp.dma_start(out[bass.ds(s2 * GROUP, GROUP)].rearrange("b s d -> s b d"), result[:, par]
                                 ).then_inc(stored[par], 16)

            run(sp, step)
            for par in range(2):
                sp.wait_ge(stored[par], GROUPS // 2 * 16)

        @block.gpsimd
        def _(pool):
            nc.gpsimd.memset(half[:], -0.5).then_inc(half_ready, 1)
            for e in range(EXPERTS):
                nc.gpsimd.memset(index[:, e:e + 1], float(e)).then_inc(index_ready, 1)
            nc.gpsimd.memset(cT[:].bitcast(F32), 0.0).then_inc(zero_ready, 1)
            pool.wait_ge(half_ready, 1)

            def hidden_lo(s, n):
                rows = rows_of[n]
                pool.wait_ge(hidden_hi_ready, s * NB + n + 1)
                nc.gpsimd.tensor_tensor(hidden_part[1][0:rows, n % RING, :], hidden[0:rows, n % 2, :],
                                        hidden_part[0][0:rows, n % RING, :].bitcast(F32), ALU.subtract
                                        ).then_inc(hidden_lo_ready, 1)

            def step(t, par):
                s1, s2 = t - 1, t - 2
                for n in range(NB):
                    if n == 0 and here(s2):
                        hidden_lo(s2, NB - 1)
                    if n and here(s1):
                        hidden_lo(s1, n - 1)
                    if n == 4 and here(s2):
                        wait_apart(pool, half_ready, (mom_ready, (s2 + 1) * GROUP))
                        nc.gpsimd.tensor_scalar(vare[:], mom[:, :, 1], EPS, None, ALU.add).then_inc(vare_ready, 1)
                        pool.wait_ge(vare_ready, s2 + 1)
                        nc.gpsimd.tensor_tensor(rstd[:], vare[:], half[:], ALU.pow).then_inc(rstd_ready, 1)
                    if n in (5, 7, 9, 11) and here(s2):
                        k = (n - 5) // 2
                        wait_apart(pool, half_ready, (rstd_ready, s2 + 1), (stored[par], landed(s2, par) - 16))
                        nc.gpsimd.tensor_scalar(result[:, par, k, :], hsum[:, k, :], mom[:, k, 0:1], rstd[:, k:k + 1],
                                                ALU.subtract, ALU.mult).then_inc(result_ready, 1)

            run(pool, step)

        @block.scalar
        def _(act):
            act.wait_ge(gw_psum, 1)
            nc.scalar.copy(gw_part[0][:], ps_m[:, 0:EXPERTS]).then_inc(gw_hi_ready, 1)
            act.wait_ge(zero_ready, 1)

            def down_hi():
                act.wait_ge(later.down_loaded, 48)
                nc.scalar.copy(down_part[0][:, 0:NB - 1, :], later.down[:, 0:NB - 1, :]).then_inc(down_hi_ready, 1)
                nc.scalar.copy(down_part[0][0:rows_of[-1], NB - 1, :], later.down[0:rows_of[-1], NB - 1, :]
                               ).then_inc(down_hi_ready, 1)

            def hidden_hi(s, n):
                rows = rows_of[n]
                if n < NE:
                    act.wait_ge(scaled_ready, s * NE + n + 1)
                else:
                    act.wait_ge(act_ready, s * NB + n + 1)
                nc.scalar.copy(hidden_part[0][0:rows, n % RING, :], hidden[0:rows, n % 2, :]).then_inc(hidden_hi_ready, 1)

            def step(t, par):
                s1, s2 = t - 1, t - 2
                for n in range(NB):
                    if n == LAG and here(s2):
                        act.wait_ge(y_psum, s2 + 1)
                        nc.scalar.copy(yT[:], ps_y[:]).then_inc(yT_ready, 1)
                    if here(s1):
                        act.wait_ge(gate_psum, s1 * NB + n + 1)
                        wait(act, act_ready, s1 * NB + n - 1)
                        nc.scalar.activation(silu[0:rows_of[n], n % 2, :], ps_gate[0:rows_of[n], n % 2, :], ACT.Silu
                                             ).then_inc(silu_ready, 1)
                    if n == 0 and here(s2):
                        hidden_hi(s2, NB - 1)
                    if n and here(s1):
                        hidden_hi(s1, n - 1)
                    if n == 0 and here(s1):
                        act.wait_ge(c_psum, s1 + 1)
                        nc.scalar.copy(cT[0:2 * EXPERTS, 1 - par, :], ps_m[0:2 * EXPERTS, :]).then_inc(cT_ready, 1)
                    if n == 1 and here(t):
                        act.wait_ge(x_psum, t + 1)
                        nc.scalar.copy(xT_part[0][:, par, :], ps_m[:]).then_inc(hi_ready, 1)
                    if n == 4 and here(t):
                        act.wait_ge(logitT_psum, t + 1)
                        nc.scalar.copy(logitT[:], ps_m[0:EXPERTS, :]).then_inc(logitT_ready, 1)
                    if n == 6 and here(t):
                        act.wait_ge(shifted_ready, t + 1)
                        nc.scalar.activation(score[:], shifted[:], ACT.Exp).then_inc(score_ready, 1)
                        if isinstance(t, int) and t == 0:
                            down_hi()

            run(act, step)

        @block.vector
        def _(dve):
            dve.wait_ge(gw_hi_ready, 1)
            nc.vector.tensor_tensor(gw_part[1][:], ps_m[:, 0:EXPERTS], gw_part[0][:].bitcast(F32), ALU.subtract
                                    ).then_inc(gw_lo_ready, 1)
            dve.wait_ge(index_ready, EXPERTS)
            def down_lo():
                dve.wait_ge(down_hi_ready, 2)
                for rows, blocks in ((P, slice(0, NB - 1)), (rows_of[-1], slice(NB - 1, NB))):
                    nc.vector.tensor_tensor(down_part[1][0:rows, blocks, :], later.down[0:rows, blocks, :],
                                            down_part[0][0:rows, blocks, :].bitcast(F32), ALU.subtract
                                            ).then_inc(down_lo_ready, 1)

            def across(column):
                return column.unsqueeze(2).broadcast_to([P, GROUP, EXPERTS])

            top, z, max1, at1, max2, at2, two, den, inv_den = (col[:, n, :] for n in range(9))
            indices = index[:].unsqueeze(1).broadcast_to([P, GROUP, EXPERTS])
            v = nc.vector
            routing = [(1, lambda: v.tensor_reduce(max1, score[:], AX, ALU.max)),
                       (2, lambda: v.tensor_reduce(z, score[:], AX, ALU.add)),
                       (2, lambda: v.tensor_tensor(equal[:], score[:], across(max1), ALU.is_equal)),
                       (1, lambda: v.scalar_tensor_tensor(order[:], equal[:], TOP, indices, ALU.mult, ALU.add)),
                       (1, lambda: v.tensor_reduce(at1, order[:], AX, ALU.min)),
                       (1, lambda: v.tensor_tensor(first[:], order[:], across(at1), ALU.is_equal)),
                       (1, lambda: v.scalar_tensor_tensor(rest[:], first[:], -4.0, score[:], ALU.mult, ALU.add)),
                       (1, lambda: v.tensor_reduce(max2, rest[:], AX, ALU.max)),
                       (1, lambda: v.tensor_tensor(equal[:], rest[:], across(max2), ALU.is_equal)),
                       (2, lambda: v.tensor_tensor(two, max1, max2, ALU.add)),
                       (2, lambda: v.scalar_tensor_tensor(order[:], equal[:], TOP, indices, ALU.mult, ALU.add)),
                       (2, lambda: v.scalar_tensor_tensor(den, z, 1e-20, two, ALU.mult, ALU.add)),
                       (2, lambda: v.tensor_reduce(at2, order[:], AX, ALU.min)),
                       (2, lambda: v.reciprocal(inv_den, den)),
                       (2, lambda: v.tensor_tensor(second[:], order[:], across(at2), ALU.is_equal)),
                       (1, lambda: v.tensor_tensor(both[:], first[:], second[:], ALU.add)),
                       (1, lambda: v.tensor_tensor(picked[:], both[:], score[:], ALU.mult)),
                       (1, lambda: v.scalar_tensor_tensor(both[:], picked[:], ROUTE_SCALE, across(inv_den), ALU.mult,
                                                          ALU.mult)),
                       (1, lambda: v.tensor_copy(c_rows[:, :, 0:EXPERTS], both[:])),
                       (1, lambda: v.tensor_tensor(c_rows[:, :, EXPERTS:2 * EXPERTS], both[:],
                                                   c_rows[:, :, 0:EXPERTS].bitcast(F32), ALU.subtract))]
            assert len(routing) + 1 == STEPS

            def step(t, par):
                s1, s2 = t - 1, t - 2
                for n in range(NB):
                    if n == 0 and here(t):
                        wait(dve, x_psum, t)
                        nc.vector.tensor_copy(x_rows[:], X[:, bass.ds(t * TOKENS, TOKENS)]).then_inc(x_ready, 1)
                    if here(s1):
                        rows = rows_of[n]
                        dve.wait_ge(silu_ready, s1 * NB + n + 1)
                        dve.wait_ge(up_psum, s1 * NB + n + 1)
                        if n >= NE:
                            wait(dve, hidden_lo_ready, s1 * NB + n - 1)
                        first = act_up if n < NE else hidden
                        nc.vector.tensor_tensor(first[0:rows, n % 2, :], silu[0:rows, n % 2, :], ps_up[0:rows, n % 2, :],
                                                ALU.mult).then_inc(act_ready, 1)
                        if n < NE:
                            dve.wait_ge(act_ready, s1 * NB + n + 1)
                            dve.wait_ge(spread_psum, s1 * NE + n + 1)
                            wait(dve, hidden_lo_ready, s1 * NB + n - 1)
                            nc.vector.tensor_tensor(hidden[:, n % 2, :], act_up[:, n % 2, :],
                                                    ps_c[:, n % 2, :], ALU.mult).then_inc(scaled_ready, 1)
                    if n == 3 and here(s2):
                        dve.wait_ge(back_psum, s2 + 1)
                        wait(dve, result_ready, s2 * GROUP)
                        nc.vector.tensor_tensor(hsum[:].rearrange("p n d -> p (n d)"), ps_m[:],
                                                X[:, bass.ds(s2 * TOKENS, TOKENS)], ALU.add
                                                ).then_inc(sum_ready, 1)
                        dve.wait_ge(sum_ready, s2 + 1)
                        for k in range(GROUP):
                            nc.vector.bn_stats(stat[:, k, :], hsum[:, k, :]).then_inc(stat_ready, 1)
                        for k in range(GROUP):
                            wait_apart(dve, gw_hi_ready, (stat_ready, s2 * GROUP + k + 1))
                            nc.vector.bn_aggr(mom[:, k, :], stat[:, k, :]).then_inc(mom_ready, 1)
                    if n == 1 and here(t):
                        dve.wait_ge(hi_ready, t + 1)
                        nc.vector.tensor_tensor(xT_part[1][:, par, :], ps_m[:], xT_part[0][:, par, :].bitcast(F32),
                                                ALU.subtract).then_inc(lo_ready, 1)
                    if n == 5 and here(t):
                        logit = ps_m[:, 0:GROUP * EXPERTS].rearrange("p (b e) -> p b e", b=GROUP)
                        dve.wait_ge(logit_psum, t + 1)
                        wait(dve, score_ready, t)
                        nc.vector.tensor_reduce(top, logit, AX, ALU.max).then_inc(routed, 1)
                        dve.wait_ge(routed, t * STEPS + 1)
                        nc.vector.tensor_tensor(shifted[:], logit, across(top), ALU.subtract).then_inc(shifted_ready, 1)
                    if ROUTE_AT <= n and here(t):
                        blocks = NB - ROUTE_AT
                        if n == ROUTE_AT:
                            dve.wait_ge(score_ready, t + 1)
                            wait(dve, c_psum, t)
                        first_k, end_k = ((n + i - ROUTE_AT) * len(routing) // blocks for i in range(2))
                        for k in range(first_k, end_k):
                            back, operation = routing[k]
                            dve.wait_ge(routed, t * STEPS + k + 2 - back)
                            operation().then_inc(routed, 1)
                if isinstance(t, int) and t == 0:
                    down_lo()

            run(dve, step)

        @block.tensor
        def _(pe):
            pe.wait_ge(later.gate_loaded, 16)
            nc.tensor.transpose(ps_m[:, 0:EXPERTS], later.gw_rows[:], ident[0:EXPERTS, 0:EXPERTS]).then_inc(gw_psum, 1)
            pe.wait_ge(gw_lo_ready, 1)

            def project_down(s, n):
                rows = rows_of[n]
                if isinstance(s, int) and s == 0 and n == 0:
                    pe.wait_ge(down_lo_ready, 2)
                pe.wait_ge(hidden_lo_ready, s * NB + n + 1)
                last = split_product(nc, ps_y[:], [w[0:rows, n, :] for w in down_part],
                                     [h[0:rows, n % RING, :] for h in hidden_part], first=(n == 0), last=(n == NB - 1))
                if n == NB - 1:
                    last.then_inc(y_psum, 1)

            def spread_weights(s, n, par):
                pe.wait_ge(cT_ready, s + 1)
                wait(pe, scaled_ready, s * NE + n - 1 if n else s * NE)
                nc.tensor.matmul(ps_c[:, n % 2, :], spread[:, n * P:(n + 1) * P], cT[:, par, :], start=True, stop=True
                                 ).then_inc(spread_psum, 1)

            def step(t, par):
                s1, s2 = t - 1, t - 2
                for n in range(NB):
                    if here(s1):
                        rows = rows_of[n]
                        xT = [x[:, 1 - par, :] for x in xT_part]
                        wait(pe, silu_ready, s1 * NB + n - 1)
                        split_product(nc, ps_gate[0:rows, n % 2, :], [g[:, n * P:n * P + rows] for g in gate_part], xT
                                      ).then_inc(gate_psum, 1)
                        wait(pe, act_ready, s1 * NB + n - 1)
                        split_product(nc, ps_up[0:rows, n % 2, :], [u[:, n * P:n * P + rows] for u in up_part], xT
                                      ).then_inc(up_psum, 1)
                        if n == 1:
                            spread_weights(s1, 0, 1 - par)
                    if n < LAG and here(s2):
                        project_down(s2, NB - LAG + n)
                    if n == 0 and here(s1):
                        pe.wait_ge(routed, (s1 + 1) * STEPS)
                        for k in range(GROUP):
                            last = nc.tensor.transpose(ps_m[0:2 * EXPERTS, k * S:(k + 1) * S],
                                                       c_rows[:, k, :].bitcast(F32), ident[:])
                        last.then_inc(c_psum, 1)
                    if 0 < n < NE and here(s1):
                        spread_weights(s1, n, 1 - par)
                    if n == LAG and here(s1):
                        wait(pe, yT_ready, s1)
                    if n >= LAG and here(s1):
                        project_down(s1, n - LAG)
                    if n == LAG and here(s2):
                        pe.wait_ge(yT_ready, s2 + 1)
                        wait(pe, lo_ready, s2 + 3 if not isinstance(s2, int) else min(s2 + 3, GROUPS))
                        for k in range(GROUP):
                            last = nc.tensor.transpose(ps_m[:, k * D:(k + 1) * D], yT[:, k * S:(k + 1) * S], ident[:])
                        last.then_inc(back_psum, 1)
                    if n == 1 and here(t):
                        pe.wait_ge(x_ready, t + 1)
                        wait(pe, cT_ready, t)
                        for k in range(GROUP):
                            last = nc.tensor.transpose(ps_m[:, k * S:(k + 1) * S], x_rows[:, k * S:(k + 1) * S], ident[:])
                        last.then_inc(x_psum, 1)
                    if n == 4 and here(t):
                        pe.wait_ge(lo_ready, t + 1)
                        wait(pe, sum_ready, t - 1)
                        split_product(nc, ps_m[0:EXPERTS, :], [g[:] for g in gw_part], [x[:, par, :] for x in xT_part]
                                      ).then_inc(logitT_psum, 1)
                    if n == 5 and here(t):
                        wait_apart(pe, gw_lo_ready, (logitT_ready, t + 1))
                        for k in range(GROUP):
                            last = nc.tensor.transpose(ps_m[:, k * EXPERTS:(k + 1) * EXPERTS],
                                                       logitT[:, k * S:(k + 1) * S], ident[0:EXPERTS, 0:EXPERTS])
                        last.then_inc(logit_psum, 1)

            run(pe, step)


def decoder(nc, x, ctx, Wq, bq, Wk, bk, Wv, bv, Wo, bo, m_g, m_b, l_g, l_b, xWq, xWkv, xWout,
            gate_w, w_gate, w_up, w_down, sw_gate, sw_up, sw_down, out):
    lat = nc.dram_tensor("latents", (B, S, D), F32, kind="Internal").ap()
    with ExitStack() as stack:
        X = stack.enter_context(nc.sbuf_tensor("X", [P, B * D], F32))
        ident = stack.enter_context(nc.sbuf_tensor("ident", [P, P], F32))
        tri = stack.enter_context(nc.sbuf_tensor("tri", [P, P], F32))
        later = LaterWeights(nc, stack, (m_g, m_b, l_g, l_b), xWq, xWkv, xWout, gate_w, w_gate, w_up, w_down, sw_gate,
                             sw_up, sw_down)
        constants(nc, ident, tri)
        linear_attention(nc, X, lat, ident, tri, x, (Wq, Wk, Wv, Wo), (bq, bk, bv, bo), later)
        cross_attention(nc, X, lat, ctx, ident, later)
        experts(nc, X, ident, later, out)


INPUTS = ["x", "ctx_1024", "L0_attn_Wq", "L0_attn_bq", "L0_attn_Wk", "L0_attn_bk", "L0_attn_Wv", "L0_attn_bv",
          "L0_attn_Wo", "L0_attn_bo", "L0_xattn_ln_m_g", "L0_xattn_ln_m_b", "L0_xattn_ln_l_g", "L0_xattn_ln_l_b",
          "L0_xattn_Wq", "L0_xattn_Wkv", "L0_xattn_Wout", "L0_ffn_gate_w", "L0_ffn_w_gate", "L0_ffn_w_up",
          "L0_ffn_w_down", "L0_ffn_sw_gate", "L0_ffn_sw_up", "L0_ffn_sw_down"]


def kernel(**inputs):
    import numpy as np
    import concourse.bacc as bacc
    from concourse.bass_utils import run_bass_kernel_spmd

    nc = bacc.Bacc("TRN2", target_bir_lowering=False, num_devices=1)
    arrays, args = {}, []
    for name in INPUTS:
        a = np.ascontiguousarray(inputs[name])
        arrays[f"in_{name}"] = a
        args.append(nc.dram_tensor(f"in_{name}", a.shape, mybir.dt.from_np(a.dtype), kind="ExternalInput").ap())
    args.append(nc.dram_tensor("out_dram", (B, S, D), F32, kind="ExternalOutput").ap())
    decoder(nc, *args)
    result = run_bass_kernel_spmd(nc, [arrays], core_ids=[0])
    return result.results[0]["out_dram"]
```
